# Optimizing a Trainium2 kernel written in Bass

```python
import numpy as np
import jax
import jax.numpy as jnp

def _softmax(x, axis=-1):
    return jax.nn.softmax(x, axis=axis)

def _gelu(x):
    return jax.nn.gelu(x, approximate=True)

def _silu(x):
    return jax.nn.silu(x)

def _sigmoid(x):
    return jax.nn.sigmoid(x)

def _layernorm(x, axis=-1, eps=1e-05):
    m = jnp.mean(x, axis=axis, keepdims=True)
    v = jnp.var(x, axis=axis, keepdims=True)
    return (x - m) / jnp.sqrt(v + eps)

def _scatter_add(tgt, idx, src, axis=0):
    return tgt.at[idx].add(src)

def _segment_sum(src, seg, n):
    return jax.ops.segment_sum(src, seg, n)
kernel_name = 'mk_flamingo_gated_d2_seqx_r2_e774e9'

def setup_inputs(seed: int=0):
    np.random.seed(seed)
    _w = jnp.asarray

    def _rec_inputs():
        import jax
        import jax.numpy as jnp
        _rk = jax.random.key(seed)
        x = -0.0003929 + 0.9999 * jax.random.normal(jax.random.fold_in(_rk, 1), (16, 224, 512), jnp.float32)
        _lenS = 224 - jax.random.randint(jax.random.fold_in(_rk, 7), (16,), 0, max(1, 224 // 4) + 1, jnp.int32)
        _lenS2 = 750 - jax.random.randint(jax.random.fold_in(_rk, 8), (16,), 0, max(1, 750 // 4) + 1, jnp.int32)
        _ctx_768P = jax.random.normal(jax.random.fold_in(_rk, 11), (16, 16, 384), jnp.float32)
        _ctx_768c = jax.random.dirichlet(jax.random.fold_in(_rk, 511), 0.3 * jnp.ones((16,), jnp.float32), (16, 750))
        _ctx_768t = jnp.einsum('bsk,bkd->bsd', _ctx_768c, _ctx_768P)
        _ctx_768t = _ctx_768t * jax.lax.rsqrt(jnp.mean(jnp.square(_ctx_768t)) + 1e-12) * 0.953939
        ctx_768 = 0.00095986 + 0.999812 * (_ctx_768t + 0.3 * jax.random.normal(jax.random.fold_in(_rk, 611), (16, 750, 384), jnp.float32))
        _validS = jnp.arange(224)[None, :] < _lenS[:, None]
        _validS2 = jnp.arange(750)[None, :] < _lenS2[:, None]
        _causal = jnp.tril(jnp.ones((224, 224), dtype=bool))
        mask_BxS2_bf1 = jnp.ones((16, 750), dtype=bool)
        _g = jax.random.normal(jax.random.fold_in(_rk, 9001), (2, 2), jnp.float32)
        _g = jnp.sign(_g) * jnp.maximum(jnp.abs(_g), 1.0) + (_g == 0) * 1.0
        g_xattn = _g[0]
        g_ffn = _g[1]
        return (x, ctx_768, mask_BxS2_bf1, g_xattn, g_ffn)
    x, ctx_768, mask_BxS2_bf1, g_xattn, g_ffn = _rec_inputs()

    def _L0_xattn_setup():
        import jax, jax.numpy as jnp
        import numpy as np
        DIM = 512
        CTX_DIM = 384
        HEADS = 16
        key = jax.random.key(seed)
        ks = jax.random.split(key, 7)
        B, N, M = (4, 2048, 128)
        x = jax.random.normal(ks[0], (B, N, DIM), dtype=jnp.float32)
        context = jax.random.normal(ks[1], (B, M, CTX_DIM), dtype=jnp.float32)
        context_mask = jnp.ones((B, M), dtype=bool)
        s_d = 1.0 / np.sqrt(DIM)
        s_c = 1.0 / np.sqrt(CTX_DIM)
        Wq = jax.random.normal(ks[2], (DIM, DIM), dtype=jnp.float32) * s_d
        Wk = jax.random.normal(ks[3], (CTX_DIM, DIM), dtype=jnp.float32) * s_c
        Wv = jax.random.normal(ks[4], (CTX_DIM, DIM), dtype=jnp.float32) * s_c
        Wo = jax.random.normal(ks[5], (DIM, DIM), dtype=jnp.float32) * s_d
        return {'x': x, 'context': context, 'context_mask': context_mask, 'Wq': Wq, 'Wk': Wk, 'Wv': Wv, 'Wo': Wo}
    _L0_xattn_all = _L0_xattn_setup()
    _L0_xattn_in = {k: v for k, v in _L0_xattn_all.items() if k in ('Wq', 'Wk', 'Wv', 'Wo')}
    del _L0_xattn_all

    def _L0_ffn_setup():
        import jax, jax.numpy as jnp
        import numpy as np
        BLOCK = 32
        W_BITS = 4
        ACT_BITS = 16

        def act_qdq(x):
            qmax = 2.0 ** (ACT_BITS - 1) - 1.0
            scale = jnp.maximum(jnp.max(jnp.abs(x)) / qmax, 1e-12)
            return jnp.clip(jnp.round(x / scale), -qmax - 1.0, qmax) * scale

        def fixed_qdq_u16(x):
            scale = 1.0 / 65536.0
            return jnp.clip(jnp.round(x / scale), 0.0, 65535.0) * scale

        def lpbq_dequant(w):
            O, I = w.shape
            qmax = 2.0 ** (W_BITS - 1) - 1.0
            wb = w.reshape(O, I // BLOCK, BLOCK)
            s = jnp.maximum(jnp.max(jnp.abs(wb), axis=-1, keepdims=True) / qmax, 1e-12)
            wq = jnp.clip(jnp.round(wb / s), -qmax - 1.0, qmax) * s
            return wq.reshape(O, I)
        key = jax.random.key(seed)
        k1, k2, k3, k4 = jax.random.split(key, 4)
        B, S, H, I = (2, 2048, 512, 1536)
        x = jax.random.normal(k1, (B, S, H), jnp.float32)
        w_gate = jax.random.normal(k2, (I, H), jnp.float32) * 0.02
        w_up = jax.random.normal(k3, (I, H), jnp.float32) * 0.02
        w_down = jax.random.normal(k4, (H, I), jnp.float32) * 0.02
        return {'x': x, 'w_gate': w_gate, 'w_up': w_up, 'w_down': w_down}
    _L0_ffn_all = _L0_ffn_setup()
    _L0_ffn_in = {k: v for k, v in _L0_ffn_all.items() if k in ('w_gate', 'w_up', 'w_down')}
    del _L0_ffn_all

    def _L1_xattn_setup():
        import jax, jax.numpy as jnp
        import numpy as np
        Q_DIM, K_DIM, V_DIM, OUT_DIM = (512, 384, 384, 512)
        key = jax.random.key(seed)
        ks = jax.random.split(key, 9)
        s = lambda d: 1.0 / np.sqrt(d)
        return {'query': jax.random.normal(ks[0], (16, 1024, Q_DIM), jnp.float32), 'key': jax.random.normal(ks[1], (16, 1024, K_DIM), jnp.float32), 'value': jax.random.normal(ks[2], (16, 1024, V_DIM), jnp.float32), 'Wq': jax.random.uniform(ks[3], (OUT_DIM, Q_DIM), jnp.float32, -s(Q_DIM), s(Q_DIM)), 'bq': jax.random.uniform(ks[4], (OUT_DIM,), jnp.float32, -s(Q_DIM), s(Q_DIM)), 'Wk': jax.random.uniform(ks[5], (OUT_DIM, K_DIM), jnp.float32, -s(K_DIM), s(K_DIM)), 'bk': jax.random.uniform(ks[6], (OUT_DIM,), jnp.float32, -s(K_DIM), s(K_DIM)), 'Wv': jax.random.uniform(ks[7], (OUT_DIM, V_DIM), jnp.float32, -s(V_DIM), s(V_DIM)), 'bv': jax.random.uniform(ks[8], (OUT_DIM,), jnp.float32, -s(V_DIM), s(V_DIM))}
    _L1_xattn_all = _L1_xattn_setup()
    _L1_xattn_in = {k: v for k, v in _L1_xattn_all.items() if k in ('Wq', 'bq', 'Wk', 'bk', 'Wv', 'bv')}
    del _L1_xattn_all

    def _L1_ffn_setup():
        import jax, jax.numpy as jnp
        import numpy as np
        IN_F, OUT_F, BLOCK, NBLK = (512, 2048, 128, 16)
        TOPK = NBLK // 4
        key = jax.random.key(seed)
        ks = jax.random.split(key, 7)
        s = 1.0 / np.sqrt(IN_F)
        s2 = 1.0 / np.sqrt(OUT_F)
        return {'x': jax.random.normal(ks[0], (4, 2048, IN_F), jnp.float32), 'router_w': jax.random.uniform(ks[1], (NBLK, IN_F), jnp.float32, -s, s), 'router_b': jax.random.uniform(ks[2], (NBLK,), jnp.float32, -s, s), 'w1': jax.random.uniform(ks[3], (OUT_F, IN_F), jnp.float32, -s, s), 'b1': jax.random.uniform(ks[4], (OUT_F,), jnp.float32, -s, s), 'w2': jax.random.uniform(ks[5], (IN_F, OUT_F), jnp.float32, -s2, s2), 'b2': jax.random.uniform(ks[6], (IN_F,), jnp.float32, -s2, s2)}
    _L1_ffn_all = _L1_ffn_setup()
    _L1_ffn_in = {k: v for k, v in _L1_ffn_all.items() if k in ('router_w', 'router_b', 'w1', 'b1', 'w2', 'b2')}
    del _L1_ffn_all
    return {'x': x, 'ctx_768': ctx_768, 'mask_BxS2_bf1': mask_BxS2_bf1, 'g_xattn': g_xattn, 'g_ffn': g_ffn, 'L0_xattn_Wq': _L0_xattn_in['Wq'], 'L0_xattn_Wk': _L0_xattn_in['Wk'], 'L0_xattn_Wv': _L0_xattn_in['Wv'], 'L0_xattn_Wo': _L0_xattn_in['Wo'], 'L0_ffn_w_gate': _L0_ffn_in['w_gate'], 'L0_ffn_w_up': _L0_ffn_in['w_up'], 'L0_ffn_w_down': _L0_ffn_in['w_down'], 'L1_xattn_Wq': _L1_xattn_in['Wq'], 'L1_xattn_bq': _L1_xattn_in['bq'], 'L1_xattn_Wk': _L1_xattn_in['Wk'], 'L1_xattn_bk': _L1_xattn_in['bk'], 'L1_xattn_Wv': _L1_xattn_in['Wv'], 'L1_xattn_bv': _L1_xattn_in['bv'], 'L1_ffn_router_w': _L1_ffn_in['router_w'], 'L1_ffn_router_b': _L1_ffn_in['router_b'], 'L1_ffn_w1': _L1_ffn_in['w1'], 'L1_ffn_b1': _L1_ffn_in['b1'], 'L1_ffn_w2': _L1_ffn_in['w2'], 'L1_ffn_b2': _L1_ffn_in['b2']}

def reference(x, ctx_768, mask_BxS2_bf1, g_xattn, g_ffn, L0_xattn_Wq, L0_xattn_Wk, L0_xattn_Wv, L0_xattn_Wo, L0_ffn_w_gate, L0_ffn_w_up, L0_ffn_w_down, L1_xattn_Wq, L1_xattn_bq, L1_xattn_Wk, L1_xattn_bk, L1_xattn_Wv, L1_xattn_bv, L1_ffn_router_w, L1_ffn_router_b, L1_ffn_w1, L1_ffn_b1, L1_ffn_w2, L1_ffn_b2):
    import jax
    import jax.numpy as jnp

    def _L0_xattn_ref(x, context, context_mask, Wq, Wk, Wv, Wo):
        import jax, jax.numpy as jnp
        import numpy as np
        DIM = 512
        CTX_DIM = 384
        HEADS = 16
        B, N, _ = x.shape
        M = context.shape[1]
        hd = DIM // HEADS
        scale = hd ** (-0.5)
        q = (x @ Wq).reshape(B, N, HEADS, hd).transpose(0, 2, 1, 3)
        k = (context @ Wk).reshape(B, M, HEADS, hd).transpose(0, 2, 1, 3)
        v = (context @ Wv).reshape(B, M, HEADS, hd).transpose(0, 2, 1, 3)
        scores = jnp.einsum('bhid,bhjd->bhij', q, k) * scale
        max_neg = -jnp.finfo(scores.dtype).max
        scores = jnp.where(context_mask[:, None, None, :], scores, max_neg)
        attn = jax.nn.softmax(scores, axis=-1)
        out = jnp.einsum('bhij,bhjd->bhid', attn, v)
        out = out.transpose(0, 2, 1, 3).reshape(B, N, DIM)
        return out @ Wo

    def _L0_ffn_ref(x, w_gate, w_up, w_down):
        import jax, jax.numpy as jnp
        import numpy as np
        BLOCK = 32
        W_BITS = 4
        ACT_BITS = 16

        def act_qdq(x):
            qmax = 2.0 ** (ACT_BITS - 1) - 1.0
            scale = jnp.maximum(jnp.max(jnp.abs(x)) / qmax, 1e-12)
            return jnp.clip(jnp.round(x / scale), -qmax - 1.0, qmax) * scale

        def fixed_qdq_u16(x):
            scale = 1.0 / 65536.0
            return jnp.clip(jnp.round(x / scale), 0.0, 65535.0) * scale

        def lpbq_dequant(w):
            O, I = w.shape
            qmax = 2.0 ** (W_BITS - 1) - 1.0
            wb = w.reshape(O, I // BLOCK, BLOCK)
            s = jnp.maximum(jnp.max(jnp.abs(wb), axis=-1, keepdims=True) / qmax, 1e-12)
            wq = jnp.clip(jnp.round(wb / s), -qmax - 1.0, qmax) * s
            return wq.reshape(O, I)
        x = act_qdq(x)
        up = act_qdq(x @ lpbq_dequant(w_up).T)
        gate = act_qdq(x @ lpbq_dequant(w_gate).T)
        sig = fixed_qdq_u16(jax.nn.sigmoid(gate))
        gate = act_qdq(gate * sig)
        o = act_qdq(gate * up)
        return o @ lpbq_dequant(w_down).T

    def _L1_xattn_ref(query, key, value, Wq, bq, Wk, bk, Wv, bv):
        import jax, jax.numpy as jnp
        import numpy as np
        Q_DIM, K_DIM, V_DIM, OUT_DIM = (512, 384, 384, 512)
        scale = OUT_DIM ** (-0.5)
        q = jnp.einsum('bsd,od->bso', query, Wq) + bq
        k = jnp.einsum('bsd,od->bso', key, Wk) + bk
        v = jnp.einsum('bsd,od->bso', value, Wv) + bv
        scores = jnp.einsum('bqo,bko->bqk', q, k) * scale
        probs = jax.nn.softmax(scores, axis=-1)
        return jnp.einsum('bqk,bko->bqo', probs, v)

    def _L1_ffn_ref(x, router_w, router_b, w1, b1, w2, b2):
        import jax, jax.numpy as jnp
        import numpy as np
        IN_F, OUT_F, BLOCK, NBLK = (512, 2048, 128, 16)
        TOPK = NBLK // 4
        x_shape = x.shape
        xf = x.reshape(-1, IN_F)
        n = xf.shape[0]
        prob = jax.nn.softmax(xf @ router_w.T + router_b, axis=-1)
        _, idx = jax.lax.top_k(prob, TOPK)
        mask = jnp.zeros((n, NBLK), bool).at[jnp.arange(n)[:, None], idx].set(True)
        w1b = w1.reshape(NBLK, BLOCK, IN_F)
        b1b = b1.reshape(NBLK, BLOCK)
        h = jnp.einsum('nd,ibd->nib', xf, w1b) + b1b
        h = jnp.where(mask[:, :, None], h, jnp.zeros((), h.dtype))
        h = jax.nn.relu(h)
        w2b = w2.reshape(IN_F, NBLK, BLOCK)
        y = jnp.einsum('nib,dib->nd', jnp.where(mask[:, :, None], h, 0.0), w2b) + b2
        return y.reshape(x_shape)
    x = x + jnp.tanh(g_xattn[0]) * _L0_xattn_ref(_layernorm(x, axis=-1), ctx_768, mask_BxS2_bf1, L0_xattn_Wq, L0_xattn_Wk, L0_xattn_Wv, L0_xattn_Wo)
    x = x + jnp.tanh(g_ffn[0]) * _L0_ffn_ref(_layernorm(x, axis=-1), L0_ffn_w_gate, L0_ffn_w_up, L0_ffn_w_down)
    x = x + jnp.tanh(g_xattn[1]) * _L1_xattn_ref(_layernorm(x, axis=-1), ctx_768, ctx_768, L1_xattn_Wq, L1_xattn_bq, L1_xattn_Wk, L1_xattn_bk, L1_xattn_Wv, L1_xattn_bv)
    x = x + jnp.tanh(g_ffn[1]) * _L1_ffn_ref(_layernorm(x, axis=-1), L1_ffn_router_w, L1_ffn_router_b, L1_ffn_w1, L1_ffn_b1, L1_ffn_w2, L1_ffn_b2)
    return x

_drawn_inputs = setup_inputs


def setup_inputs(seed=0):
    import zlib

    import numpy as np

    out = dict(_drawn_inputs(seed))
    spreads = {'g_ffn': (-1.0, 0.6)}
    factors = {'L1_xattn_bq': 31.701,
     'L1_xattn_bk': 64.0,
     'L1_ffn_router_b': 3.214,
     'L1_ffn_b1': 8.0,
     'L1_ffn_b2': 6.025}
    for name, (base, spread) in spreads.items():
        noise = np.random.default_rng([zlib.crc32(name.encode()), seed]).standard_normal(out[name].shape)
        drawn = base * np.exp(spread * noise) if base else spread * noise
        out[name] = jnp.asarray(drawn.astype(out[name].dtype))
    for name, factor in factors.items():
        out[name] = (out[name] * factor).astype(out[name].dtype)
    return out
```

```python
from contextlib import ExitStack

import concourse.bass as bass
from concourse import mybir

F32 = mybir.dt.float32
F32R = mybir.dt.float32r
BF16 = mybir.dt.bfloat16
F16 = mybir.dt.float16
ALU = mybir.AluOpType
ACT = mybir.ActivationFunctionType
AX = mybir.AxisListType

B, S, D = 16, 224, 512
TOK = B * S
M, C = 750, 384
H, HD = 16, 32
I0 = 1536
I1, NBLK = 2048, 16
DC, CC = D // 128, C // 128
KC, KP = 6, 125
NH = 376
HALVES = (slice(0, NH), slice(NH, M))
COVER = (slice(0, NH), slice(M - NH, M))
EPS = 1e-5
QMAX = 32767.0
ROUND = 12582912.0
G5 = TOK // 512
PASSES = ((0, 0), (0, 1), (1, 0))


def width(half):
    return HALVES[half].stop - HALVES[half].start


class Stage:

    def __init__(self, nc, sems, name):
        self.nc, self.sems, self.name, self.stack = nc, sems, name, ExitStack()

    def __enter__(self):
        self.stack.__enter__()
        return self

    def __exit__(self, *what):
        return self.stack.__exit__(*what)

    def sb(self, name, shape, dt=F32):
        return self.stack.enter_context(self.nc.sbuf_tensor(f"{self.name}_{name}", shape, dt))

    def ps(self, name, shape=(128, 512), dt=F32):
        return self.stack.enter_context(self.nc.psum_tensor(f"{self.name}_{name}", list(shape), dt))

    def sem(self, name):
        self.sems.append(self.nc.alloc_semaphore(name=f"{self.name}_{name}"))
        return self.sems[-1]


def clear(nc, sems):
    nc.clear_and_free_semaphores(sems)
    sems.clear()
    nc.all_engine_barrier()


def pairs(eng, first, end, body):
    rounds = (end - first) // 2
    if rounds:
        with eng.Fori(0, rounds) as r:
            body(2 * r + first, first % 2, r + first // 2)
            body(2 * r + first + 1, (first + 1) % 2, r + (first + 1) // 2)
    if 2 * rounds < end - first:
        body(end - 1, (end - 1) % 2, (end - 1) // 2)


class Norm:

    def __init__(self, st, rt, nt=4):
        self.rt, self.nt = rt, nt
        self.stats = st.sb("ln_stats", [128, nt, 6])
        (self.total, self.apart, self.m2, self.mean, self.apart2, self.m2e, self.ve, self.sd, self.r0,
         self.a, self.b, self.c, self.r) = (st.sb(f"ln_{n}", [128, nt]) for n in (
             "total", "apart", "m2", "mean", "apart2", "m2e", "ve", "sd", "r0", "a", "b", "c", "r"))
        self.dve = st.sem("ln_dve")
        self.var_ready = st.sem("ln_var_ready")
        self.sd_ready = st.sem("ln_sd_ready")

    def vector(self, v, g, x, y, out_ready):
        rt, nt = self.rt, self.nt
        at = g * (11 + nt) + nt
        for j in range(nt):
            v.bn_stats(self.stats[:rt, j, :], x[:rt, j, :]).then_inc(self.dve, 1)
        v.wait_ge(self.dve, at)
        even, odd = self.stats[:rt, :, 1], self.stats[:rt, :, 4]
        v.tensor_tensor(self.total[:rt, :], even, odd, ALU.add).then_inc(self.dve, 1)
        v.tensor_tensor(self.apart[:rt, :], even, odd, ALU.subtract).then_inc(self.dve, 1)
        v.tensor_tensor(self.m2[:rt, :], self.stats[:rt, :, 2], self.stats[:rt, :, 5], ALU.add).then_inc(self.dve, 1)
        v.wait_ge(self.dve, at + 3)
        v.tensor_scalar(self.mean[:rt, :], self.total[:rt, :], 0.5, None, ALU.mult).then_inc(self.dve, 1)
        v.tensor_tensor(self.apart2[:rt, :], self.apart[:rt, :], self.apart[:rt, :], ALU.mult).then_inc(self.dve, 1)
        v.tensor_scalar(self.m2e[:rt, :], self.m2[:rt, :], 1.0 / D, EPS, ALU.mult, ALU.add).then_inc(self.dve, 1)
        v.wait_ge(self.dve, at + 6)
        v.scalar_tensor_tensor(self.ve[:rt, :], self.apart2[:rt, :], 0.25, self.m2e[:rt, :], ALU.mult, ALU.add).then_inc(self.var_ready, 1)
        v.wait_ge(self.sd_ready, g + 1)
        v.reciprocal(self.r0[:rt, :], self.sd[:rt, :]).then_inc(self.dve, 1)
        v.wait_ge(self.dve, at + 7)
        v.tensor_tensor(self.a[:rt, :], self.r0[:rt, :], self.r0[:rt, :], ALU.mult).then_inc(self.dve, 1)
        v.wait_ge(self.dve, at + 8)
        v.tensor_tensor(self.b[:rt, :], self.a[:rt, :], self.ve[:rt, :], ALU.mult).then_inc(self.dve, 1)
        v.wait_ge(self.dve, at + 9)
        v.tensor_scalar(self.c[:rt, :], self.b[:rt, :], -0.5, 1.5, ALU.mult, ALU.add).then_inc(self.dve, 1)
        v.wait_ge(self.dve, at + 10)
        v.tensor_tensor(self.r[:rt, :], self.r0[:rt, :], self.c[:rt, :], ALU.mult).then_inc(self.dve, 1)
        v.wait_ge(self.dve, at + 11)
        for j in range(nt):
            v.tensor_scalar(y[:rt, j, :], x[:rt, j, :], self.mean[:rt, j:j + 1], self.r[:rt, j:j + 1],
                            ALU.subtract, ALU.mult).then_inc(out_ready, 1)

    def scalar(self, a, g):
        a.wait_ge(self.var_ready, g + 1)
        a.activation(self.sd[:self.rt, :], self.ve[:self.rt, :], ACT.Sqrt).then_inc(self.sd_ready, 1)


class Turn:

    def __init__(self, st, rt, n, src_ready, per_group=4):
        self.rt, self.n, self.w = rt, n, 4 * rt
        self.src_ready, self.per = src_ready, per_group
        self.bank = st.ps("turn", (128, 2, 512))
        self.hi = [st.sb(f"turn_hi{k}", [128, n, self.w], F32R) for k in range(2)]
        self.lo = [st.sb(f"turn_lo{k}", [128, n, self.w], F32R) for k in range(2)]
        self.turned = st.sem("turned")
        self.hi_ready = st.sem("turn_hi")
        self.lo_ready = st.sem("turn_lo")

    def tensor(self, t, g, src, ident):
        if self.src_ready is not None:
            t.wait_ge(self.src_ready, self.per * (g + 1))
        rt = self.rt
        for d in range(self.n):
            use = g * self.n + d
            if not (isinstance(use, int) and use < 2):
                t.wait_ge(self.lo_ready, use - 1)
            for j in range(4):
                last = t.transpose(self.bank[:, use_bank(d), j * rt:(j + 1) * rt],
                                   src[:rt, j, d * 128:(d + 1) * 128], ident[:rt, :rt])
            last.then_inc(self.turned, 1)

    def scalar(self, a, g, k, free=None):
        if free is not None:
            a.wait_ge(*free)
        for d in range(self.n):
            a.wait_ge(self.turned, g * self.n + d + 1)
            a.activation(self.hi[k][:, d, :], self.bank[:, use_bank(d), 0:self.w], ACT.Copy).then_inc(self.hi_ready, 1)

    def vector(self, v, g, k):
        for d in range(self.n):
            v.wait_ge(self.hi_ready, g * self.n + d + 1)
            v.tensor_tensor(self.lo[k][:, d, :], self.bank[:, use_bank(d), 0:self.w],
                            self.hi[k][:, d, :].bitcast(F32), ALU.subtract).then_inc(self.lo_ready, 1)


def use_bank(d):
    return d % 2


def split_weights(v, raw, hi, lo, chain, at):
    v.tensor_copy(hi, raw).then_inc(chain, 1)
    v.wait_ge(chain, at + 1)
    v.tensor_tensor(lo, raw, hi.bitcast(F32), ALU.subtract).then_inc(chain, 1)


def project_queries(nc, sems, x, wq, ident_d, q_parts):
    with Stage(nc, sems, "q0") as st:
        ident = st.sb("ident", [128, 128])
        w_raw = st.sb("w_raw", [128, DC, D])
        w = [st.sb("w_hi", [128, DC, D], F32R), st.sb("w_lo", [128, DC, D], F32R)]
        xt = [st.sb(f"x{k}", [128, 4, D]) for k in range(2)]
        q_hi = [st.sb(f"q_hi{k}", [128, 4, 512], F32R) for k in range(2)]
        q_lo = [st.sb(f"q_lo{k}", [128, 4, 512], F32R) for k in range(2)]
        out = st.ps("out", (128, 4, 512))
        x_in = [st.sem(f"x_in{k}") for k in range(2)]
        q_out = [st.sem(f"q_out{k}") for k in range(2)]
        ident_in, w_in, xn_ready = st.sem("ident_in"), st.sem("w_in"), st.sem("xn_ready")
        w_split, mm_done = st.sem("w_split"), st.sem("mm_done")
        qh_ready, ql_ready = st.sem("qh_ready"), st.sem("ql_ready")
        norm, turn = Norm(st, 128), Turn(st, 128, DC, xn_ready)
        block = st.stack.enter_context(nc.Block())

        @block.sync
        def _(sp):
            def load(g, k, u):
                if not (isinstance(g, int) and g < 2):
                    sp.wait_ge(turn.turned, 4 * g - 4)
                sp.dma_start(xt[k][:], x[bass.ds(g * 512, 512), :].rearrange("(j p) c -> p j c", p=128)).then_inc(x_in[k], 16)
            def store(g, k, u):
                sp.wait_ge(qh_ready, 4 * g + 4)
                sp.dma_start(q_parts[0][:, bass.ds(g * 512, 512)].rearrange("(c p) t -> p c t", p=128), q_hi[k][:].bitcast(F32)).then_inc(q_out[k], 16)
                sp.wait_ge(ql_ready, 4 * g + 4)
                sp.dma_start(q_parts[1][:, bass.ds(g * 512, 512)].rearrange("(c p) t -> p c t", p=128), q_lo[k][:].bitcast(F32)).then_inc(q_out[k], 16)

            def step(g, k, u):
                load(g + 2, k, u + 1)
                store(g, k, u)
            load(0, 0, 0)
            sp.dma_start(ident[:], ident_d).then_inc(ident_in, 16)
            sp.dma_start(w_raw[:], wq.rearrange("(c p) n -> p c n", p=128)).then_inc(w_in, 16)
            load(1, 1, 0)
            sp.sem_inc(q_out[0], 32)
            sp.sem_inc(q_out[1], 32)
            pairs(sp, 0, G5 - 2, step)
            store(G5 - 2, 1, 2)
            store(G5 - 1, 0, 3)
            sp.wait_ge(q_out[0], 32 + 32 * 4)
            sp.wait_ge(q_out[1], 32 + 32 * 3)

        @block.scalar
        def _(a):
            def step(g, k, u, more=True):
                if more:
                    norm.scalar(a, g + 1)
                for o in range(4):
                    if o == 2 and more:
                        turn.scalar(a, g + 1, 1 - k, (mm_done, 4 * g) if not isinstance(g, int) or g else None)
                    if o == 0:
                        a.wait_ge(q_out[k], 32 * u + 32)
                    a.wait_ge(mm_done, 4 * g + o + 1)
                    a.activation(q_hi[k][:, o, :], out[:, o, :], ACT.Copy).then_inc(qh_ready, 1)
            norm.scalar(a, 0)
            turn.scalar(a, 0, 0)
            step(0, 0, 0)
            pairs(a, 1, G5 - 1, step)
            step(G5 - 1, 0, 3, False)

        @block.vector
        def _(v):
            def front(g, k, u):
                v.wait_ge(x_in[k], 16 * u + 16)
                norm.vector(v, g, xt[k], xt[k], xn_ready)

            def step(g, k, u, more=True):
                if more:
                    front(g + 1, 1 - k, u + k)
                for o in range(4):
                    if o == 2 and more:
                        turn.vector(v, g + 1, 1 - k)
                    v.wait_ge(qh_ready, 4 * g + o + 1)
                    v.tensor_tensor(q_lo[k][:, o, :], out[:, o, :], q_hi[k][:, o, :].bitcast(F32), ALU.subtract).then_inc(ql_ready, 1)
            front(0, 0, 0)
            turn.vector(v, 0, 0)
            v.wait_ge(w_in, 16)
            split_weights(v, w_raw[:], w[0][:], w[1][:], w_split, 0)
            step(0, 0, 0)
            pairs(v, 1, G5 - 1, step)
            step(G5 - 1, 0, 3, False)

        @block.tensor
        def _(t):
            def step(g, k, u, more=True):
                x2 = (turn.hi[k], turn.lo[k])
                for o in range(4):
                    if o == 2 and more:
                        turn.tensor(t, g + 1, xt[1 - k], ident)
                    if o == 0:
                        t.wait_ge(turn.lo_ready, 4 * g + 4)
                    if not isinstance(g, int) or g:
                        t.wait_ge(ql_ready, 4 * g - 3 + o)
                    for n, (pw, px) in enumerate(PASSES):
                        for d in range(DC):
                            mm = t.matmul(out[:, o, :], w[pw][:, d, o * 128:(o + 1) * 128], x2[px][:, d, :],
                                          start=(n == 0 and d == 0), stop=(n == 2 and d == DC - 1))
                    mm.then_inc(mm_done, 1)
            t.wait_ge(ident_in, 16)
            turn.tensor(t, 0, xt[0], ident)
            t.wait_ge(w_split, 2)
            step(0, 0, 0)
            pairs(t, 1, G5 - 1, step)
            step(G5 - 1, 0, 3, False)



NEG = -2.0 ** 127
VW = 98
CH = 4


def attention_fills(c, h, last):
    def later(n):
        return (c + n) % CH, (c + n) // CH
    side = []
    if (c, h) in ((0, 0), (1, 2)):
        side = [("K", *later(3), 0), ("K", *later(3), 1)]
    elif c > 1 and h < 2:
        side = [("K", *later(3), h)]
    if c == 0:
        side += [("V", 1, 0, kc) for kc in ((0,), (1, 2, 3), (4, 5), ())[h]]
    elif c > 1 and h > 1:
        side += [("V", 0, 1, 3 * (c - 2) + kc) for kc in ((0, 1), (2,))[h - 2]]
    maxima = [("max", *later(2), h, qt, half) for qt in range(2) for half in range(2)]
    out = [("mT", *later(1))] if h == 0 else []
    for n in range(max(len(side), len(maxima))):
        out += side[n:n + 1] + maxima[n:n + 1]
    next_batch = {"K": 2, "V": 2, "max": 2, "mT": 2}
    return [p for p in out if not (last and p[next_batch[p[0]]])]


def attention_order():
    first = [("K", c, 0, half) for c in range(3) for half in range(2)] + [("V", 0, 0, kc) for kc in range(KC)]
    first += [("max", c, 0, h, qt, half) for c in range(2) for h in range(4) for qt in range(2) for half in range(2)]
    first += [("mT", 0, 0)]
    batch = [(c, h, attention_fills(c, h, False)) for c in range(CH) for h in range(4)]
    return first, batch


def attend0(nc, sems, ctx_t, mask, wk, wv, q_parts, mask_row, some_row, ident_d, attn):
    with Stage(nc, sems, "a0") as st:
        first, batch = attention_order()
        P0 = len(first)
        PB = sum(len(f) for _, _, f in batch)
        assert P0 % 3 == 0 and PB % 3 == 1

        ident = st.sb("ident", [128, 128])
        zero = st.sb("zero", [128, M])
        w_raw = st.sb("w_raw", [128, CC, D])
        wk2 = [st.sb(f"wk{p}", [128, CC, D], F32R) for p in range(2)]
        wv2 = [st.sb(f"wv{p}", [128, CC, D], F32R) for p in range(2)]
        c_raw = st.sb("c_raw", [128, CC, M])
        c2 = [st.sb(f"c{p}", [128, CC, M], F32R) for p in range(2)]
        k_hi = [st.sb(f"k_hi{k}", [128, M], F32R) for k in range(2)]
        k_lo = [st.sb(f"k_lo{k}", [128, M], F32R) for k in range(2)]
        keys = [st.sb(f"keys{c}", [128, 4, M], F32R) for c in range(CH)]
        queries = [st.sb(f"queries{c}", [128, 4, S], F32R) for c in range(CH)]
        vals = st.sb("vals", [128, KC, H, VW], BF16)
        v_rest = [st.sb(f"v_rest{k}", [128, 256]) for k in range(2)]
        mx = [st.sb(f"mx{k}", [112, 8, 2]) for k in range(2)]
        neg_max = [st.sb(f"neg_max{k}", [112, 8]) for k in range(2)]
        m_rows = [st.sb(f"m_rows{k}", [8, 112], F32R) for k in range(2)]
        p32 = [st.sb(f"p32_{k}", [128, KC * S]) for k in range(2)]
        p_hi = [st.sb(f"p_hi{k}", [128, KC * S], F16) for k in range(2)]
        p_lo = [st.sb(f"p_lo{k}", [128, KC * S], F16) for k in range(2)]
        o_sum = st.sb("o_sum", [112, 4, HD])
        o_rec = st.sb("o_rec", [112, 4])
        o_out = [st.sb(f"o_out{k}", [112, 2, 128]) for k in range(2)]
        mask_u8 = st.sb("mask_u8", [B, M], mybir.dt.uint8)
        some = st.sb("some", [B, 1])
        some_all = st.sb("some_all", [128, B])
        some_now = st.sb("some_now", [128, 1])
        mask_f = st.sb("mask_f", [B, M])

        fill = [st.ps(f"fill{k}") for k in range(3)]
        score = [st.ps(f"score{k}") for k in range(3)]
        out = [st.ps(f"out{k}") for k in range(2)]

        zero_set = st.sem("zero_set")
        some_in, some_set = st.sem("some_in"), st.sem("some_set")
        prep_in, mask_ready, mask_stored = st.sem("prep_in"), st.sem("mask_ready"), st.sem("mask_stored")
        wv_in, w_split, ones_set = st.sem("wv_in"), st.sem("w_split"), st.sem("ones_set")
        c_in, c_ready, c_step = st.sem("c_in"), st.sem("c_ready"), st.sem("c_step")
        keys_in = [st.sem(f"keys_in{c}") for c in range(CH)]
        q_in = [st.sem(f"q_in{c}") for c in range(CH)]
        m_in = [st.sem(f"m_in{c}") for c in range(CH)]
        filled, fill_free = st.sem("filled"), st.sem("fill_free")
        side_hi = st.sem("side_hi")
        v_mid, v_ready = st.sem("v_mid"), st.sem("v_ready")
        m_ready = st.sem("m_ready")
        score_full, exp_done = st.sem("score_full"), st.sem("exp_done")
        hi_done, lo_done, pv_done = st.sem("hi_done"), st.sem("lo_done"), st.sem("pv_done")
        norm_step, o_ready = st.sem("norm_step"), st.sem("o_ready")
        o_stored = [st.sem(f"o_stored{k}") for k in range(2)]

        SIDE0 = sum(p[0] in "KV" for p in first)
        SIDEB = sum(p[0] in "KV" for _, _, f in batch for p in f)
        V0 = sum(p[0] == "V" for p in first)
        VB = sum(p[0] == "V" for _, _, f in batch for p in f)

        class Place:

            def __init__(self, b=None):
                self.at = 0 if b is None else P0 + PB * b
                self.side = 0 if b is None else SIDE0 + SIDEB * b
                self.v = 0 if b is None else V0 + VB * b
                self.local = 1 if b is None else 0
                self.start = b is not None
                self.some = 1 if b is None else b + 2

            def next(self, piece):
                self.at, self.local = self.at + 1, self.local + 1
                if piece[0] in "KV":
                    self.side = self.side + 1
                if piece[0] == "V":
                    self.v = self.v + 1

            @property
            def bank(self):
                return self.local % 3

            @property
            def previous(self):
                if self.start and self.local < 3:
                    return self.at - (0, 3, 3)[self.local]
                return self.at - 2

        def steps(eng, step, before, between=None):
            place = Place()
            for piece in first:
                before(piece, place)
                place.next(piece)
            if between:
                between()

            def of_batch(b, last):
                place = Place(b)
                for c in range(CH):
                    for h in range(4):
                        step(b, c, h, place, last)
            with eng.Fori(0, B - 1) as b:
                of_batch(b, False)
            of_batch(B - 1, True)

        def heads_after(c, h):
            return (c + (h + 1) // 4) % CH, (h + 1) % 4, (4 * c + h + 1) // 16

        block = st.stack.enter_context(nc.Block())

        @block.sync
        def _(sp):
            def load_queries(c, b):
                for part, rows in ((0, 0), (0, 32), (1, 64)):
                    sp.dma_start(queries[c][rows:rows + 32, :, :].bitcast(F32),
                                 q_parts[part][c * 128:(c + 1) * 128, bass.ds(b * S, S)].rearrange("(h p) t -> p h t", p=32)).then_inc(q_in[c], 16)

            def load_mask(c, b):
                sp.dma_start(keys[c][96:97, :, :].bitcast(F32),
                             mask_row[bass.ds(b, 1), :].unsqueeze(1).broadcast_to([1, 4, M])).then_inc(keys_in[c], 16)

            def load_context(b):
                sp.dma_start(c_raw[:], ctx_t[bass.ds(b, 1), :, :].rearrange("a (c p) m -> p (a c) m", p=128)).then_inc(c_in, 16)

            def stack_keys(c, place):
                k = c % 2
                sp.wait_ge(side_hi, place.side)
                for h in range(4):
                    for rows in (0, 64):
                        sp.dma_start(keys[c][rows:rows + 32, h, :].bitcast(F32), k_hi[k][32 * h:32 * h + 32, :].bitcast(F32)).then_inc(keys_in[c], 16)
                sp.wait_ge(fill_free, place.at)
                for h in range(4):
                    sp.dma_start(keys[c][32:64, h, :].bitcast(F32), k_lo[k][32 * h:32 * h + 32, :].bitcast(F32)).then_inc(keys_in[c], 16)

            sp.dma_start(mask_u8[:], mask).then_inc(prep_in, 16)
            load_context(0)
            sp.dma_start(w_raw[:], wk.rearrange("(c p) n -> p c n", p=128)).then_inc(prep_in, 16)
            sp.dma_start(ident[:], ident_d).then_inc(prep_in, 16)
            sp.wait_ge(mask_ready, 2)
            sp.dma_start(mask_row, mask_f[:]).then_inc(mask_stored, 16)
            sp.dma_start(some_row.unsqueeze(1), some[:]).then_inc(mask_stored, 16)
            sp.wait_ge(w_split, 2)
            sp.dma_start(w_raw[:], wv.rearrange("(c p) n -> p c n", p=128)).then_inc(wv_in, 16)
            sp.wait_ge(mask_stored, 32)
            sp.dma_start(some_all[:], some_row.partition_broadcast(128)).then_inc(some_in, 16)
            sp.wait_ge(ones_set, 9)
            for c in range(3):
                load_queries(c, 0)
                load_mask(c, 0)
            sp.sem_inc(o_stored[0], 16)
            sp.sem_inc(o_stored[1], 16)

            def before(piece, place):
                if piece[0] == "K" and piece[3] == 1:
                    after = Place()
                    after.at, after.side = place.at + 1, place.side + 1
                    stack_keys(piece[1], after)
                if piece[0] == "mT":
                    sp.wait_ge(fill_free, place.at + 1)
                    sp.dma_start(queries[0][97:98, :, :].rearrange("p h (q t) -> p (h q) t", q=2).bitcast(F32), m_rows[0][:].bitcast(F32)).then_inc(m_in[0], 16)

            def step(b, c, h, place, last):
                if h == 0:
                    nc_, nb = (c + 3) % CH, (c + 3) // CH
                    if not (last and nb):
                        sp.wait_ge(score_full, 3 * (16 * b + 4 * c) + 3)
                        load_queries(nc_, b + nb)
                        load_mask(nc_, b + nb)
                    if c == 0 and not last:
                        sp.wait_ge(c_ready, b + 1)
                        load_context(b + 1)
                for piece in attention_fills(c, h, last):
                    place.next(piece)
                    if piece[0] == "K" and piece[3] == 1:
                        stack_keys(piece[1], place)
                    if piece[0] == "mT":
                        target, ahead = piece[1], piece[2]
                        sp.wait_ge(fill_free, place.at)
                        sp.dma_start(queries[target][97:98, :, :].rearrange("p h (q t) -> p (h q) t", q=2).bitcast(F32),
                                     m_rows[target % 2][:].bitcast(F32)).then_inc(m_in[target], 16)
                if h == 0 and c > 0:
                    store(c - 1, b)
                if (c, h) == (3, 3):
                    store(c, b)

            def store(c, b):
                sp.wait_ge(o_ready, 8 * b + 2 * c + 4)
                sp.dma_start(attn[bass.ds(b * S, S), c * 128:(c + 1) * 128].rearrange("(q p) n -> p q n", p=112),
                             o_out[c % 2][:]).then_inc(o_stored[c % 2], 16)

            steps(sp, step, before)
            sp.wait_ge(o_stored[0], 16 + 32 * B)
            sp.wait_ge(o_stored[1], 16 + 32 * B)

        @block.gpsimd
        def _(pool):
            pool.memset(vals[:, :, :, 96:98], 1.0).then_inc(ones_set, 1)
            pool.memset(zero[:], 0.0).then_inc(zero_set, 1)
            pool.wait_ge(zero_set, 1)

            def split_context(b):
                pool.wait_ge(c_in, 16 * b + 16)
                pool.tensor_tensor(c2[0][:], c_raw[:], zero[:].unsqueeze(1).broadcast_to([128, CC, M]), ALU.add).then_inc(c_step, 1)
                pool.wait_ge(c_step, b + 1)
                pool.tensor_tensor(c2[1][:], c_raw[:], c2[0][:].bitcast(F32), ALU.subtract).then_inc(c_ready, 1)

            def value(piece, place):
                half, kc = piece[1], piece[3]
                rest = v_rest[kc % 2][:KP, :].rearrange("p (h d) -> p h d", d=HD)
                mid = vals[:KP, kc, 8 * half:8 * half + 8, 32:64]
                pool.wait_ge(fill_free, place.at + 1)
                pool.tensor_tensor(mid, rest, zero[:KP, 0:256].rearrange("p (h d) -> p h d", d=HD), ALU.add).then_inc(v_mid, 1)
                pool.wait_ge(v_mid, place.v + 1)
                pool.tensor_tensor(vals[:KP, kc, 8 * half:8 * half + 8, 64:96], rest, mid, ALU.subtract).then_inc(v_ready, 1)

            def before(piece, place):
                if piece[0] == "V":
                    value(piece, place)

            def step(b, c, h, place, last):
                if (c, h) == (1, 0) and not last:
                    pool.wait_ge(filled, place.at)
                    split_context(b + 1)
                for piece in attention_fills(c, h, last):
                    if piece[0] == "V":
                        value(piece, place)
                    place.next(piece)
            split_context(0)
            steps(pool, step, before)

        @block.scalar
        def _(a):
            def exps(s, k):
                a.wait_ge(lo_done, s + 1)
                for j in range(3):
                    a.wait_ge(score_full, 3 * s + j + 1)
                    a.activation(p32[k][:KP, j * 448:(j + 1) * 448], score[j][:KP, 0:448], ACT.Exp, scale=HD ** -0.5).then_inc(exp_done, 1)
                a.wait_ge(pv_done, s + 1)
                a.wait_ge(exp_done, 3 * s + 6)
                a.activation(p_hi[k][:KP, :], p32[k][:KP, :], ACT.Copy).then_inc(hi_done, 1)

            def side(piece, place):
                if piece[0] == "K":
                    c, half = piece[1], piece[3]
                    a.wait_ge(filled, place.at + 1)
                    a.activation(k_hi[c % 2][:, HALVES[half]], fill[place.bank][:, 0:width(half)], ACT.Copy, scale=some_now[:, 0:1]).then_inc(side_hi, 1)
                if piece[0] == "V":
                    half, kc = piece[1], piece[3]
                    a.wait_ge(filled, place.at + 1)
                    a.activation(vals[:KP, kc, 8 * half:8 * half + 8, 0:32],
                                 fill[place.bank][:KP, 0:256].rearrange("p (h d) -> p h d", d=HD), ACT.Copy).then_inc(side_hi, 1)

            def free_before(piece, place, b):
                if piece[0] == "K" and piece[3] == 0:
                    c, ahead = piece[1], piece[2]
                    a.wait_ge(some_set, b + ahead + 1)
                    if c >= 2:
                        a.wait_ge(keys_in[c - 2], 208 * (b + ahead + 1))
                    elif not (isinstance(b, int) and b + ahead == 0):
                        a.wait_ge(keys_in[c + 2], 208 * (b + ahead))
                if piece[0] == "V" and b is not None:
                    half = piece[1]
                    if half == 0:
                        a.wait_ge(pv_done, 16 * b + 8 + 2)
                    elif not (isinstance(b, int) and b == 0):
                        a.wait_ge(pv_done, 16 * b + 2)

            def before(piece, place):
                if piece[0] == "K":
                    free_before(piece, place, 0)
                side(piece, place)

            def step(b, c, h, place, last):
                if not (last and (c, h) == (3, 3)):
                    exps(16 * b + 4 * c + h + 1, (h + 1) % 2)
                for piece in attention_fills(c, h, last):
                    free_before(piece, place, b)
                    side(piece, place)
                    place.next(piece)
            a.sem_inc(exp_done, 3)
            steps(a, step, before, lambda: exps(0, 0))

        @block.vector
        def _(v):
            v.sem_inc(lo_done, 2)
            v.sem_inc(o_ready, 2)
            v.wait_ge(prep_in, 48)
            v.tensor_scalar(mask_f[:], mask_u8[:], 1.0, -NEG, ALU.subtract, ALU.mult).then_inc(mask_ready, 1)
            v.tensor_reduce(some[:], mask_u8[:], AX.X, ALU.max).then_inc(mask_ready, 1)
            for c in range(CH):
                v.memset(keys[c][96:128, :, :].bitcast(F32), 1.0).then_inc(ones_set, 1)
                v.memset(queries[c][96:128, :, :].bitcast(F32), 1.0).then_inc(ones_set, 1)
            split_weights(v, w_raw[:], wk2[0][:], wk2[1][:], w_split, 0)
            v.wait_ge(wv_in, 16)
            split_weights(v, w_raw[:], wv2[0][:], wv2[1][:], w_split, 2)

            def take_some(b):
                v.tensor_copy(some_now[:], some_all[:, bass.ds(b, 1)]).then_inc(some_set, 1)

            v.wait_ge(some_in, 16)
            take_some(0)
            v.wait_ge(some_set, 1)

            def piece_of(piece, place):
                kind, bank = piece[0], fill[place.bank]
                if kind in "KV":
                    v.wait_ge(side_hi, place.side + 1)
                else:
                    v.wait_ge(filled, place.at + 1)
                if kind == "K":
                    if piece[1:] == (0, 1, 0):
                        v.wait_ge(some_set, place.some)
                    c, half = piece[1], piece[3]
                    part = HALVES[half]
                    v.scalar_tensor_tensor(k_lo[c % 2][:, part], bank[:, 0:width(half)], some_now[:, 0:1], k_hi[c % 2][:, part].bitcast(F32),
                                           ALU.mult, ALU.subtract).then_inc(fill_free, 1)
                elif kind == "V":
                    half, kc = piece[1], piece[3]
                    if not (isinstance(place.v, int) and place.v < 2):
                        v.wait_ge(v_ready, place.v - 1)
                    v.tensor_tensor(v_rest[kc % 2][:KP, :].rearrange("p (h d) -> p h d", d=HD),
                                    bank[:KP, 0:256].rearrange("p (h d) -> p h d", d=HD),
                                    vals[:KP, kc, 8 * half:8 * half + 8, 0:32], ALU.subtract).then_inc(fill_free, 1)
                elif kind == "max":
                    c, h, qt, half = piece[1], *piece[3:]
                    v.tensor_reduce(mx[c % 2][:, 2 * h + qt, half:half + 1], bank[:112, 0:NH], AX.X, ALU.max).then_inc(fill_free, 1)
                else:
                    v.tensor_copy(m_rows[piece[1] % 2][:], bank[:8, 0:112]).then_inc(fill_free, 1)

            def close_max(piece, place):
                if piece[0] == "max" and piece[3:] == (3, 1, 1):
                    k = piece[1] % 2
                    v.wait_ge(fill_free, place.at + 1)
                    v.tensor_reduce(neg_max[k][:], mx[k][:], AX.X, ALU.max, negate=True).then_inc(m_ready, 1)

            def low(s, k):
                v.wait_ge(hi_done, s + 1)
                if k is not None:
                    v.wait_ge(pv_done, s + 1)
                v.tensor_tensor(p_lo[k][:KP, :], p32[k][:KP, :], p_hi[k][:KP, :], ALU.subtract).then_inc(lo_done, 1)

            def normalise(n, pair, c, b):
                v.wait_ge(pv_done, 2 * n + 4)
                bank = out[pair][:112, 0:4 * 97].rearrange("p (x w) -> p x w", w=97)
                v.tensor_reduce(o_sum[:], bank[:, :, 0:96].rearrange("p x (s d) -> p x d s", s=3), AX.X, ALU.add).then_inc(norm_step, 1)
                v.reciprocal(o_rec[:], bank[:, :, 96]).then_inc(norm_step, 1)
                if pair == 0:
                    v.wait_ge(o_stored[c % 2], 32 * b + 16 * (c // 2) + 16)
                v.wait_ge(norm_step, 2 * n + 2)
                v.tensor_tensor(o_out[c % 2][:, :, 64 * pair:64 * pair + 64].rearrange("p q (h d) -> p q h d", d=HD),
                                o_sum[:].rearrange("p (q h) d -> p q h d", q=2),
                                o_rec[:].rearrange("p (q h) -> p q h", q=2).unsqueeze(3).broadcast_to([112, 2, 2, HD]),
                                ALU.mult).then_inc(o_ready, 1)

            def before(piece, place):
                piece_of(piece, place)
                close_max(piece, place)

            def step(b, c, h, place, last):
                if h in (0, 2) and (c, h) != (0, 0):
                    pc, pair = (c - 1, 1) if h == 0 else (c, 0)
                    normalise(8 * b + 2 * pc + pair, pair, pc, b)
                if (c, h) == (1, 0) and not last:
                    take_some(b + 1)
                for piece in attention_fills(c, h, last):
                    piece_of(piece, place)
                    close_max(piece, place)
                    place.next(piece)
                if not (last and (c, h) == (3, 3)):
                    low(16 * b + 4 * c + h + 1, (h + 1) % 2)
                if (c, h) == (3, 3):
                    normalise(8 * b + 7, 1, 3, b)

            steps(v, step, before, lambda: low(0, 0))

        @block.tensor
        def _(t):
            def product(piece, place, b):
                kind, bank = piece[0], fill[place.bank]
                c, ahead = piece[1], piece[2]
                if not (isinstance(place.at, int) and place.at < 3):
                    t.wait_ge(fill_free, place.previous)
                if kind == "K":
                    half = piece[3]
                    t.wait_ge(c_ready, b + ahead + 1)
                    for n, (pw, px) in enumerate(PASSES):
                        for d in range(CC):
                            mm = t.matmul(bank[:, 0:width(half)], wk2[pw][:, d, c * 128:(c + 1) * 128], c2[px][:, d, HALVES[half]],
                                          start=(n == 0 and d == 0), stop=(n == 2 and d == CC - 1))
                elif kind == "V":
                    half, kc = piece[1], piece[3]
                    t.wait_ge(c_ready, b + ahead + 1)
                    for n, (pw, px) in enumerate(PASSES):
                        for d in range(CC):
                            mm = t.matmul(bank[:KP, 0:256], c2[pw][:, d, kc * KP:(kc + 1) * KP], wv2[px][:, d, 256 * half:256 * half + 256],
                                          start=(n == 0 and d == 0), stop=(n == 2 and d == CC - 1))
                elif kind == "max":
                    h, qt, half = piece[3:]
                    if (h, qt, half) == (0, 0, 0):
                        t.wait_ge(keys_in[c], 208 * (b + ahead + 1))
                        t.wait_ge(q_in[c], 48 * (b + ahead + 1))
                    mm = t.matmul(bank[:112, 0:NH], queries[c][0:97, h, qt * 112:(qt + 1) * 112], keys[c][0:97, h, COVER[half]],
                                  start=True, stop=True)
                else:
                    t.wait_ge(m_ready, 4 * (b + ahead) + c + 1)
                    mm = t.transpose(bank[:8, 0:112], neg_max[c % 2][:], ident[:112, :112])
                mm.then_inc(filled, 1)

            def scores(s, b, c, h):
                if h == 0:
                    t.wait_ge(m_in[c], 16 * (b + 1))
                for j in range(3):
                    t.wait_ge(exp_done, 3 * s + j + 1)
                    for i in range(2):
                        kc = 2 * j + i
                        mm = t.matmul(score[j][:KP, i * S:(i + 1) * S], keys[c][0:98, h, kc * KP:(kc + 1) * KP], queries[c][0:98, h, :],
                                      start=True, stop=True)
                    mm.then_inc(score_full, 1)

            def weigh(s, b, c, h):
                t.wait_ge(lo_done, s + 3)
                if h % 2 == 0:
                    t.wait_ge(o_ready, 8 * b + 2 * c + h // 2 + 1)
                if h == 0 and c in (0, 2):
                    t.wait_ge(v_ready, V0 + VB * b + (0 if c == 0 else KC))
                for qt in range(2):
                    off = (2 * qt + h % 2) * 97
                    for kc in range(KC):
                        for n, part in enumerate((p_hi, p_lo)):
                            mm = t.matmul(out[h // 2][:112, off:off + 97], part[h % 2][:KP, kc * S + qt * 112:kc * S + qt * 112 + 112],
                                          vals[:KP, kc, 4 * c + h, 0:97], start=(kc == 0 and n == 0), stop=(kc == KC - 1 and n == 1))
                mm.then_inc(pv_done, 1)

            def step(b, c, h, place, last):
                s = 16 * b + 4 * c + h
                nc_, nh, ahead = heads_after(c, h)
                if not (last and ahead):
                    scores(s + 1, b + ahead, nc_, nh)
                for piece in attention_fills(c, h, last):
                    product(piece, place, b)
                    place.next(piece)
                weigh(s, b, c, h)

            t.sem_inc(pv_done, 2)
            t.wait_ge(prep_in, 48)
            t.wait_ge(w_split, 4)
            t.wait_ge(ones_set, 9)
            steps(t, step, lambda piece, place: product(piece, place, 0), lambda: scores(0, 0, 0, 0))


def load_weight(sp, raw, w, sem):
    sp.dma_start(raw[:], w.rearrange("(c p) n -> p c n", p=128)).then_inc(sem, 16)


def is_first(g):
    return isinstance(g, int) and g == 0


def gates(nc, sems, g_xattn, g_ffn, glob):
    with Stage(nc, sems, "g") as st:
        raw = st.sb("raw", [128, 4])
        g_in, g_done, const_set = st.sem("in"), st.sem("done"), st.sem("const_set")
        block = st.stack.enter_context(nc.Block())

        @block.vector
        def _(v):
            v.memset(glob[:, ONE:ONE + 1], 1.0).then_inc(const_set, 1)
            v.memset(glob[:, RND:RND + 1], ROUND).then_inc(const_set, 1)
            v.wait_ge(const_set, 2)

        @block.sync
        def _(sp):
            sp.dma_start(raw[:, 0:2], g_xattn.partition_broadcast(128)).then_inc(g_in, 16)
            sp.dma_start(raw[:, 2:4], g_ffn.partition_broadcast(128)).then_inc(g_in, 16)

        @block.scalar
        def _(a):
            a.wait_ge(g_in, 32)
            a.activation(glob[:, 0:4], raw[:], ACT.Tanh).then_inc(g_done, 1)
            a.wait_ge(g_done, 1)


def project_out(nc, sems, src, w_d, ident_d, glob, x, x_out, xn_out):
    with Stage(nc, sems, "o0") as st:
        ident = st.sb("ident", [128, 128])
        w_raw = st.sb("w_raw", [128, DC, D])
        w = [st.sb("w_hi", [128, DC, D], F32R), st.sb("w_lo", [128, DC, D], F32R)]
        at = [st.sb(f"a{k}", [128, 4, D]) for k in range(2)]
        xt = [st.sb(f"x{k}", [128, 4, D]) for k in range(2)]
        xo = [st.sb(f"xo{k}", [128, 4, D]) for k in range(2)]
        xn = [st.sb(f"xn{k}", [128, 4, D]) for k in range(2)]
        peak = st.sb("peak", [128, 1 + G5 * 4])
        out = st.ps("out", (128, 4, 512))
        a_in = [st.sem(f"a_in{k}") for k in range(2)]
        x_in = [st.sem(f"x_in{k}") for k in range(2)]
        stored = [st.sem(f"stored{k}") for k in range(2)]
        ident_in, w_in, w_split, mm_done = st.sem("ident_in"), st.sem("w_in"), st.sem("w_split"), st.sem("mm_done")
        a_ready, xo_ready, xn_ready, peaks, top = st.sem("a_ready"), st.sem("xo_ready"), st.sem("xn_ready"), st.sem("peaks"), st.sem("top")
        norm, turn = Norm(st, 128), Turn(st, 128, DC, None)
        block = st.stack.enter_context(nc.Block())

        def tiles(t, g):
            return t[bass.ds(g * 512, 512), :].rearrange("(j p) c -> p j c", p=128)

        @block.sync
        def _(sp):
            def load(g, k, u):
                if not (isinstance(g, int) and g < 2):
                    sp.wait_ge(turn.turned, 4 * g - 4)
                sp.dma_start(at[k][:], tiles(src, g)).then_inc(a_in[k], 16)
                if not (isinstance(g, int) and g < 2):
                    sp.wait_ge(xo_ready, 4 * g - 4)
                sp.dma_start(xt[k][:], tiles(x, g)).then_inc(x_in[k], 16)

            def store(g, k, u):
                sp.wait_ge(xo_ready, 4 * g + 4)
                sp.dma_start(tiles(x_out, g), xo[k][:]).then_inc(stored[k], 16)
                sp.wait_ge(xn_ready, 4 * g + 4)
                sp.dma_start(tiles(xn_out, g), xn[k][:]).then_inc(stored[k], 16)

            def step(g, k, u):
                store(g, k, u)
                load(g + 2, k, u + 1)
            load(0, 0, 0)
            sp.dma_start(ident[:], ident_d).then_inc(ident_in, 16)
            load_weight(sp, w_raw, w_d, w_in)
            load(1, 1, 0)
            sp.sem_inc(stored[0], 32)
            sp.sem_inc(stored[1], 32)
            pairs(sp, 0, G5 - 2, step)
            store(G5 - 2, 1, 2)
            store(G5 - 1, 0, 3)
            sp.wait_ge(stored[0], 32 + 32 * 4)
            sp.wait_ge(stored[1], 32 + 32 * 3)

        @block.scalar
        def _(a):
            def step(g, k, u, more=True):
                if more:
                    turn.scalar(a, g + 1, 1 - k, None if is_first(g) else (mm_done, 4 * g))
                norm.scalar(a, g)
            turn.scalar(a, 0, 0)
            step(0, 0, 0)
            pairs(a, 1, G5 - 1, step)
            step(G5 - 1, 0, 3, False)

        @block.vector
        def _(v):
            def step(g, k, u, more=True):
                if more:
                    turn.vector(v, g + 1, 1 - k)
                v.wait_ge(x_in[k], 16 * u + 16)
                v.wait_ge(stored[k], 32 * u + 32)
                for j in range(4):
                    v.wait_ge(mm_done, 4 * g + j + 1)
                    v.scalar_tensor_tensor(xo[k][:, j, :], out[:, j, :], glob[:, 0:1], xt[k][:, j, :], ALU.mult, ALU.add).then_inc(xo_ready, 1)
                v.wait_ge(xo_ready, 4 * g + 4)
                norm.vector(v, g, xo[k], xn[k], xn_ready)
                v.wait_ge(xn_ready, 4 * g + 4)
                v.tensor_reduce(peak[:, bass.ds(g, 1)], xn[k][:], AX.XY, ALU.max, apply_absolute_value=True).then_inc(peaks, 1)
            turn.vector(v, 0, 0)
            v.wait_ge(w_in, 16)
            split_weights(v, w_raw[:], w[0][:], w[1][:], w_split, 0)
            step(0, 0, 0)
            pairs(v, 1, G5 - 1, step)
            step(G5 - 1, 0, 3, False)
            v.wait_ge(peaks, G5)
            v.tensor_reduce(glob[:, 4:5], peak[:, 0:G5], AX.X, ALU.max).then_inc(top, 1)
            v.wait_ge(top, 1)

        @block.tensor
        def _(t):
            def step(g, k, u, more=True):
                x2 = (turn.hi[k], turn.lo[k])
                for j in range(4):
                    if j == 0:
                        t.wait_ge(turn.lo_ready, 4 * g + 4)
                    if not is_first(g):
                        t.wait_ge(xo_ready, 4 * g - 3 + j)
                    for n, (px, pw) in enumerate(PASSES):
                        for d in range(DC):
                            mm = t.matmul(out[:, j, :], x2[px][:, d, j * 128:(j + 1) * 128], w[pw][:, d, :],
                                          start=(n == 0 and d == 0), stop=(n == 2 and d == DC - 1))
                    mm.then_inc(mm_done, 1)
                    if j == 0 and more:
                        t.wait_ge(a_in[1 - k], 16 * (u + k) + 16)
                        turn.tensor(t, g + 1, at[1 - k], ident)
            t.wait_ge(ident_in, 16)
            t.wait_ge(a_in[0], 16)
            turn.tensor(t, 0, at[0], ident)
            t.wait_ge(w_split, 2)
            step(0, 0, 0)
            pairs(t, 1, G5 - 1, step)
            step(G5 - 1, 0, 3, False)



(GX0, GX1, GF0, GF1, PEAK_X, SX, FX, PEAK_G, PEAK_U, SG, FG, SU, FU, PEAK_T, S2, F2, PEAK_V, SO, FO, GSO, SG16, ONE, RND) = range(23)
NGLOB = 24
WBLK = 32
QUADS = I0 // 512
UNITS = G5 * QUADS


def scales(nc, sems, glob, name, jobs):
    with Stage(nc, sems, name) as st:
        top = st.sb("top", [128, len(jobs)])
        unit, raw, rec = (st.sb(n, [128, len(jobs)]) for n in ("unit", "raw", "rec"))
        reduced, step = st.sem("reduced"), st.sem("step")
        block = st.stack.enter_context(nc.Block())

        @block.gpsimd
        def _(pool):
            for i, job in enumerate(jobs):
                pool.partition_all_reduce(top[:, i:i + 1], glob[:, job[0]:job[0] + 1], 128, bass.bass_isa.ReduceOp.max).then_inc(reduced, 1)

        @block.vector
        def _(v):
            n = 0
            for i, (_, a, b, const, s, f) in enumerate(jobs):
                def col(c):
                    return glob[:, c:c + 1]
                v.tensor_scalar(unit[:, i:i + 1], col(a), col(b), const, ALU.mult, ALU.mult).then_inc(step, 1)
                v.wait_ge(step, n + 1)
                v.wait_ge(reduced, i + 1)
                v.tensor_scalar(raw[:, i:i + 1], top[:, i:i + 1], unit[:, i:i + 1], 1.0 / QMAX, ALU.mult, ALU.mult).then_inc(step, 1)
                v.wait_ge(step, n + 2)
                v.tensor_scalar(col(s), raw[:, i:i + 1], 1e-12, None, ALU.max).then_inc(step, 1)
                v.wait_ge(step, n + 3)
                v.reciprocal(rec[:, i:i + 1], col(s)).then_inc(step, 1)
                v.wait_ge(step, n + 4)
                v.tensor_tensor(col(f), rec[:, i:i + 1], unit[:, i:i + 1], ALU.mult).then_inc(step, 1)
                v.wait_ge(step, n + 5)
                n += 5


def quantise_weight(nc, sems, name, tiles, ident_d, w_parts):
    with Stage(nc, sems, name) as st:
        ident = st.sb("ident", [128, 128])
        wt = [st.sb(f"w{k}", [128, 4, 512]) for k in range(2)]
        top, s, rec = (st.sb(n, [128, 4 * 512 // WBLK]) for n in ("top", "s", "rec"))
        ident_in, q_step, deq = st.sem("ident_in"), st.sem("q_step"), st.sem("deq")
        w_in = [st.sem(f"w_in{k}") for k in range(2)]
        w_out = st.sem("w_out")
        turn = Turn(st, 128, 4, deq, 1)
        block = st.stack.enter_context(nc.Block())

        @block.sync
        def _(sp):
            sp.dma_start(wt[0][:], tiles[0]).then_inc(w_in[0], 16)
            sp.dma_start(ident[:], ident_d).then_inc(ident_in, 16)
            sp.dma_start(wt[1][:], tiles[1]).then_inc(w_in[1], 16)
            for g in range(3):
                if g == 1:
                    sp.wait_ge(turn.turned, 4)
                    sp.dma_start(wt[0][:], tiles[2]).then_inc(w_in[0], 16)
                sp.wait_ge(turn.hi_ready, 4 * g + 4)
                sp.dma_start(w_parts[0][g], turn.hi[g % 2][:].bitcast(F32)).then_inc(w_out, 16)
                sp.wait_ge(turn.lo_ready, 4 * g + 4)
                sp.dma_start(w_parts[1][g], turn.lo[g % 2][:].bitcast(F32)).then_inc(w_out, 16)
            sp.wait_ge(w_out, 96)

        @block.vector
        def _(v):
            for g in range(3):
                w, at = wt[g % 2], 6 * g
                blocks = w[:].rearrange("p j (n e) -> p (j n) e", e=WBLK)

                def spread(x):
                    return x[:].unsqueeze(2).broadcast_to([128, 4 * 512 // WBLK, WBLK])
                v.wait_ge(w_in[g % 2], 16 * (g // 2) + 16)
                v.tensor_reduce(top[:], blocks, AX.X, ALU.max, apply_absolute_value=True).then_inc(q_step, 1)
                v.wait_ge(q_step, at + 1)
                v.tensor_scalar(s[:], top[:], 1.0 / 7.0, 1e-12, ALU.mult, ALU.max).then_inc(q_step, 1)
                v.wait_ge(q_step, at + 2)
                v.reciprocal(rec[:], s[:]).then_inc(q_step, 1)
                v.wait_ge(q_step, at + 3)
                v.tensor_tensor(blocks, blocks, spread(rec), ALU.mult).then_inc(q_step, 1)
                v.wait_ge(q_step, at + 4)
                v.tensor_scalar(w[:], w[:], ROUND, None, ALU.add).then_inc(q_step, 1)
                v.wait_ge(q_step, at + 5)
                v.tensor_scalar(w[:], w[:], ROUND, None, ALU.subtract).then_inc(q_step, 1)
                v.wait_ge(q_step, at + 6)
                v.tensor_tensor(blocks, blocks, spread(s), ALU.mult).then_inc(deq, 1)
                turn.vector(v, g, g % 2)

        @block.tensor
        def _(t):
            t.wait_ge(ident_in, 16)
            for g in range(3):
                turn.tensor(t, g, wt[g % 2], ident)

        @block.scalar
        def _(a):
            for g in range(3):
                turn.scalar(a, g, g % 2, (w_out, 32) if g == 2 else None)


def up_gate(nc, sems, xn, gate_w, up_w, ident_d, glob, gate_d, up_d):
    with Stage(nc, sems, "ug") as st:
        ident = st.sb("ident", [128, 128])
        w = [[st.sb(f"w{s}{p}", [128, DC, I0], F32R) for p in range(2)] for s in range(2)]
        xt = [st.sb(f"x{k}", [128, 4, D]) for k in range(2)]
        h = [st.sb(f"h{k}", [128, 4, 512]) for k in range(2)]
        now, best = st.sb("now", [128, 2 * QUADS]), st.sb("best", [128, 2 * QUADS])
        out = st.ps("out", (128, 4, 512))
        x_in = [st.sem(f"x_in{k}") for k in range(2)]
        stored = [st.sem(f"stored{k}") for k in range(2)]
        ident_in, w_in, r_ready, xq_ready = st.sem("ident_in"), st.sem("w_in"), st.sem("r_ready"), st.sem("xq_ready")
        mm_done, copied, peaked, topped = st.sem("mm_done"), st.sem("copied"), st.sem("peaked"), st.sem("topped")
        turn = Turn(st, 128, DC, xq_ready, 1)
        CHUNKS, Q2 = 8 * QUADS, 2 * QUADS
        block = st.stack.enter_context(nc.Block())

        @block.sync
        def _(sp):
            def load(g, k, u):
                if not (isinstance(g, int) and g < 2):
                    sp.wait_ge(turn.turned, 4 * g - 4)
                sp.dma_start(xt[k][:], xn[bass.ds(g * 512, 512), :].rearrange("(j p) c -> p j c", p=128)).then_inc(x_in[k], 16)

            def store(g, k, u):
                for q in range(Q2):
                    dst = (gate_d, up_d)[q // QUADS]
                    sp.wait_ge(copied, CHUNKS * g + 4 * q + 4)
                    sp.dma_start(dst[bass.ds(QUADS * g + q % QUADS, 1), :, :].rearrange("a p n -> (a p) n"),
                                 h[q % 2][:].rearrange("p j n -> p (j n)")).then_inc(stored[q % 2], 16)

            def step(g, k, u):
                load(g + 2, k, u + 1)
                store(g, k, u)
            load(0, 0, 0)
            sp.dma_start(ident[:], ident_d).then_inc(ident_in, 16)
            for s, parts in enumerate((gate_w, up_w)):
                for p in range(2):
                    sp.dma_start(w[s][p][:].bitcast(F32), parts[p].rearrange("(c p) n -> p c n", p=128)).then_inc(w_in, 16)
            load(1, 1, 0)
            sp.sem_inc(stored[0], 16)
            sp.sem_inc(stored[1], 16)
            pairs(sp, 0, G5 - 2, step)
            store(G5 - 2, 1, 2)
            store(G5 - 1, 0, 3)
            for k in range(2):
                sp.wait_ge(stored[k], 16 + 16 * QUADS * G5)

        @block.scalar
        def _(a):
            def step(g, k, u, more=True):
                for c in range(CHUNKS):
                    if c == 10 and more:
                        turn.scalar(a, g + 1, 1 - k, None if is_first(g) else (mm_done, CHUNKS * g))
                    if c % 4 == 0:
                        q = c // 4
                        a.wait_ge(stored[q % 2], 16 * QUADS * g + 16 * (q // 2) + 16)
                        a.wait_ge(peaked, Q2 * g + q + 1)
                    a.wait_ge(mm_done, CHUNKS * g + c + 1)
                    a.activation(h[(c // 4) % 2][:, c % 4, :], out[:, c % 4, :], ACT.Copy).then_inc(copied, 1)
            turn.scalar(a, 0, 0)
            step(0, 0, 0)
            pairs(a, 1, G5 - 1, step)
            step(G5 - 1, 0, 3, False)

        @block.vector
        def _(v):
            def front(g, k, u):
                v.wait_ge(x_in[k], 16 * u + 16)
                v.tensor_scalar(xt[k][:], xt[k][:], glob[:, FX:FX + 1], ROUND, ALU.mult, ALU.add).then_inc(r_ready, 1)
                v.wait_ge(r_ready, g + 1)
                v.tensor_scalar(xt[k][:], xt[k][:], ROUND, None, ALU.subtract).then_inc(xq_ready, 1)

            def step(g, k, u, more=True):
                if more:
                    front(g + 1, 1 - k, u + k)
                v.wait_ge(topped, g + 1)
                for q in range(Q2):
                    if q == 2 and more:
                        turn.vector(v, g + 1, 1 - k)
                    v.wait_ge(copied, CHUNKS * g + 4 * q + 4)
                    v.tensor_reduce(now[:, q:q + 1], h[q % 2][:], AX.XY, ALU.max, apply_absolute_value=True).then_inc(peaked, 1)
                v.wait_ge(peaked, Q2 * (g + 1) + 2)
                v.tensor_tensor(best[:], best[:], now[:], ALU.max).then_inc(topped, 1)
            v.memset(best[:], 0.0).then_inc(topped, 1)
            v.sem_inc(peaked, 2)
            front(0, 0, 0)
            turn.vector(v, 0, 0)
            step(0, 0, 0)
            pairs(v, 1, G5 - 1, step)
            step(G5 - 1, 0, 3, False)
            v.wait_ge(topped, G5 + 1)
            for s, c in enumerate((PEAK_G, PEAK_U)):
                v.tensor_reduce(glob[:, c:c + 1], best[:, s * QUADS:(s + 1) * QUADS], AX.X, ALU.max).then_inc(topped, 1)
            v.wait_ge(topped, G5 + 3)

        @block.tensor
        def _(t):
            def step(g, k, u, more=True):
                x2 = (turn.hi[k], turn.lo[k])
                for c in range(CHUNKS):
                    if c == 10 and more:
                        turn.tensor(t, g + 1, xt[1 - k], ident)
                    if c == 0:
                        t.wait_ge(turn.lo_ready, 4 * g + 4)
                    if not (is_first(g) and c < 4):
                        t.wait_ge(copied, CHUNKS * g + c - 3)
                    s, f = divmod(c, 4 * QUADS)
                    for n, (pw, px) in enumerate(PASSES):
                        for d in range(DC):
                            mm = t.matmul(out[:, c % 4, :], w[s][pw][:, d, f * 128:(f + 1) * 128], x2[px][:, d, :],
                                          start=(n == 0 and d == 0), stop=(n == 2 and d == DC - 1))
                    mm.then_inc(mm_done, 1)
            t.wait_ge(ident_in, 16)
            turn.tensor(t, 0, xt[0], ident)
            t.wait_ge(w_in, 64)
            step(0, 0, 0)
            pairs(t, 1, G5 - 1, step)
            step(G5 - 1, 0, 3, False)


def unit_view(t, n):
    return t[bass.ds(n, 1), :, :].rearrange("a p n -> (a p) n")


def gate_sigmoid(nc, sems, gate_d, t_d, glob):
    N = 2048
    with Stage(nc, sems, "gs") as st:
        gt = [st.sb(f"g{k}", [128, N]) for k in range(2)]
        gq = [st.sb(f"gq{k}", [128, N]) for k in range(2)]
        sg = [st.sb(f"s{k}", [128, N]) for k in range(2)]
        sq = [st.sb(f"sq{k}", [128, N]) for k in range(2)]
        tt = [st.sb(f"t{k}", [128, N]) for k in range(2)]
        now, best = st.sb("now", [128, 1]), st.sb("best", [128, 1])
        g_in = [st.sem(f"g_in{k}") for k in range(2)]
        stored = [st.sem(f"stored{k}") for k in range(2)]
        r_ready, gq_ready, sig_ready, sr_ready, sq_ready = (st.sem(n) for n in ("r_ready", "gq_ready", "sig_ready", "sr_ready", "sq_ready"))
        t_ready, peaked, topped = st.sem("t_ready"), st.sem("peaked"), st.sem("topped")
        block = st.stack.enter_context(nc.Block())

        @block.sync
        def _(sp):
            def load(n, k, u):
                if not (isinstance(n, int) and n < 2):
                    sp.wait_ge(gq_ready, n - 1)
                sp.dma_start(gt[k][:], unit_view(gate_d, n)).then_inc(g_in[k], 16)

            def store(n, k, u):
                sp.wait_ge(t_ready, n + 3)
                sp.dma_start(unit_view(t_d, n), tt[k][:]).then_inc(stored[k], 16)

            def step(n, k, u):
                load(n + 2, k, u + 1)
                store(n, k, u)
            sp.sem_inc(stored[0], 16)
            sp.sem_inc(stored[1], 16)
            load(0, 0, 0)
            load(1, 1, 0)
            pairs(sp, 0, UNITS - 2, step)
            store(UNITS - 2, 1, 0)
            store(UNITS - 1, 0, 0)
            sp.wait_ge(stored[0], 16 + 16 * (UNITS // 2 + 1))
            sp.wait_ge(stored[1], 16 + 16 * (UNITS // 2))

        @block.scalar
        def _(a):
            def first(n, k, u):
                a.wait_ge(g_in[k], 16 * u + 16)
                a.activation(gt[k][:], gt[k][:], ACT.Identity, bias=glob[:, RND:RND + 1], scale=glob[:, FG:FG + 1]).then_inc(r_ready, 1)

            def step(n, k, u, more=True):
                if more:
                    first(n + 1, 1 - k, u + k)
                a.wait_ge(gq_ready, n + 1)
                a.wait_ge(sq_ready, n + 1)
                a.activation(sg[k][:], gq[k][:], ACT.Sigmoid, scale=glob[:, SG:SG + 1]).then_inc(sig_ready, 1)
                a.wait_ge(sig_ready, n + 1)
                a.activation(sg[k][:], sg[k][:], ACT.Identity, bias=glob[:, RND:RND + 1], scale=65536.0).then_inc(sr_ready, 1)
            a.sem_inc(sq_ready, 2)
            first(0, 0, 0)
            step(0, 0, 0)
            pairs(a, 1, UNITS - 1, step)
            step(UNITS - 1, 0, 0, False)

        @block.vector
        def _(v):
            def first(n, k, u):
                v.wait_ge(r_ready, n + 1)
                v.wait_ge(t_ready, n + 1)
                v.tensor_scalar(gq[k][:], gt[k][:], ROUND, None, ALU.subtract).then_inc(gq_ready, 1)

            def peak(n, k):
                v.wait_ge(t_ready, n + 3)
                v.wait_ge(topped, n + 1)
                v.tensor_reduce(now[:], tt[k][:], AX.X, ALU.max, apply_absolute_value=True).then_inc(peaked, 1)
                v.wait_ge(peaked, n + 1)
                v.tensor_tensor(best[:], best[:], now[:], ALU.max).then_inc(topped, 1)

            def step(n, k, u, more=True):
                if more:
                    first(n + 1, 1 - k, u + k)
                v.wait_ge(sr_ready, n + 1)
                v.tensor_scalar(sq[k][:], sg[k][:], ROUND, 65535.0, ALU.subtract, ALU.min).then_inc(sq_ready, 1)
                v.wait_ge(stored[k], 16 * u + 16)
                v.wait_ge(sq_ready, n + 3)
                v.tensor_tensor(tt[k][:], gq[k][:], sq[k][:], ALU.mult).then_inc(t_ready, 1)
                peak(n, k)
            v.sem_inc(t_ready, 2)
            v.memset(best[:], 0.0).then_inc(topped, 1)
            first(0, 0, 0)
            step(0, 0, 0)
            pairs(v, 1, UNITS - 1, step)
            step(UNITS - 1, 0, UNITS // 2, False)
            v.wait_ge(topped, UNITS + 1)
            v.tensor_copy(glob[:, PEAK_T:PEAK_T + 1], best[:]).then_inc(peaked, 1)
            v.wait_ge(peaked, UNITS + 1)


def gate_times_up(nc, sems, t_d, up_d, v_d, glob):
    N = 2048
    with Stage(nc, sems, "gu") as st:
        tt = [st.sb(f"t{k}", [128, N]) for k in range(2)]
        ut = [st.sb(f"u{k}", [128, N]) for k in range(2)]
        uq = [st.sb(f"uq{k}", [128, N]) for k in range(2)]
        vt = [st.sb(f"v{k}", [128, N]) for k in range(2)]
        now, best = st.sb("now", [128, 1]), st.sb("best", [128, 1])
        t_in = [st.sem(f"t_in{k}") for k in range(2)]
        stored = [st.sem(f"stored{k}") for k in range(2)]
        r_ready, uq_ready, v_ready, peaked, topped = (st.sem(n) for n in ("r_ready", "uq_ready", "v_ready", "peaked", "topped"))
        block = st.stack.enter_context(nc.Block())

        @block.sync
        def _(sp):
            def load(n, k, u):
                if not (isinstance(n, int) and n < 2):
                    sp.wait_ge(v_ready, n - 1)
                sp.dma_start(ut[k][:], unit_view(up_d, n)).then_inc(t_in[k], 16)
                sp.dma_start(tt[k][:], unit_view(t_d, n)).then_inc(t_in[k], 16)

            def store(n, k, u):
                sp.wait_ge(v_ready, n + 1)
                sp.dma_start(unit_view(v_d, n), vt[k][:]).then_inc(stored[k], 16)

            def step(n, k, u):
                load(n + 2, k, u + 1)
                store(n, k, u)
            sp.sem_inc(stored[0], 16)
            sp.sem_inc(stored[1], 16)
            load(0, 0, 0)
            load(1, 1, 0)
            pairs(sp, 0, UNITS - 2, step)
            store(UNITS - 2, 1, 0)
            store(UNITS - 1, 0, 0)
            sp.wait_ge(stored[0], 16 + 16 * (UNITS // 2 + 1))
            sp.wait_ge(stored[1], 16 + 16 * (UNITS // 2))

        @block.scalar
        def _(a):
            def step(n, k, u):
                a.wait_ge(t_in[k], 32 * u + 32)
                a.activation(ut[k][:], ut[k][:], ACT.Identity, bias=glob[:, RND:RND + 1], scale=glob[:, FU:FU + 1]).then_inc(r_ready, 1)
                a.activation(tt[k][:], tt[k][:], ACT.Identity, bias=glob[:, RND:RND + 1], scale=glob[:, F2:F2 + 1]).then_inc(r_ready, 1)
            pairs(a, 0, UNITS, step)

        @block.vector
        def _(v):
            def step(n, k, u):
                v.wait_ge(r_ready, 2 * n + 2)
                v.tensor_scalar(uq[k][:], ut[k][:], ROUND, None, ALU.subtract).then_inc(uq_ready, 1)
                v.wait_ge(stored[k], 16 * u + 16)
                v.wait_ge(uq_ready, n + 1)
                v.scalar_tensor_tensor(vt[k][:], tt[k][:], -ROUND, uq[k][:], ALU.add, ALU.mult).then_inc(v_ready, 1)
                v.wait_ge(v_ready, n + 1)
                v.wait_ge(topped, n + 1)
                v.tensor_reduce(now[:], vt[k][:], AX.X, ALU.max, apply_absolute_value=True).then_inc(peaked, 1)
                v.wait_ge(peaked, n + 1)
                v.tensor_tensor(best[:], best[:], now[:], ALU.max).then_inc(topped, 1)
            v.memset(best[:], 0.0).then_inc(topped, 1)
            pairs(v, 0, UNITS, step)
            v.wait_ge(topped, UNITS + 1)
            v.tensor_copy(glob[:, PEAK_V:PEAK_V + 1], best[:]).then_inc(peaked, 1)
            v.wait_ge(peaked, UNITS + 1)


def down(nc, sems, v_d, w_parts, glob, x, x_out, xn_out):
    N = 2048
    with Stage(nc, sems, "dn") as st:
        w = [st.sb(f"w{p}", [128, 4 * QUADS, D], F32R) for p in range(2)]
        vt = [st.sb(f"v{k}", [128, N]) for k in range(2)]
        hi = [st.sb(f"hi{k}", [128, N], F32R) for k in range(2)]
        lo = [st.sb(f"lo{k}", [128, N], F32R) for k in range(2)]
        xt = [st.sb(f"x{k}", [128, 4, D]) for k in range(2)]
        xo = [st.sb(f"xo{k}", [128, 4, D]) for k in range(2)]
        xn = [st.sb(f"xn{k}", [128, 4, D]) for k in range(2)]
        out = [st.ps(f"out{k}", (128, 4, 512)) for k in range(2)]
        v_in = [st.sem(f"v_in{k}") for k in range(2)]
        x_in = [st.sem(f"x_in{k}") for k in range(2)]
        stored = [st.sem(f"stored{k}") for k in range(2)]
        w_in, r_ready, hi_ready, lo_ready, mm_done = (st.sem(n) for n in ("w_in", "r_ready", "hi_ready", "lo_ready", "mm_done"))
        xo_ready, xn_ready, scale_set = st.sem("xo_ready"), st.sem("xn_ready"), st.sem("scale_set")
        norm = Norm(st, 128)
        block = st.stack.enter_context(nc.Block())

        def tiles(t, g):
            return t[bass.ds(g * 512, 512), :].rearrange("(j p) c -> p j c", p=128)

        def units(g, k, u, body):
            for q in range(QUADS):
                body(QUADS * g + q, (k + q) % 2, QUADS * u + (QUADS * k + q) // 2)

        @block.sync
        def _(sp):
            def load(g, k, u):
                def one(n, s, used):
                    if not (isinstance(n, int) and n < 2):
                        sp.wait_ge(lo_ready, n - 1)
                    sp.dma_start(vt[s][:], unit_view(v_d, n)).then_inc(v_in[s], 16)
                units(g, k, u, one)
                if not (isinstance(g, int) and g < 2):
                    sp.wait_ge(xo_ready, 4 * g - 4)
                sp.dma_start(xt[k][:], tiles(x, g)).then_inc(x_in[k], 16)

            def store(g, k, u):
                sp.wait_ge(xo_ready, 4 * g + 4)
                sp.dma_start(tiles(x_out, g), xo[k][:]).then_inc(stored[k], 16)
                sp.wait_ge(xn_ready, 4 * g + 4)
                sp.dma_start(tiles(xn_out, g), xn[k][:]).then_inc(stored[k], 16)

            def step(g, k, u):
                load(g + 1, 1 - k, u + k)
                store(g, k, u)
            for p in range(2):
                sp.dma_start(w[p][:].bitcast(F32), w_parts[p].rearrange("(c p) n -> p c n", p=128)).then_inc(w_in, 16)
            load(0, 0, 0)
            sp.sem_inc(stored[0], 32)
            sp.sem_inc(stored[1], 32)
            pairs(sp, 0, G5 - 1, step)
            store(G5 - 1, 0, 3)
            sp.wait_ge(stored[0], 32 + 32 * 4)
            sp.wait_ge(stored[1], 32 + 32 * 3)

        @block.scalar
        def _(a):
            def one(n, s, used):
                a.wait_ge(v_in[s], 16 * used + 16)
                a.activation(vt[s][:], vt[s][:], ACT.Identity, bias=glob[:, RND:RND + 1], scale=glob[:, FO:FO + 1]).then_inc(r_ready, 1)

            def step(g, k, u, more=True):
                if more:
                    units(g + 1, 1 - k, u + k, one)
                norm.scalar(a, g)
            units(0, 0, 0, one)
            step(0, 0, 0)
            pairs(a, 1, G5 - 1, step)
            step(G5 - 1, 0, 3, False)

        @block.vector
        def _(v):
            def one(n, s, used):
                v.wait_ge(r_ready, n + 1)
                v.wait_ge(mm_done, n + 1)
                v.tensor_scalar(hi[s][:], vt[s][:], ROUND, None, ALU.subtract).then_inc(hi_ready, 1)
                v.wait_ge(hi_ready, n + 1)
                v.scalar_tensor_tensor(lo[s][:], vt[s][:], -ROUND, hi[s][:].bitcast(F32), ALU.add, ALU.subtract).then_inc(lo_ready, 1)

            def step(g, k, u, more=True):
                if more:
                    units(g + 1, 1 - k, u + k, one)
                v.wait_ge(mm_done, QUADS * (g + 1) + 2)
                v.wait_ge(x_in[k], 16 * u + 16)
                v.wait_ge(stored[k], 32 * u + 32)
                for j in range(4):
                    v.scalar_tensor_tensor(xo[k][:, j, :], out[k][:, j, :], glob[:, GSO:GSO + 1], xt[k][:, j, :], ALU.mult, ALU.add).then_inc(xo_ready, 1)
                v.wait_ge(xo_ready, 4 * g + 4)
                norm.vector(v, g, xo[k], xn[k], xn_ready)
            v.sem_inc(mm_done, 2)
            v.tensor_tensor(glob[:, GSO:GSO + 1], glob[:, GF0:GF0 + 1], glob[:, SO:SO + 1], ALU.mult).then_inc(scale_set, 1)
            v.wait_ge(scale_set, 1)
            units(0, 0, 0, one)
            step(0, 0, 0)
            pairs(v, 1, G5 - 1, step)
            step(G5 - 1, 0, 3, False)

        @block.tensor
        def _(t):
            def step(g, k, u):
                if not (isinstance(g, int) and g < 2):
                    t.wait_ge(xo_ready, 4 * g - 4)
                q = iter(range(QUADS))

                def one(n, s, used):
                    quad = next(q)
                    t.wait_ge(lo_ready, n + 1)
                    for j in range(4):
                        for m, (px, pw) in enumerate(PASSES):
                            for c in range(4):
                                at = c * 512 + j * 128
                                mm = t.matmul(out[k][:, j, :], (hi, lo)[px][s][:, at:at + 128], w[pw][:, 4 * quad + c, :],
                                              start=(quad == 0 and m == 0 and c == 0), stop=(quad == QUADS - 1 and m == 2 and c == 3))
                    mm.then_inc(mm_done, 1)
                units(g, k, u, one)
            t.wait_ge(w_in, 32)
            step(0, 0, 0)
            step(1, 1, 0)
            pairs(t, 2, G5, step)


def ffn0(nc, sems, xn, w_gate, w_up, w_down, w_parts, ident_d, glob, gate_d, up_d, t_d, v_d, x, x_out, xn_out):
    gate_t, up_t, down_t = w_parts
    for name, w, parts in (("wg", w_gate, gate_t), ("wu", w_up, up_t)):
        quantise_weight(nc, sems, name, [w[g * 512:(g + 1) * 512, :].rearrange("(j p) c -> p j c", p=128) for g in range(QUADS)], ident_d,
                        [[t[:, g * 512:(g + 1) * 512].rearrange("(d p) c -> p d c", p=128) for g in range(QUADS)] for t in parts])
    quantise_weight(nc, sems, "wd", [w_down[:, g * 512:(g + 1) * 512].rearrange("(j p) c -> p j c", p=128) for g in range(QUADS)], ident_d,
                    [[t[g * 512:(g + 1) * 512, :].rearrange("(d p) c -> p d c", p=128) for g in range(QUADS)] for t in down_t])
    scales(nc, sems, glob, "sc_x", [(PEAK_X, ONE, ONE, 1.0, SX, FX)])
    up_gate(nc, sems, xn, gate_t, up_t, ident_d, glob, gate_d, up_d)
    scales(nc, sems, glob, "sc_gu", [(PEAK_G, SX, ONE, 1.0, SG, FG), (PEAK_U, SX, ONE, 1.0, SU, FU)])
    gate_sigmoid(nc, sems, gate_d, t_d, glob)
    scales(nc, sems, glob, "sc_t", [(PEAK_T, SG, ONE, 1.0 / 65536.0, S2, F2)])
    gate_times_up(nc, sems, t_d, up_d, v_d, glob)
    scales(nc, sems, glob, "sc_v", [(PEAK_V, S2, SU, 1.0, SO, FO)])
    down(nc, sems, v_d, down_t, glob, x, x_out, xn_out)



def after(eng, sem, value):
    if not (isinstance(value, int) and value <= 0):
        eng.wait_ge(sem, value)


def attend1(nc, sems, xn, ctx, ctx_t, wq, bq, wk, bk, wv_t, bv, ident_d, glob, x, x_out, xn_out):
    NG, W, Q = B // 2, 2 * S, S // 2
    with Stage(nc, sems, "a1") as st:
        ident = st.sb("ident", [128, 128])
        bq_sb, bk_sb = st.sb("bq", [128, DC]), st.sb("bk", [128, DC])
        wv_raw, gbv = st.sb("wv_raw", [128, CC, D]), st.sb("gbv", [Q, D])
        wv2 = [st.sb(f"wv{p}", [128, CC, D], F32R) for p in range(2)]
        a2 = [st.sb(f"a{p}", [128, DC, C], F32R) for p in range(2)]
        cb, wcq, bb = st.sb("cb", [128, CC]), st.sb("wcq", [128, DC], F32R), st.sb("bb", [1, 1])
        ones = st.sb("ones", [1, NH], F32R)
        ones_col = st.sb("ones_col", [128, 2], F32R)
        xt = st.sb("xt", [Q, 4, D])
        x2 = [st.sb(f"xT{p}", [128, DC, W], F32R) for p in range(2)]
        q2 = [st.sb(f"q{p}", [128, CC, W], F32R) for p in range(2)]
        cq = st.sb("cq", [1, W], F32R)
        ct_raw, cn_raw = st.sb("ct_raw", [128, CC, M]), st.sb("cn_raw", [128, KC, C])
        ct2 = [[st.sb(f"ct{k}{p}", [128, CC, M], F32R) for p in range(2)] for k in range(2)]
        cn2 = [[st.sb(f"cn{k}{p}", [KP, KC, C], F32R) for p in range(2)] for k in range(2)]
        wq_sb = ct_raw[:].rearrange("p c m -> p (c m)")[:, 0:DC * D].rearrange("p (c n) -> p c n", n=D)
        wk_sb = cn_raw[:].rearrange("p c m -> p (c m)")[:, 0:DC * C].rearrange("p (c n) -> p c n", n=C)
        neg_max, row = st.sb("neg_max", [Q, 2]), st.sb("row", [1, S], F32R)
        p32 = st.sb("p32", [KP, KC * S])
        p2 = [st.sb(f"p{p}", [KP, KC * S], F32R) for p in range(2)]
        pc2 = [st.sb(f"pc{p}", [128, CC, S], F32R) for p in range(2)]
        rec, rg = st.sb("rec", [Q, 2]), st.sb("rg", [Q, 2])
        xr = [st.sb(f"xr{k}", [Q, 2, D]) for k in range(2)]
        xo = [st.sb(f"xo{k}", [Q, 2, D]) for k in range(2)]
        xno = [st.sb(f"xno{k}", [Q, 2, D]) for k in range(2)]

        turn_bank = st.ps("turn")
        sc = st.ps("sc", (128, 3, 512))
        mx = st.ps("mx", (128, 2, 512))
        pc = st.ps("pc", (128, 2, 512))

        (w_in, bias_in, wv_in, ones_set, pre_mm, pre_hi, pre_done, gbv_set, wv_split) = (st.sem(n) for n in (
            "w_in", "bias_in", "wv_in", "ones_set", "pre_mm", "pre_hi", "pre_done", "gbv_set", "wv_split"))
        x_in, ct_in, cn_in = st.sem("x_in"), st.sem("ct_in"), st.sem("cn_in")
        xr_in = [st.sem(f"xr_in{k}") for k in range(2)]
        stored = [st.sem(f"stored{k}") for k in range(2)]
        turned, q_full, mx_full, row_full, st_full, pc_full, wv_full = (st.sem(n) for n in (
            "turned", "q_full", "mx_full", "row_full", "st_full", "pc_full", "wv_full"))
        x_hi, cq_done, q_hi, ct_hi, cn_hi, exp_done, p_hi, pc_hi = (st.sem(n) for n in (
            "x_hi", "cq_done", "q_hi", "ct_hi", "cn_hi", "exp_done", "p_hi", "pc_hi"))
        x_lo, q_lo, ct_lo, cn_lo, p_lo, pc_lo = (st.sem(n) for n in ("x_lo", "q_lo", "ct_lo", "cn_lo", "p_lo", "pc_lo"))
        mx_done, row_done, sum_step, xb_done, xo_ready, xn_ready = (st.sem(n) for n in (
            "mx_done", "row_done", "sum_step", "xb_done", "xo_ready", "xn_ready"))
        norm = Norm(st, Q, 2)
        block = st.stack.enter_context(nc.Block())

        def batches(eng, step):
            with eng.Fori(0, NG - 1) as g:
                step(2 * g, 0, g, True, True)
                step(2 * g + 1, 1, g, True, True)
            step(B - 2, 0, NG - 1, True, False)
            step(B - 1, 1, NG - 1, False, False)

        def rows(t, b):
            return t[bass.ds(b * S, S), :].rearrange("(q p) c -> p q c", p=Q)

        def pre_bank(i):
            return sc[:, i, :] if i < 3 else mx[:, 0, :]

        @block.sync
        def _(sp):
            def load_x(g):
                after(sp, turned, 5 * g - 1)
                sp.dma_start(xt[:], xn[bass.ds(g * W, W), :].rearrange("(j p) c -> p j c", p=Q)).then_inc(x_in, 16)

            def load_ct(b):
                after(sp, ct_lo, b)
                sp.dma_start(ct_raw[:], ctx_t[bass.ds(b, 1), :, :].rearrange("a (c p) m -> p (a c) m", p=128)).then_inc(ct_in, 16)

            def load_cn(b):
                after(sp, cn_lo, b)
                sp.dma_start(cn_raw[:KP], ctx[bass.ds(b, 1), :, :].rearrange("a (c p) m -> p (a c) m", p=KP)).then_inc(cn_in, 16)

            def load_xr(b, k):
                after(sp, xo_ready, 2 * b - 2)
                sp.dma_start(xr[k][:], rows(x, b)).then_inc(xr_in[k], 16)

            def step(b, e, g, more, turn):
                if e == 0 and turn:
                    load_x(g + 1)
                if more:
                    load_cn(b + 1)
                if turn:
                    load_ct(b + 2)
                sp.wait_ge(xo_ready, 2 * b + 2)
                sp.dma_start(rows(x_out, b), xo[e][:]).then_inc(stored[e], 16)
                if turn:
                    load_xr(b + 2, e)
                sp.wait_ge(xn_ready, 2 * b + 2)
                sp.dma_start(rows(xn_out, b), xno[e][:]).then_inc(stored[e], 16)

            sp.dma_start(wq_sb, wq.rearrange("(c p) n -> p c n", p=128)).then_inc(w_in, 16)
            sp.dma_start(wk_sb, wk.rearrange("(c p) n -> p c n", p=128)).then_inc(w_in, 16)
            sp.dma_start(bq_sb[:], bq.rearrange("(c p) -> p c", p=128), allow_slow_non_contiguous=True).then_inc(bias_in, 16)
            sp.dma_start(bk_sb[:], bk.rearrange("(c p) -> p c", p=128), allow_slow_non_contiguous=True).then_inc(bias_in, 16)
            sp.dma_start(ident[:], ident_d).then_inc(bias_in, 16)
            sp.dma_start(xt[:], xn[0:W, :].rearrange("(j p) c -> p j c", p=Q)).then_inc(x_in, 16)
            sp.dma_start(wv_raw[:], wv_t.rearrange("(c p) n -> p c n", p=128)).then_inc(wv_in, 16)
            sp.dma_start(gbv[:], bv.partition_broadcast(Q)).then_inc(wv_in, 16)
            load_xr(0, 0)
            load_xr(1, 1)
            sp.wait_ge(pre_mm, DC + 1)
            load_ct(0)
            load_cn(0)
            load_ct(1)
            sp.sem_inc(stored[0], 32)
            sp.sem_inc(stored[1], 32)
            batches(sp, step)
            for k in range(2):
                sp.wait_ge(stored[k], 32 + 16 * B)

        @block.gpsimd
        def _(pool):
            def split_ct(b, k):
                pool.wait_ge(ct_hi, b + 1)
                pool.tensor_tensor(ct2[k][1][:], ct_raw[:], ct2[k][0][:].bitcast(F32), ALU.subtract).then_inc(ct_lo, 1)

            def split_cn(b, k):
                pool.wait_ge(cn_hi, b + 1)
                pool.tensor_tensor(cn2[k][1][:], cn_raw[:KP], cn2[k][0][:].bitcast(F32), ALU.subtract).then_inc(cn_lo, 1)

            def add_bias(b, k, used):
                pool.wait_ge(xr_in[k], 16 * used + 16)
                pool.tensor_tensor(xr[k][:], xr[k][:], gbv[:].unsqueeze(1).broadcast_to([Q, 2, D]), ALU.add).then_inc(xb_done, 1)

            def step(b, e, g, more, turn):
                if more:
                    split_cn(b + 1, 1 - e)
                if turn:
                    split_ct(b + 2, e)
                    add_bias(b + 2, e, g + 1)

            split_ct(0, 0)
            split_cn(0, 0)
            split_ct(1, 1)
            pool.wait_ge(gbv_set, 1)
            add_bias(0, 0, 0)
            add_bias(1, 1, 0)
            batches(pool, step)

        @block.scalar
        def _(a):
            def split_ct(b, k):
                after(a, st_full, 3 * b - 3)
                a.wait_ge(ct_in, 16 * b + 16)
                a.activation(ct2[k][0][:], ct_raw[:], ACT.Copy).then_inc(ct_hi, 1)

            def split_cn(b, k):
                after(a, pc_full, 2 * b - 2)
                a.wait_ge(cn_in, 16 * b + 16)
                a.activation(cn2[k][0][:], cn_raw[:KP], ACT.Copy).then_inc(cn_hi, 1)

            def turn_hi(g, d):
                if d == 0:
                    after(a, q_full, 3 * g)
                a.wait_ge(turned, 5 * g + d + 1)
                a.activation(x2[0][:, d, :], turn_bank[:, 0:W], ACT.Copy).then_inc(x_hi, 1)

            def queries(g):
                after(a, st_full, 6 * g)
                for c in range(CC):
                    a.wait_ge(q_full, 3 * g + c + 1)
                    a.activation(q2[0][:, c, :], sc[:, c, 0:W], ACT.Identity, bias=cb[:, c:c + 1]).then_inc(q_hi, 1)
                after(a, row_done, 2 * g)
                a.wait_ge(turned, 5 * g + 5)
                a.activation(cq[:], turn_bank[0:1, 0:W], ACT.Identity, bias=bb[:, 0:1]).then_inc(cq_done, 1)

            def probs(b):
                after(a, p_lo, b)
                for j in range(3):
                    a.wait_ge(st_full, 3 * b + j + 1)
                    a.activation(p32[:, j * 448:(j + 1) * 448], sc[:KP, j, 0:448], ACT.Exp, scale=D ** -0.5).then_inc(exp_done, 1)
                after(a, pc_full, 2 * b)
                a.wait_ge(exp_done, 3 * b + 3)
                a.activation(p2[0][:], p32[:], ACT.Copy).then_inc(p_hi, 1)

            def step(b, e, g, more, turn):
                if e == 1 and turn:
                    queries(g + 1)
                if e == 0 and turn:
                    turn_hi(g + 1, 0)
                after(a, wv_full, 2 * b)
                for i, (c0, c1) in enumerate(((0, 2), (2, 3))):
                    a.wait_ge(pc_full, 2 * b + i + 1)
                    a.activation(pc2[0][:, c0:c1, :], pc[:, i, 0:(c1 - c0) * S].rearrange("p (c q) -> p c q", q=S), ACT.Copy).then_inc(pc_hi, 1)
                if e == 0 and turn:
                    turn_hi(g + 1, 1)
                if more:
                    probs(b + 1)
                if e == 0 and turn:
                    turn_hi(g + 1, 2)
                    turn_hi(g + 1, 3)
                if more:
                    split_cn(b + 1, 1 - e)
                if turn:
                    split_ct(b + 2, e)
                norm.scalar(a, b)

            for d in range(DC):
                turn_hi(0, d)
            for i in range(DC):
                a.wait_ge(pre_mm, i + 1)
                a.activation(a2[0][:, i, :], pre_bank(i)[:, 0:C], ACT.Copy).then_inc(pre_hi, 1)
            a.wait_ge(pre_done, 6)
            split_ct(0, 0)
            split_cn(0, 0)
            a.wait_ge(ct_lo, 1)
            split_ct(1, 1)
            queries(0)
            probs(0)
            batches(a, step)

        @block.vector
        def _(v):
            def turn_lo(g, d):
                v.wait_ge(x_hi, 4 * g + d + 1)
                v.tensor_tensor(x2[1][:, d, :], turn_bank[:, 0:W], x2[0][:, d, :].bitcast(F32), ALU.subtract).then_inc(x_lo, 1)

            def queries(g):
                for c in range(CC):
                    v.wait_ge(q_hi, 3 * g + c + 1)
                    v.scalar_tensor_tensor(q2[1][:, c, :], sc[:, c, 0:W], cb[:, c:c + 1], q2[0][:, c, :].bitcast(F32), ALU.add, ALU.subtract).then_inc(q_lo, 1)

            def maxima(b):
                after(v, row_full, b)
                for qt in range(2):
                    v.wait_ge(mx_full, 2 * b + qt + 1)
                    v.tensor_reduce(neg_max[:, qt:qt + 1], (mx, sc)[qt][:Q, 0:2, 0:NH], AX.XY, ALU.max, negate=True).then_inc(mx_done, 1)

            def shift(b, e):
                v.wait_ge(row_full, b + 1)
                v.tensor_tensor(row[:].rearrange("p (q t) -> p q t", q=2), mx[0:1, :, 384:384 + Q],
                                cq[:, e * S:(e + 1) * S].bitcast(F32).rearrange("p (q t) -> p q t", q=2), ALU.add).then_inc(row_done, 1)

            def step(b, e, g, more, turn):
                if e == 1 and turn:
                    queries(g + 1)
                if more:
                    maxima(b + 1)
                if e == 0 and turn:
                    turn_lo(g + 1, 0)
                if more:
                    v.wait_ge(cq_done, g + 1 + e)
                    shift(b + 1, 1 - e)
                for i, (c0, c1) in enumerate(((0, 2), (2, 3))):
                    v.wait_ge(pc_hi, 2 * b + i + 1)
                    v.tensor_tensor(pc2[1][:, c0:c1, :], pc[:, i, 0:(c1 - c0) * S].rearrange("p (c q) -> p c q", q=S),
                                    pc2[0][:, c0:c1, :].bitcast(F32), ALU.subtract).then_inc(pc_lo, 1)
                v.reciprocal(rec[:], pc[:Q, 1, 256:260].rearrange("p (q t) -> p q t", t=2)[:, :, 0]).then_inc(sum_step, 1)
                v.wait_ge(sum_step, 2 * b + 1)
                v.tensor_scalar(rg[:], rec[:], glob[:Q, GX1:GX1 + 1], None, ALU.mult).then_inc(sum_step, 1)
                if e == 0 and turn:
                    turn_lo(g + 1, 1)
                if more:
                    v.wait_ge(p_hi, b + 2)
                    v.tensor_tensor(p2[1][:], p32[:], p2[0][:].bitcast(F32), ALU.subtract).then_inc(p_lo, 1)
                if e == 0 and turn:
                    turn_lo(g + 1, 2)
                v.wait_ge(stored[e], 32 * g + 32)
                v.wait_ge(xb_done, b + 1)
                v.wait_ge(sum_step, 2 * b + 2)
                for qt in range(2):
                    v.wait_ge(wv_full, 2 * b + qt + 1)
                    v.scalar_tensor_tensor(xo[e][:, qt, :], mx[:Q, qt, :], rg[:, qt:qt + 1], xr[e][:, qt, :], ALU.mult, ALU.add).then_inc(xo_ready, 1)
                if e == 0 and turn:
                    turn_lo(g + 1, 3)
                v.wait_ge(xo_ready, 2 * b + 2)
                norm.vector(v, b, xo[e], xno[e], xn_ready)

            v.memset(ones[:].bitcast(F32), 1.0).then_inc(ones_set, 1)
            v.memset(ones_col[:].bitcast(F32), 1.0).then_inc(ones_set, 1)
            for d in range(DC):
                turn_lo(0, d)
            v.wait_ge(pre_mm, DC + 1)
            v.tensor_copy(cb[:], pc[:, 0, 0:CC]).then_inc(pre_done, 1)
            v.tensor_copy(wcq[:], pc[:, 0, CC:CC + DC]).then_inc(pre_done, 1)
            v.tensor_copy(bb[:], pc[0:1, 0, 8:9]).then_inc(pre_done, 1)
            for i in range(DC):
                v.wait_ge(pre_hi, i + 1)
                v.tensor_tensor(a2[1][:, i, :], pre_bank(i)[:, 0:C], a2[0][:, i, :].bitcast(F32), ALU.subtract).then_inc(pre_done, 1)
            v.wait_ge(wv_in, 32)
            v.tensor_scalar(gbv[:], gbv[:], glob[:Q, GX1:GX1 + 1], None, ALU.mult).then_inc(gbv_set, 1)
            split_weights(v, wv_raw[:], wv2[0][:], wv2[1][:], wv_split, 0)
            queries(0)
            maxima(0)
            v.wait_ge(cq_done, 1)
            shift(0, 0)
            v.wait_ge(p_hi, 1)
            v.tensor_tensor(p2[1][:], p32[:], p2[0][:].bitcast(F32), ALU.subtract).then_inc(p_lo, 1)
            batches(v, step)

        @block.tensor
        def _(t):
            def turn_tile(g, d):
                if d == 0:
                    t.wait_ge(x_in, 16 * g + 16)
                    after(t, cq_done, g)
                else:
                    t.wait_ge(x_lo, 4 * g + d)
                for j in range(4):
                    mm = t.transpose(turn_bank[:, j * Q:(j + 1) * Q], xt[:, j, d * 128:(d + 1) * 128], ident[:Q, :Q])
                mm.then_inc(turned, 1)

            def queries(g):
                t.wait_ge(x_lo, 4 * g + 4)
                after(t, exp_done, 6 * g)
                for c in range(CC):
                    for n, (pw, px) in enumerate(PASSES):
                        for d in range(DC):
                            mm = t.matmul(sc[:, c, 0:W], a2[pw][:, d, c * 128:(c + 1) * 128], x2[px][:, d, :],
                                          start=(n == 0 and d == 0), stop=(n == 2 and d == DC - 1))
                    mm.then_inc(q_full, 1)
                for d in range(DC):
                    mm = t.matmul(turn_bank[0:1, 0:W], wcq[:, d:d + 1], x2[0][:, d, :], start=(d == 0), stop=(d == DC - 1))
                mm.then_inc(turned, 1)

            def maxima(b, e, g, k):
                t.wait_ge(ct_hi, b + 1)
                t.wait_ge(q_hi, 3 * g + 3)
                t.wait_ge(cq_done, g + 1)
                after(t, xo_ready, 2 * b - 2)
                for qt in range(2):
                    if qt == 1:
                        after(t, exp_done, 3 * b)
                        t.wait_ge(q_lo, 3 * g + 3)
                    off = e * S + qt * Q
                    for half in range(2):
                        bank = (mx, sc)[qt][:Q, half, 0:NH]
                        for c in range(CC):
                            t.matmul(bank, q2[0][:, c, off:off + Q], ct2[k][0][:, c, COVER[half]], start=(c == 0), stop=False)
                        mm = t.matmul(bank, cq[:, off:off + Q], ones[:, 0:NH], start=False, stop=True)
                    mm.then_inc(mx_full, 1)

            def turn_maxima(b):
                t.wait_ge(mx_done, 2 * b + 2)
                for qt in range(2):
                    mm = t.transpose(mx[0:1, qt, 384:384 + Q], neg_max[:, qt:qt + 1], ident[:Q, :Q])
                mm.then_inc(row_full, 1)

            def scores(b, e, k):
                t.wait_ge(row_done, b + 1)
                t.wait_ge(ct_lo, b + 1)
                for j in range(3):
                    for i in range(2):
                        kc = 2 * j + i
                        bank = sc[:KP, j, i * S:(i + 1) * S]
                        for n, (pc_, pq) in enumerate(PASSES):
                            for c in range(CC):
                                t.matmul(bank, ct2[k][pc_][:, c, kc * KP:(kc + 1) * KP], q2[pq][:, c, e * S:(e + 1) * S],
                                         start=(n == 0 and c == 0), stop=False)
                        mm = t.matmul(bank, ones[:, 0:KP], row[:], start=False, stop=True)
                    mm.then_inc(st_full, 1)

            def weigh(b, k):
                t.wait_ge(p_lo, b + 1)
                t.wait_ge(cn_lo, b + 1)
                after(t, pc_lo, 2 * b)
                after(t, sum_step, 2 * b)
                for c in range(CC):
                    bank = pc[:, c // 2, (c % 2) * S:(c % 2 + 1) * S]
                    for n, (pw, pp) in enumerate(PASSES):
                        for kc in range(KC):
                            mm = t.matmul(bank, cn2[k][pw][:, kc, c * 128:(c + 1) * 128], p2[pp][:, kc * S:(kc + 1) * S],
                                          start=(n == 0 and kc == 0), stop=(n == 2 and kc == KC - 1))
                    if c == 1:
                        mm.then_inc(pc_full, 1)
                for qt in range(2):
                    for pp in range(2):
                        for kc in range(KC):
                            mm = t.matmul(pc[:Q, 1, 256 + 2 * qt:258 + 2 * qt], p2[pp][:, kc * S + qt * Q:kc * S + (qt + 1) * Q], ones_col[:KP, :],
                                          start=(pp == 0 and kc == 0), stop=(pp == 1 and kc == KC - 1))
                mm.then_inc(pc_full, 1)

            def values(b):
                t.wait_ge(pc_lo, 2 * b + 2)
                for qt in range(2):
                    for n, (pp, pw) in enumerate(PASSES):
                        for c in range(CC):
                            mm = t.matmul(mx[:Q, qt, :], pc2[pp][:, c, qt * Q:(qt + 1) * Q], wv2[pw][:, c, :],
                                          start=(n == 0 and c == 0), stop=(n == 2 and c == CC - 1))
                    mm.then_inc(wv_full, 1)

            def step(b, e, g, more, turn):
                if e == 1 and turn:
                    queries(g + 1)
                if more:
                    maxima(b + 1, 1 - e, g + e, 1 - e)
                if e == 0 and turn:
                    turn_tile(g + 1, 0)
                weigh(b, e)
                if e == 0 and turn:
                    turn_tile(g + 1, 1)
                if more:
                    turn_maxima(b + 1)
                    scores(b + 1, 1 - e, 1 - e)
                if e == 0 and turn:
                    turn_tile(g + 1, 2)
                values(b)
                if e == 0 and turn:
                    turn_tile(g + 1, 3)

            t.wait_ge(bias_in, 48)
            for d in range(DC):
                turn_tile(0, d)
            t.wait_ge(w_in, 32)
            for i in range(DC):
                for o in range(DC):
                    mm = t.matmul(pre_bank(i)[:, 0:C], wq_sb[:, o, i * 128:(i + 1) * 128], wk_sb[:, o, :], start=(o == 0), stop=(o == DC - 1))
                mm.then_inc(pre_mm, 1)
            for c in range(CC):
                for o in range(DC):
                    t.matmul(pc[:, 0, c:c + 1], wk_sb[:, o, c * 128:(c + 1) * 128], bq_sb[:, o:o + 1], start=(o == 0), stop=(o == DC - 1))
            for c in range(DC):
                for o in range(DC):
                    t.matmul(pc[:, 0, CC + c:CC + c + 1], wq_sb[:, o, c * 128:(c + 1) * 128], bk_sb[:, o:o + 1], start=(o == 0), stop=(o == DC - 1))
            for o in range(DC):
                mm = t.matmul(pc[0:1, 0, 8:9], bq_sb[:, o:o + 1], bk_sb[:, o:o + 1], start=(o == 0), stop=(o == DC - 1))
            mm.then_inc(pre_mm, 1)
            t.wait_ge(pre_done, 7)
            t.wait_ge(ones_set, 2)
            queries(0)
            maxima(0, 0, 0, 0)
            turn_maxima(0)
            scores(0, 0, 0)
            t.wait_ge(wv_split, 2)
            batches(t, step)



NTOP = NBLK // 4
OFF = -1e30
TINY = -87.3365
TAKEN, SPARE = -3e38, -2e38


def load_ffn1(nc, sems, router_t, w1_t, w2_t, rw, w1, w2):
    with Stage(nc, sems, "fw") as st:
        raw = [st.sb(f"raw{k}", [128, I1]) for k in range(4)]
        w_in = [st.sem(f"w_in{k}") for k in range(4)]
        hi_done, lo_done = st.sem("hi_done"), st.sem("lo_done")
        block = st.stack.enter_context(nc.Block())

        def flat(t):
            return t.rearrange("p c n -> p (c n)")
        pieces = [(router_t.rearrange("(c p) n -> p c n", p=128), [flat(r[:]) for r in rw], DC)]
        pieces += [(w1_t[c * 128:(c + 1) * 128, :].unsqueeze(1), [w[:, c, :] for w in w1], 1) for c in range(DC)]
        pieces += [(w2_t[c * 512:(c + 1) * 512, :].rearrange("(c p) n -> p c n", p=128),
                    [flat(w[:, 4 * c:4 * c + 4, :]) for w in w2], 4) for c in range(NBLK // 4)]

        def columns(i):
            return DC * NBLK if i == 0 else I1

        @block.sync
        def _(sp):
            for i, (src, _, rows) in enumerate(pieces):
                if i >= 4:
                    sp.wait_ge(lo_done, i - 3)
                sp.dma_start(raw[i % 4][:, 0:columns(i)].rearrange("p (c n) -> p c n", c=rows), src).then_inc(w_in[i % 4], 16)

        @block.scalar
        def _(a):
            for i, (_, parts, _) in enumerate(pieces):
                a.wait_ge(w_in[i % 4], 16 * (i // 4) + 16)
                a.activation(parts[0], raw[i % 4][:, 0:columns(i)], ACT.Copy).then_inc(hi_done, 1)

        @block.vector
        def _(v):
            for i, (_, parts, _) in enumerate(pieces):
                v.wait_ge(hi_done, i + 1)
                v.tensor_tensor(parts[1], raw[i % 4][:, 0:columns(i)], parts[0].bitcast(F32), ALU.subtract).then_inc(lo_done, 1)
            v.wait_ge(lo_done, len(pieces))


def ffn1(nc, sems, xn, router_t, router_b, w1_t, b1, w2_t, b2, ident_d, glob, x, result):
    with Stage(nc, sems, "f1") as st:
        ident = st.sb("ident", [128, 128])
        w1 = [st.sb(f"w1{p}", [128, DC, I1], F32R) for p in range(2)]
        w2 = [st.sb(f"w2{p}", [128, NBLK, D], F32R) for p in range(2)]
        rw = [st.sb(f"rw{p}", [128, DC, NBLK], F32R) for p in range(2)]
        load_ffn1(nc, sems, router_t, w1_t, w2_t, rw, w1, w2)
        b1_sb, rb, gb2 = st.sb("b1", [128, NBLK]), st.sb("rb", [128, NBLK]), st.sb("gb2", [128, D])
        select = st.sb("select", [NBLK, NBLK, 128], BF16)
        xt, xr = st.sb("xt", [128, 4, D]), st.sb("xr", [128, 4, D])
        x2 = [[st.sb(f"xT{k}{p}", [128, DC, 512], F32R) for p in range(2)] for k in range(2)]
        r32 = [st.sb(f"r32_{k}", [128, 512]) for k in range(2)]
        h2 = [[st.sb(f"h{s}{p}", [128, 512], F32R) for p in range(2)] for s in range(4)]
        lg, z, unused = (st.sb(n, [128, 4, NBLK]) for n in ("lg", "z", "unused"))
        zc, left = (st.sb(n, [128, 4, NBLK + 8 - NTOP]) for n in ("zc", "left"))
        top1, top8, top4 = st.sb("top1", [128, 4]), st.sb("top8", [128, 4, 8]), st.sb("top4", [128, 4, 8])
        off = [st.sb(f"off{k}", [NBLK, 512], BF16) for k in range(2)]

        turn_bank, route_bank = st.ps("turn"), st.ps("route")
        hid = [st.ps(f"hid{k}") for k in range(2)]
        out = st.ps("out", (128, 4, 512))

        small_in, rb_in, x_in, xr_in, stored = (st.sem(n) for n in ("small_in", "rb_in", "x_in", "xr_in", "stored"))
        turned, lg_full, off_full, h_full, dn_done = (st.sem(n) for n in ("turned", "lg_full", "off_full", "h_full", "dn_done"))
        x_hi, relu_done, h_hi, x_lo, h_lo = (st.sem(n) for n in ("x_hi", "relu_done", "h_hi", "x_lo", "h_lo"))
        prep = st.sem("prep")
        route, xb_done, off_ready, xo_ready = st.sem("route"), st.sem("xb_done"), st.sem("off_ready"), st.sem("xo_ready")
        TURN_AT, ROUTE_AT, OFF_AT = (2, 4, 6, 8), 10, 13
        ROUTE_STEPS = 14
        block = st.stack.enter_context(nc.Block())

        def tiles(t, g):
            return t[bass.ds(g * 512, 512), :].rearrange("(j p) c -> p j c", p=128)

        @block.sync
        def _(sp):
            def load_x(g):
                after(sp, turned, 4 * g)
                sp.dma_start(xt[:], tiles(xn, g)).then_inc(x_in, 16)

            def load_xr(g):
                after(sp, stored, 16 * g)
                sp.dma_start(xr[:], tiles(x, g)).then_inc(xr_in, 16)

            def step(g, k, u, more=True):
                if more:
                    load_x(g + 1)
                sp.wait_ge(xo_ready, 4 * g + 4)
                sp.dma_start(tiles(result, g), xr[:]).then_inc(stored, 16)
                if more:
                    load_xr(g + 1)
            load_x(0)
            sp.dma_start(ident[:], ident_d).then_inc(small_in, 16)
            sp.dma_start(b1_sb[:], b1.rearrange("(c p) -> p c", p=128), allow_slow_non_contiguous=True).then_inc(small_in, 16)
            sp.dma_start(rb[:], router_b.partition_broadcast(128)).then_inc(rb_in, 16)
            sp.dma_start(gb2[:], b2.partition_broadcast(128)).then_inc(rb_in, 16)
            load_xr(0)
            step(0, 0, 0)
            pairs(sp, 1, G5 - 1, step)
            step(G5 - 1, 0, 3, False)
            sp.wait_ge(stored, 16 * G5)

        @block.gpsimd
        def _(pool):
            def step(g, k, u):
                pool.wait_ge(xr_in, 16 * g + 16)
                pool.tensor_tensor(xr[:], xr[:], gb2[:].unsqueeze(1).broadcast_to([128, 4, D]), ALU.add).then_inc(xb_done, 1)
            pool.wait_ge(prep, 3)
            pairs(pool, 0, G5, step)

        @block.scalar
        def _(a):
            def turn_hi(g, k, d):
                if d == 0:
                    after(a, h_full, 16 * g - 16)
                a.wait_ge(turned, 4 * g + d + 1)
                a.activation(x2[k][0][:, d, :], turn_bank[:], ACT.Copy).then_inc(x_hi, 1)

            def step(g, k, u, more=True):
                for i in range(NBLK):
                    if not (is_first(g) and i < 2):
                        a.wait_ge(h_lo, 16 * g + i - 1)
                    a.wait_ge(h_full, 16 * g + i + 1)
                    a.activation(r32[i % 2][:], hid[i % 2][:], ACT.Relu, bias=b1_sb[:, i:i + 1]).then_inc(relu_done, 1)
                    if not (is_first(g) and i < 4):
                        a.wait_ge(dn_done, 16 * g + i - 3)
                    a.wait_ge(relu_done, 16 * g + i + 1)
                    a.activation(h2[i % 4][0][:], r32[i % 2][:], ACT.Copy).then_inc(h_hi, 1)
                    if i in TURN_AT and more:
                        turn_hi(g + 1, 1 - k, TURN_AT.index(i))
            for d in range(DC):
                turn_hi(0, 0, d)
            step(0, 0, 0)
            pairs(a, 1, G5 - 1, step)
            step(G5 - 1, 0, 3, False)

        @block.vector
        def _(v):
            def turn_lo(g, k, d):
                v.wait_ge(x_hi, 4 * g + d + 1)
                v.tensor_tensor(x2[k][1][:, d, :], turn_bank[:], x2[k][0][:, d, :].bitcast(F32), ALU.subtract).then_inc(x_lo, 1)

            def choose(g):
                at = ROUTE_STEPS * g
                v.wait_ge(lg_full, g + 1)
                v.tensor_tensor(lg[:], route_bank[:, 0:4 * NBLK].rearrange("p (j n) -> p j n", n=NBLK),
                                rb[:].unsqueeze(1).broadcast_to([128, 4, NBLK]), ALU.add).then_inc(route, 1)
                v.wait_ge(route, at + 1)
                v.tensor_reduce(top1[:], lg[:], AX.X, ALU.max).then_inc(route, 1)
                v.wait_ge(route, at + 2)
                v.tensor_tensor(z[:], lg[:], top1[:].unsqueeze(2).broadcast_to([128, 4, NBLK]), ALU.subtract).then_inc(route, 1)
                v.wait_ge(route, at + 3)
                v.tensor_scalar(zc[:, :, 0:NBLK], z[:], TINY, None, ALU.max).then_inc(route, 1)
                v.wait_ge(route, at + 4)
                v.memset(top4[:, :, NTOP:8], SPARE).then_inc(route, 1)
                for j in range(4):
                    v.max(top8[:, j, :], zc[:, j, 0:NBLK]).then_inc(route, 1)
                v.wait_ge(route, at + 9)
                v.tensor_copy(top4[:, :, 0:NTOP], top8[:, :, 0:NTOP]).then_inc(route, 1)

            def take_out(g):
                at = ROUTE_STEPS * g
                for j in range(4):
                    v.match_replace(left[:, j, :], top4[:, j, :], zc[:, j, :], TAKEN).then_inc(route, 1)
                v.wait_ge(route, at + 14)
                v.tensor_scalar(unused[:], left[:, :, 0:NBLK], TAKEN, None, ALU.not_equal).then_inc(off_ready, 1)

            def take_off(g, k):
                v.wait_ge(off_full, g + 1)
                after(v, h_full, 16 * g - 16)
                v.tensor_copy(off[k][:], route_bank[:NBLK, :]).then_inc(off_ready, 1)

            def step(g, k, u, more=True):
                for i in range(NBLK):
                    if not (is_first(g) and i < 4):
                        v.wait_ge(dn_done, 16 * g + i - 3)
                    v.wait_ge(h_hi, 16 * g + i + 1)
                    if i == ROUTE_AT + 1 and more:
                        v.wait_ge(route, ROUTE_STEPS * (g + 1) + 10)
                    v.tensor_tensor(h2[i % 4][1][:], r32[i % 2][:], h2[i % 4][0][:].bitcast(F32), ALU.subtract).then_inc(h_lo, 1)
                    if i in TURN_AT and more:
                        turn_lo(g + 1, 1 - k, TURN_AT.index(i))
                    if i == ROUTE_AT and more:
                        choose(g + 1)
                    if i == ROUTE_AT + 1 and more:
                        take_out(g + 1)
                    if i == OFF_AT and more:
                        take_off(g + 1, 1 - k)
                v.wait_ge(dn_done, 16 * g + 16)
                v.wait_ge(xb_done, g + 1)
                for j in range(4):
                    v.scalar_tensor_tensor(xr[:, j, :], out[:, j, :], glob[:, GF1:GF1 + 1], xr[:, j, :], ALU.mult, ALU.add).then_inc(xo_ready, 1)
            v.memset(zc[:, :, NBLK:], SPARE).then_inc(prep, 1)
            v.wait_ge(small_in, 32)
            v.tensor_scalar(select[:], ident[:NBLK, 0:NBLK].unsqueeze(2).broadcast_to([NBLK, NBLK, 128]), OFF, None, ALU.mult).then_inc(prep, 1)
            v.wait_ge(rb_in, 32)
            v.tensor_scalar(gb2[:], gb2[:], glob[:, GF1:GF1 + 1], None, ALU.mult).then_inc(prep, 1)
            v.wait_ge(prep, 3)
            for d in range(DC):
                turn_lo(0, 0, d)
            choose(0)
            v.wait_ge(route, 10)
            take_out(0)
            take_off(0, 0)
            step(0, 0, 0)
            pairs(v, 1, G5 - 1, step)
            step(G5 - 1, 0, 3, False)

        @block.tensor
        def _(t):
            def turn_tile(g, d):
                if d == 0:
                    t.wait_ge(x_in, 16 * g + 16)
                after(t, x_lo, 4 * g + d)
                for j in range(4):
                    mm = t.transpose(turn_bank[:, j * 128:(j + 1) * 128], xt[:, j, d * 128:(d + 1) * 128], ident[:])
                mm.then_inc(turned, 1)

            def logits(g, k):
                t.wait_ge(x_lo, 4 * g + 4)
                after(t, off_ready, 2 * g)
                for j in range(4):
                    for n, (px, pw) in enumerate(PASSES):
                        for d in range(DC):
                            mm = t.matmul(route_bank[:, j * NBLK:(j + 1) * NBLK], x2[k][px][:, d, j * 128:(j + 1) * 128], rw[pw][:, d, :],
                                          start=(n == 0 and d == 0), stop=(n == 2 and d == DC - 1))
                mm.then_inc(lg_full, 1)

            def turn_off(g):
                t.wait_ge(off_ready, 2 * g + 1)
                for j in range(4):
                    mm = t.transpose(route_bank[:NBLK, j * 128:(j + 1) * 128], unused[:, j, :], ident[:])
                mm.then_inc(off_full, 1)

            def up(g, k, i):
                if i == 0:
                    t.wait_ge(off_ready, 2 * g + 2)
                if not (is_first(g) and i < 2):
                    t.wait_ge(relu_done, 16 * g + i - 1)
                for n, (pw, px) in enumerate(PASSES):
                    for d in range(DC):
                        t.matmul(hid[i % 2][:], w1[pw][:, d, i * 128:(i + 1) * 128], x2[k][px][:, d, :], start=(n == 0 and d == 0), stop=False)
                t.matmul(hid[i % 2][:], select[:, i, :], off[k][:], start=False, stop=True).then_inc(h_full, 1)

            def down_chunk(g, i):
                t.wait_ge(h_lo, 16 * g + i + 1)
                if i == 0:
                    after(t, xo_ready, 4 * g)
                for j in range(4):
                    for n, (ph, pw) in enumerate(PASSES):
                        mm = t.matmul(out[:, j, :], h2[i % 4][ph][:, j * 128:(j + 1) * 128], w2[pw][:, i, :],
                                      start=(i == 0 and n == 0), stop=(i == NBLK - 1 and n == 2))
                mm.then_inc(dn_done, 1)

            def step(g, k, u, more=True):
                for i in range(NBLK + 2):
                    if i < NBLK:
                        up(g, k, i)
                    if i >= 2:
                        down_chunk(g, i - 2)
                    if i in TURN_AT and more:
                        turn_tile(g + 1, TURN_AT.index(i))
                    if i == ROUTE_AT and more:
                        logits(g + 1, 1 - k)
                    if i == OFF_AT and more:
                        turn_off(g + 1)
            t.wait_ge(small_in, 32)
            for d in range(DC):
                turn_tile(0, d)
            t.wait_ge(prep, 2)
            logits(0, 0)
            turn_off(0)
            step(0, 0, 0)
            pairs(t, 1, G5 - 1, step)
            step(G5 - 1, 0, 3, False)


def gated_stack(nc, ins, result):
    def dram(name, *shape):
        return nc.dram_tensor(name, shape, F32).ap()
    q_parts = [dram(f"q_part{p}", D, TOK) for p in range(2)]
    mask_row, some_row, attn = dram("mask_row", B, M), dram("some_row", B), dram("attn", TOK, D)
    w_parts = [[dram(f"{n}{p}", *shape) for p in range(2)] for n, shape in (("gate_t", (D, I0)), ("up_t", (D, I0)), ("down_t", (I0, D)))]
    gate_d, up_d, t_d, v_d = (dram(n, UNITS, 128, 2048) for n in ("gate", "up", "gated", "hidden"))
    x1, x2, x3 = (dram(f"x{i}", TOK, D) for i in range(1, 4))
    xn1, xn2, xn3 = (dram(f"xn{i}", TOK, D) for i in range(1, 4))
    x, ident = ins["x"], ins["ident"]
    sems = []
    with nc.sbuf_tensor("glob", [128, NGLOB], F32) as glob:
        gates(nc, sems, ins["g_xattn"], ins["g_ffn"], glob)
        project_queries(nc, sems, x, ins["L0_xattn_Wq"], ident, q_parts)
        attend0(nc, sems, ins["ctx_t"], ins["mask"], ins["L0_xattn_Wk"], ins["L0_xattn_Wv"], q_parts, mask_row, some_row, ident, attn)
        project_out(nc, sems, attn, ins["L0_xattn_Wo"], ident, glob, x, x1, xn1)
        clear(nc, sems)
        ffn0(nc, sems, xn1, ins["L0_ffn_w_gate"], ins["L0_ffn_w_up"], ins["L0_ffn_w_down"], w_parts, ident, glob,
             gate_d, up_d, t_d, v_d, x1, x2, xn2)
        clear(nc, sems)
        attend1(nc, sems, xn2, ins["ctx"], ins["ctx_t"], ins["L1_xattn_Wq"], ins["L1_xattn_bq"], ins["L1_xattn_Wk"], ins["L1_xattn_bk"],
                ins["L1_wv_t"], ins["L1_xattn_bv"], ident, glob, x2, x3, xn3)
        ffn1(nc, sems, xn3, ins["L1_router_t"], ins["L1_ffn_router_b"], ins["L1_w1_t"], ins["L1_ffn_b1"], ins["L1_w2_t"], ins["L1_ffn_b2"],
             ident, glob, x3, result)


def kernel(**inputs):
    import numpy as np
    import concourse.bacc as bacc
    from concourse.bass_utils import run_bass_kernel_spmd

    given = {n: np.asarray(a) for n, a in inputs.items()}
    ins = {n: given[n] for n in ("g_xattn", "g_ffn", "L0_xattn_Wq", "L0_xattn_Wk", "L0_xattn_Wv", "L0_xattn_Wo",
                                 "L0_ffn_w_gate", "L0_ffn_w_up", "L0_ffn_w_down", "L1_xattn_Wq", "L1_xattn_bq", "L1_xattn_Wk",
                                 "L1_xattn_bk", "L1_xattn_bv", "L1_ffn_router_b", "L1_ffn_b1", "L1_ffn_b2")}
    ins["x"] = given["x"].reshape(TOK, D)
    ins["ctx"] = given["ctx_768"]
    ins["ctx_t"] = given["ctx_768"].transpose(0, 2, 1)
    ins["mask"] = np.ascontiguousarray(given["mask_BxS2_bf1"]).view(np.uint8)
    ins["L1_wv_t"] = given["L1_xattn_Wv"].T
    ins["L1_router_t"] = given["L1_ffn_router_w"].T
    ins["L1_w1_t"] = given["L1_ffn_w1"].T
    ins["L1_w2_t"] = given["L1_ffn_w2"].T
    ins["ident"] = np.eye(128, dtype=np.float32)

    nc = bacc.Bacc("TRN2", target_bir_lowering=False, num_devices=1)
    arrays, aps = {}, {}
    for name, a in ins.items():
        a = np.ascontiguousarray(a)
        arrays[f"in_{name}_dram"] = a
        aps[name] = nc.dram_tensor(f"in_{name}_dram", a.shape, mybir.dt.from_np(a.dtype), kind="ExternalInput").ap()
    out = nc.dram_tensor("out_0_dram", (TOK, D), F32, kind="ExternalOutput").ap()
    gated_stack(nc, aps, out)
    r = run_bass_kernel_spmd(nc, [arrays], core_ids=[0])
    return r.results[0]["out_0_dram"].reshape(B, S, D)
```

```python
from contextlib import ExitStack

import concourse.bass as bass
from concourse import mybir

F32 = mybir.dt.float32
F32R = mybir.dt.float32r
BF16 = mybir.dt.bfloat16
F16 = mybir.dt.float16
ALU = mybir.AluOpType
ACT = mybir.ActivationFunctionType
AX = mybir.AxisListType

B, S, D = 16, 224, 512
TOK = B * S
M, C = 750, 384
H, HD = 16, 32
I0 = 1536
I1, NBLK = 2048, 16
DC, CC = D // 128, C // 128
KC, KP = 6, 125
NH = 376
HALVES = (slice(0, NH), slice(NH, M))
COVER = (slice(0, NH), slice(M - NH, M))
EPS = 1e-5
QMAX = 32767.0
ROUND = 12582912.0
G5 = TOK // 512
PASSES = ((0, 0), (0, 1), (1, 0))


def width(half):
    return HALVES[half].stop - HALVES[half].start


class Stage:

    def __init__(self, nc, sems, name):
        self.nc, self.sems, self.name, self.stack = nc, sems, name, ExitStack()

    def __enter__(self):
        self.stack.__enter__()
        return self

    def __exit__(self, *what):
        return self.stack.__exit__(*what)

    def sb(self, name, shape, dt=F32):
        return self.stack.enter_context(self.nc.sbuf_tensor(f"{self.name}_{name}", shape, dt))

    def ps(self, name, shape=(128, 512), dt=F32):
        return self.stack.enter_context(self.nc.psum_tensor(f"{self.name}_{name}", list(shape), dt))

    def sem(self, name):
        self.sems.append(self.nc.alloc_semaphore(name=f"{self.name}_{name}"))
        return self.sems[-1]


def clear(nc, sems):
    nc.clear_and_free_semaphores(sems)
    sems.clear()
    nc.all_engine_barrier()


def pairs(eng, first, end, body):
    rounds = (end - first) // 2
    if rounds:
        with eng.Fori(0, rounds) as r:
            body(2 * r + first, first % 2, r + first // 2)
            body(2 * r + first + 1, (first + 1) % 2, r + (first + 1) // 2)
    if 2 * rounds < end - first:
        body(end - 1, (end - 1) % 2, (end - 1) // 2)


def sixes(eng, first, end, body):
    rounds = (end - first) // 6
    if rounds:
        with eng.Fori(0, rounds) as r:
            for i in range(first, first + 6):
                body(6 * r + i, i % 6, r + i // 6)
    for g in range(first + 6 * rounds, end):
        body(g, g % 6, g // 6)


class Norm:

    def __init__(self, st, rt, nt=4):
        self.rt, self.nt = rt, nt
        self.stats = st.sb("ln_stats", [128, nt, 6])
        (self.total, self.apart, self.m2, self.mean, self.apart2, self.m2e, self.ve, self.sd, self.r0,
         self.a, self.b, self.c, self.r) = (st.sb(f"ln_{n}", [128, nt]) for n in (
             "total", "apart", "m2", "mean", "apart2", "m2e", "ve", "sd", "r0", "a", "b", "c", "r"))
        self.dve = st.sem("ln_dve")
        self.var_ready = st.sem("ln_var_ready")
        self.sd_ready = st.sem("ln_sd_ready")

    def vector(self, v, g, x, y, out_ready):
        rt, nt = self.rt, self.nt
        at = g * (11 + nt) + nt
        for j in range(nt):
            v.bn_stats(self.stats[:rt, j, :], x[:rt, j, :]).then_inc(self.dve, 1)
        v.wait_ge(self.dve, at)
        even, odd = self.stats[:rt, :, 1], self.stats[:rt, :, 4]
        v.tensor_tensor(self.total[:rt, :], even, odd, ALU.add).then_inc(self.dve, 1)
        v.tensor_tensor(self.apart[:rt, :], even, odd, ALU.subtract).then_inc(self.dve, 1)
        v.tensor_tensor(self.m2[:rt, :], self.stats[:rt, :, 2], self.stats[:rt, :, 5], ALU.add).then_inc(self.dve, 1)
        v.wait_ge(self.dve, at + 3)
        v.tensor_scalar(self.mean[:rt, :], self.total[:rt, :], 0.5, None, ALU.mult).then_inc(self.dve, 1)
        v.tensor_tensor(self.apart2[:rt, :], self.apart[:rt, :], self.apart[:rt, :], ALU.mult).then_inc(self.dve, 1)
        v.tensor_scalar(self.m2e[:rt, :], self.m2[:rt, :], 1.0 / D, EPS, ALU.mult, ALU.add).then_inc(self.dve, 1)
        v.wait_ge(self.dve, at + 6)
        v.scalar_tensor_tensor(self.ve[:rt, :], self.apart2[:rt, :], 0.25, self.m2e[:rt, :], ALU.mult, ALU.add).then_inc(self.var_ready, 1)
        v.wait_ge(self.sd_ready, g + 1)
        v.reciprocal(self.r0[:rt, :], self.sd[:rt, :]).then_inc(self.dve, 1)
        v.wait_ge(self.dve, at + 7)
        v.tensor_tensor(self.a[:rt, :], self.r0[:rt, :], self.r0[:rt, :], ALU.mult).then_inc(self.dve, 1)
        v.wait_ge(self.dve, at + 8)
        v.tensor_tensor(self.b[:rt, :], self.a[:rt, :], self.ve[:rt, :], ALU.mult).then_inc(self.dve, 1)
        v.wait_ge(self.dve, at + 9)
        v.tensor_scalar(self.c[:rt, :], self.b[:rt, :], -0.5, 1.5, ALU.mult, ALU.add).then_inc(self.dve, 1)
        v.wait_ge(self.dve, at + 10)
        v.tensor_tensor(self.r[:rt, :], self.r0[:rt, :], self.c[:rt, :], ALU.mult).then_inc(self.dve, 1)
        v.wait_ge(self.dve, at + 11)
        for j in range(nt):
            v.tensor_scalar(y[:rt, j, :], x[:rt, j, :], self.mean[:rt, j:j + 1], self.r[:rt, j:j + 1],
                            ALU.subtract, ALU.mult).then_inc(out_ready, 1)

    def scalar(self, a, g):
        a.wait_ge(self.var_ready, g + 1)
        a.activation(self.sd[:self.rt, :], self.ve[:self.rt, :], ACT.Sqrt).then_inc(self.sd_ready, 1)


class Turn:

    def __init__(self, st, rt, n, src_ready, per_group=4):
        self.rt, self.n, self.w = rt, n, 4 * rt
        self.src_ready, self.per = src_ready, per_group
        self.bank = st.ps("turn", (128, 2, 512))
        self.hi = [st.sb(f"turn_hi{k}", [128, n, self.w], F32R) for k in range(2)]
        self.lo = [st.sb(f"turn_lo{k}", [128, n, self.w], F32R) for k in range(2)]
        self.turned = st.sem("turned")
        self.hi_ready = st.sem("turn_hi")
        self.lo_ready = st.sem("turn_lo")

    def tensor(self, t, g, src, ident, chunks=None):
        chunks = range(self.n) if chunks is None else chunks
        if self.src_ready is not None and 0 in chunks:
            t.wait_ge(self.src_ready, self.per * (g + 1))
        rt = self.rt
        for d in chunks:
            use = g * self.n + d
            if not (isinstance(use, int) and use < 2):
                t.wait_ge(self.lo_ready, use - 1)
            for j in range(4):
                last = t.transpose(self.bank[:, use_bank(d), j * rt:(j + 1) * rt],
                                   src[:rt, j, d * 128:(d + 1) * 128], ident[:rt, :rt])
            last.then_inc(self.turned, 1)

    def scalar(self, a, g, k, free=None, chunks=None):
        chunks = range(self.n) if chunks is None else chunks
        if free is not None and 0 in chunks:
            a.wait_ge(*free)
        for d in chunks:
            a.wait_ge(self.turned, g * self.n + d + 1)
            a.activation(self.hi[k][:, d, :], self.bank[:, use_bank(d), 0:self.w], ACT.Copy).then_inc(self.hi_ready, 1)

    def vector(self, v, g, k, chunks=None):
        for d in range(self.n) if chunks is None else chunks:
            v.wait_ge(self.hi_ready, g * self.n + d + 1)
            v.tensor_tensor(self.lo[k][:, d, :], self.bank[:, use_bank(d), 0:self.w],
                            self.hi[k][:, d, :].bitcast(F32), ALU.subtract).then_inc(self.lo_ready, 1)


def use_bank(d):
    return d % 2


def split_weights(v, raw, hi, lo, chain, at):
    v.tensor_copy(hi, raw).then_inc(chain, 1)
    v.wait_ge(chain, at + 1)
    v.tensor_tensor(lo, raw, hi.bitcast(F32), ALU.subtract).then_inc(chain, 1)


def project_queries(nc, sems, x, wq, ident_d, q_parts):
    with Stage(nc, sems, "q0") as st:
        ident = st.sb("ident", [128, 128])
        w_raw = st.sb("w_raw", [128, DC, D])
        w = [st.sb("w_hi", [128, DC, D], F32R), st.sb("w_lo", [128, DC, D], F32R)]
        xt = [st.sb(f"x{k}", [128, 4, D]) for k in range(2)]
        q_hi = [st.sb(f"q_hi{k}", [128, 4, 512], F32R) for k in range(2)]
        q_lo = [st.sb(f"q_lo{k}", [128, 4, 512], F32R) for k in range(2)]
        out = st.ps("out", (128, 4, 512))
        x_in = [st.sem(f"x_in{k}") for k in range(2)]
        q_out = [st.sem(f"q_out{k}") for k in range(2)]
        ident_in, w_in, xn_ready = st.sem("ident_in"), st.sem("w_in"), st.sem("xn_ready")
        w_split, mm_done = st.sem("w_split"), st.sem("mm_done")
        qh_ready, ql_ready = st.sem("qh_ready"), st.sem("ql_ready")
        norm, turn = Norm(st, 128), Turn(st, 128, DC, xn_ready)
        block = st.stack.enter_context(nc.Block())

        @block.sync
        def _(sp):
            def load(g, k, u):
                if not (isinstance(g, int) and g < 2):
                    sp.wait_ge(turn.turned, 4 * g - 4)
                sp.dma_start(xt[k][:], x[bass.ds(g * 512, 512), :].rearrange("(j p) c -> p j c", p=128)).then_inc(x_in[k], 16)
            def store(g, k, u):
                sp.wait_ge(qh_ready, 4 * g + 4)
                sp.dma_start(q_parts[0][:, bass.ds(g * 512, 512)].rearrange("(c p) t -> p c t", p=128), q_hi[k][:].bitcast(F32)).then_inc(q_out[k], 16)
                sp.wait_ge(ql_ready, 4 * g + 4)
                sp.dma_start(q_parts[1][:, bass.ds(g * 512, 512)].rearrange("(c p) t -> p c t", p=128), q_lo[k][:].bitcast(F32)).then_inc(q_out[k], 16)

            def step(g, k, u):
                load(g + 2, k, u + 1)
                store(g, k, u)
            load(0, 0, 0)
            sp.dma_start(ident[:], ident_d).then_inc(ident_in, 16)
            sp.dma_start(w_raw[:], wq.rearrange("(c p) n -> p c n", p=128)).then_inc(w_in, 16)
            load(1, 1, 0)
            sp.sem_inc(q_out[0], 32)
            sp.sem_inc(q_out[1], 32)
            pairs(sp, 0, G5 - 2, step)
            store(G5 - 2, 1, 2)
            store(G5 - 1, 0, 3)
            sp.wait_ge(q_out[0], 32 + 32 * 4)
            sp.wait_ge(q_out[1], 32 + 32 * 3)

        @block.scalar
        def _(a):
            def step(g, k, u, more=True):
                if more:
                    norm.scalar(a, g + 1)
                for o in range(4):
                    if o == 2 and more:
                        turn.scalar(a, g + 1, 1 - k, (mm_done, 4 * g) if not isinstance(g, int) or g else None)
                    if o == 0:
                        a.wait_ge(q_out[k], 32 * u + 32)
                    a.wait_ge(mm_done, 4 * g + o + 1)
                    a.activation(q_hi[k][:, o, :], out[:, o, :], ACT.Copy).then_inc(qh_ready, 1)
            norm.scalar(a, 0)
            turn.scalar(a, 0, 0)
            step(0, 0, 0)
            pairs(a, 1, G5 - 1, step)
            step(G5 - 1, 0, 3, False)

        @block.vector
        def _(v):
            def front(g, k, u):
                v.wait_ge(x_in[k], 16 * u + 16)
                norm.vector(v, g, xt[k], xt[k], xn_ready)

            def step(g, k, u, more=True):
                if more:
                    front(g + 1, 1 - k, u + k)
                for o in range(4):
                    if o == 2 and more:
                        turn.vector(v, g + 1, 1 - k)
                    v.wait_ge(qh_ready, 4 * g + o + 1)
                    v.tensor_tensor(q_lo[k][:, o, :], out[:, o, :], q_hi[k][:, o, :].bitcast(F32), ALU.subtract).then_inc(ql_ready, 1)
            front(0, 0, 0)
            turn.vector(v, 0, 0)
            v.wait_ge(w_in, 16)
            split_weights(v, w_raw[:], w[0][:], w[1][:], w_split, 0)
            step(0, 0, 0)
            pairs(v, 1, G5 - 1, step)
            step(G5 - 1, 0, 3, False)

        @block.tensor
        def _(t):
            def step(g, k, u, more=True):
                x2 = (turn.hi[k], turn.lo[k])
                for o in range(4):
                    if o == 2 and more:
                        turn.tensor(t, g + 1, xt[1 - k], ident)
                    if o == 0:
                        t.wait_ge(turn.lo_ready, 4 * g + 4)
                    if not isinstance(g, int) or g:
                        t.wait_ge(ql_ready, 4 * g - 3 + o)
                    for n, (pw, px) in enumerate(PASSES):
                        for d in range(DC):
                            mm = t.matmul(out[:, o, :], w[pw][:, d, o * 128:(o + 1) * 128], x2[px][:, d, :],
                                          start=(n == 0 and d == 0), stop=(n == 2 and d == DC - 1))
                    mm.then_inc(mm_done, 1)
            t.wait_ge(ident_in, 16)
            turn.tensor(t, 0, xt[0], ident)
            t.wait_ge(w_split, 2)
            step(0, 0, 0)
            pairs(t, 1, G5 - 1, step)
            step(G5 - 1, 0, 3, False)



NEG = -2.0 ** 127
VW = 98
CH = 4


def attention_fills(c, h, last):
    def later(n):
        return (c + n) % CH, (c + n) // CH
    side = []
    if (c, h) in ((0, 0), (1, 2)):
        side = [("K", *later(3), 0), ("K", *later(3), 1)]
    elif c > 1 and h < 2:
        side = [("K", *later(3), h)]
    if c == 0:
        side += [("V", 1, 0, kc) for kc in ((0,), (1, 2, 3), (4, 5), ())[h]]
    elif c > 1 and h > 1:
        side += [("V", 0, 1, 3 * (c - 2) + kc) for kc in ((0, 1), (2,))[h - 2]]
    maxima = [("max", *later(2), h, qt, half) for qt in range(2) for half in range(2)]
    out = []
    for n in range(max(len(side), len(maxima))):
        out += side[n:n + 1] + maxima[n:n + 1]
    out = out[:1] + ([("mT", *later(1))] if h == 0 else []) + out[1:]
    next_batch = {"K": 2, "V": 2, "max": 2, "mT": 2}
    return [p for p in out if not (last and p[next_batch[p[0]]])]


def attention_order():
    first = [("K", c, 0, half) for c in range(3) for half in range(2)] + [("V", 0, 0, kc) for kc in range(KC)]
    first += [("max", c, 0, h, qt, half) for c in range(2) for h in range(4) for qt in range(2) for half in range(2)]
    first += [("mT", 0, 0)]
    batch = [(c, h, attention_fills(c, h, False)) for c in range(CH) for h in range(4)]
    return first, batch


def attend0(nc, sems, ctx_t, mask, wk, wv, q_parts, mask_row, some_row, ident_d, attn):
    with Stage(nc, sems, "a0") as st:
        first, batch = attention_order()
        P0 = len(first)
        PB = sum(len(f) for _, _, f in batch)
        assert P0 % 3 == 0 and PB % 3 == 1

        ident = st.sb("ident", [128, 128])
        zero = st.sb("zero", [128, M])
        w_raw = st.sb("w_raw", [128, CC, D])
        wk2 = [st.sb(f"wk{p}", [128, CC, D], F32R) for p in range(2)]
        wv2 = [st.sb(f"wv{p}", [128, CC, D], F32R) for p in range(2)]
        c_raw = st.sb("c_raw", [128, CC, M])
        c2 = [st.sb(f"c{p}", [128, CC, M], F32R) for p in range(2)]
        k_hi = [st.sb(f"k_hi{k}", [128, M], F32R) for k in range(2)]
        k_lo = [st.sb(f"k_lo{k}", [128, M], F32R) for k in range(2)]
        keys = [st.sb(f"keys{c}", [128, 4, M], F32R) for c in range(CH)]
        queries = [st.sb(f"queries{c}", [128, 4, S], F32R) for c in range(CH)]
        vals = st.sb("vals", [128, KC, H, VW], BF16)
        k32 = [st.sb(f"k32_{k}", [128, NH]) for k in range(2)]
        v_rest = [st.sb(f"v_rest{k}", [128, 256]) for k in range(2)]
        mx = [st.sb(f"mx{k}", [112, 8, 2]) for k in range(2)]
        neg_max = [st.sb(f"neg_max{k}", [112, 8]) for k in range(2)]
        m_rows = [st.sb(f"m_rows{k}", [8, 112], F32R) for k in range(2)]
        p32 = [st.sb(f"p32_{k}", [128, KC * S]) for k in range(2)]
        p_hi = [st.sb(f"p_hi{k}", [128, KC * S], F16) for k in range(2)]
        p_lo = [st.sb(f"p_lo{k}", [128, KC * S], F16) for k in range(2)]
        o_sum = st.sb("o_sum", [112, 4, HD])
        o_rec = st.sb("o_rec", [112, 4])
        o_out = [st.sb(f"o_out{k}", [112, 2, 128]) for k in range(2)]
        mask_u8 = st.sb("mask_u8", [B, M], mybir.dt.uint8)
        some = st.sb("some", [B, 1])
        some_all = st.sb("some_all", [128, B])
        some_now = st.sb("some_now", [128, 1])
        mask_f = st.sb("mask_f", [B, M])

        fill = [st.ps(f"fill{k}") for k in range(3)]
        score = [st.ps(f"score{k}") for k in range(3)]
        out = [st.ps(f"out{k}") for k in range(2)]

        zero_set = st.sem("zero_set")
        some_in, some_set = st.sem("some_in"), st.sem("some_set")
        prep_in, mask_ready, mask_stored = st.sem("prep_in"), st.sem("mask_ready"), st.sem("mask_stored")
        wv_in, w_split, ones_set = st.sem("wv_in"), st.sem("w_split"), st.sem("ones_set")
        c_in, c_ready, c_step = st.sem("c_in"), st.sem("c_ready"), st.sem("c_step")
        keys_in = [st.sem(f"keys_in{c}") for c in range(CH)]
        q_in = [st.sem(f"q_in{c}") for c in range(CH)]
        m_in = [st.sem(f"m_in{c}") for c in range(CH)]
        filled, fill_free = st.sem("filled"), st.sem("fill_free")
        side_hi, side_free, k_low = st.sem("side_hi"), st.sem("side_free"), st.sem("k_low")
        v_mid, v_ready = st.sem("v_mid"), st.sem("v_ready")
        m_ready = st.sem("m_ready")
        score_full, exp_done = st.sem("score_full"), st.sem("exp_done")
        hi_done, lo_done, pv_done = st.sem("hi_done"), st.sem("lo_done"), st.sem("pv_done")
        norm_step, o_ready = st.sem("norm_step"), st.sem("o_ready")
        o_stored = [st.sem(f"o_stored{k}") for k in range(2)]

        SIDE0 = sum(p[0] in "KV" for p in first)
        SIDEB = sum(p[0] in "KV" for _, _, f in batch for p in f)
        V0 = sum(p[0] == "V" for p in first)
        VB = sum(p[0] == "V" for _, _, f in batch for p in f)

        class Place:

            def __init__(self, b=None):
                self.at = 0 if b is None else P0 + PB * b
                self.side = 0 if b is None else SIDE0 + SIDEB * b
                self.v = 0 if b is None else V0 + VB * b
                self.local = 1 if b is None else 0
                self.k = 0 if b is None else SIDE0 - V0 + (SIDEB - VB) * b
                self.start = b is not None
                self.rest = 0 if b is None else P0 - SIDE0 + (PB - SIDEB) * b
                self.freed = []
                self.some = 1 if b is None else b + 2

            def next(self, piece):
                self.at, self.local = self.at + 1, self.local + 1
                if piece[0] in "KV":
                    self.side = self.side + 1
                else:
                    self.rest = self.rest + 1
                if piece[0] == "K":
                    self.k = self.k + 1
                if piece[0] == "V":
                    self.v = self.v + 1
                self.freed.append((piece[0] in "KV", self.side if piece[0] in "KV" else self.rest))

            @property
            def bank(self):
                return self.local % 3

            def wait_free(self, t):
                if self.start and self.local == 0:
                    t.wait_ge(side_free, self.side)
                    t.wait_ge(fill_free, self.rest)
                elif len(self.freed) >= 3:
                    side, count = self.freed[-3]
                    t.wait_ge(side_free if side else fill_free, count)

        def steps(eng, step, before, between=None):
            place = Place()
            for piece in first:
                before(piece, place)
                place.next(piece)
            if between:
                between()

            def of_batch(b, last):
                place = Place(b)
                for c in range(CH):
                    for h in range(4):
                        step(b, c, h, place, last)
            with eng.Fori(0, B - 1) as b:
                of_batch(b, False)
            of_batch(B - 1, True)

        def heads_after(c, h):
            return (c + (h + 1) // 4) % CH, (h + 1) % 4, (4 * c + h + 1) // 16

        block = st.stack.enter_context(nc.Block())

        @block.sync
        def _(sp):
            def load_queries(c, b):
                for part, rows in ((0, 0), (0, 32), (1, 64)):
                    sp.dma_start(queries[c][rows:rows + 32, :, :].bitcast(F32),
                                 q_parts[part][c * 128:(c + 1) * 128, bass.ds(b * S, S)].rearrange("(h p) t -> p h t", p=32)).then_inc(q_in[c], 16)

            def load_mask(c, b):
                sp.dma_start(keys[c][96:97, :, :].bitcast(F32),
                             mask_row[bass.ds(b, 1), :].unsqueeze(1).broadcast_to([1, 4, M])).then_inc(keys_in[c], 16)

            def load_context(b):
                sp.dma_start(c_raw[:], ctx_t[bass.ds(b, 1), :, :].rearrange("a (c p) m -> p (a c) m", p=128)).then_inc(c_in, 16)

            def stack_keys(c, side, low):
                k = c % 2
                sp.wait_ge(side_hi, side)
                for h in range(4):
                    for rows in (0, 64):
                        sp.dma_start(keys[c][rows:rows + 32, h, :].bitcast(F32), k_hi[k][32 * h:32 * h + 32, :].bitcast(F32)).then_inc(keys_in[c], 16)
                sp.wait_ge(k_low, low)
                for h in range(4):
                    sp.dma_start(keys[c][32:64, h, :].bitcast(F32), k_lo[k][32 * h:32 * h + 32, :].bitcast(F32)).then_inc(keys_in[c], 16)

            sp.dma_start(mask_u8[:], mask).then_inc(prep_in, 16)
            load_context(0)
            sp.dma_start(w_raw[:], wk.rearrange("(c p) n -> p c n", p=128)).then_inc(prep_in, 16)
            sp.dma_start(ident[:], ident_d).then_inc(prep_in, 16)
            sp.wait_ge(mask_ready, 2)
            sp.dma_start(mask_row, mask_f[:]).then_inc(mask_stored, 16)
            sp.dma_start(some_row.unsqueeze(1), some[:]).then_inc(mask_stored, 16)
            sp.wait_ge(w_split, 2)
            sp.dma_start(w_raw[:], wv.rearrange("(c p) n -> p c n", p=128)).then_inc(wv_in, 16)
            sp.wait_ge(mask_stored, 32)
            sp.dma_start(some_all[:], some_row.partition_broadcast(128)).then_inc(some_in, 16)
            sp.wait_ge(ones_set, 9)
            for c in range(3):
                load_queries(c, 0)
                load_mask(c, 0)
            sp.sem_inc(o_stored[0], 16)
            sp.sem_inc(o_stored[1], 16)

            def before(piece, place):
                if piece[0] == "K" and piece[3] == 1:
                    stack_keys(piece[1], place.side + 1, place.k + 1)
                if piece[0] == "mT":
                    sp.wait_ge(fill_free, place.rest + 1)
                    sp.dma_start(queries[0][97:98, :, :].rearrange("p h (q t) -> p (h q) t", q=2).bitcast(F32), m_rows[0][:].bitcast(F32)).then_inc(m_in[0], 16)

            def step(b, c, h, place, last):
                if h == 0:
                    nc_, nb = (c + 3) % CH, (c + 3) // CH
                    if not (last and nb):
                        sp.wait_ge(score_full, 3 * (16 * b + 4 * c) + 3)
                        load_queries(nc_, b + nb)
                        load_mask(nc_, b + nb)
                    if c == 0 and not last:
                        sp.wait_ge(c_ready, b + 1)
                        load_context(b + 1)
                for piece in attention_fills(c, h, last):
                    place.next(piece)
                    if piece[0] == "K" and piece[3] == 1:
                        stack_keys(piece[1], place.side, place.k)
                    if piece[0] == "mT":
                        target, ahead = piece[1], piece[2]
                        sp.wait_ge(fill_free, place.rest)
                        sp.dma_start(queries[target][97:98, :, :].rearrange("p h (q t) -> p (h q) t", q=2).bitcast(F32),
                                     m_rows[target % 2][:].bitcast(F32)).then_inc(m_in[target], 16)
                if h == 0 and c > 0:
                    store(c - 1, b)
                if (c, h) == (3, 3):
                    store(c, b)

            def store(c, b):
                sp.wait_ge(o_ready, 8 * b + 2 * c + 4)
                sp.dma_start(attn[bass.ds(b * S, S), c * 128:(c + 1) * 128].rearrange("(q p) n -> p q n", p=112),
                             o_out[c % 2][:]).then_inc(o_stored[c % 2], 16)

            steps(sp, step, before)
            sp.wait_ge(o_stored[0], 16 + 32 * B)
            sp.wait_ge(o_stored[1], 16 + 32 * B)

        @block.gpsimd
        def _(pool):
            pool.memset(vals[:, :, :, 96:98], 1.0).then_inc(ones_set, 1)
            pool.memset(zero[:], 0.0).then_inc(zero_set, 1)
            pool.wait_ge(zero_set, 1)

            def split_context(b):
                pool.wait_ge(c_in, 16 * b + 16)
                pool.tensor_tensor(c2[0][:], c_raw[:], zero[:].unsqueeze(1).broadcast_to([128, CC, M]), ALU.add).then_inc(c_step, 1)
                pool.wait_ge(c_step, b + 1)
                pool.tensor_tensor(c2[1][:], c_raw[:], c2[0][:].bitcast(F32), ALU.subtract).then_inc(c_ready, 1)

            def value(piece, place):
                half, kc = piece[1], piece[3]
                rest = v_rest[kc % 2][:KP, :].rearrange("p (h d) -> p h d", d=HD)
                mid = vals[:KP, kc, 8 * half:8 * half + 8, 32:64]
                pool.wait_ge(side_free, place.side + 1)
                pool.tensor_tensor(rest, rest, vals[:KP, kc, 8 * half:8 * half + 8, 0:32], ALU.subtract).then_inc(v_mid, 1)
                pool.wait_ge(v_mid, 2 * place.v + 1)
                pool.tensor_tensor(mid, rest, zero[:KP, 0:256].rearrange("p (h d) -> p h d", d=HD), ALU.add).then_inc(v_mid, 1)
                pool.wait_ge(v_mid, 2 * place.v + 2)
                pool.tensor_tensor(vals[:KP, kc, 8 * half:8 * half + 8, 64:96], rest, mid, ALU.subtract).then_inc(v_ready, 1)

            def key_low(piece, place):
                c, half = piece[1], piece[3]
                pool.wait_ge(side_free, place.side + 1)
                pool.tensor_tensor(k_lo[c % 2][:, HALVES[half]], k32[half][:, 0:width(half)],
                                   k_hi[c % 2][:, HALVES[half]].bitcast(F32), ALU.subtract).then_inc(k_low, 1)

            def before(piece, place):
                if piece[0] == "V":
                    value(piece, place)
                if piece[0] == "K":
                    key_low(piece, place)

            def step(b, c, h, place, last):
                if (c, h) == (1, 0) and not last:
                    pool.wait_ge(filled, place.at)
                    split_context(b + 1)
                for piece in attention_fills(c, h, last):
                    before(piece, place)
                    place.next(piece)
            split_context(0)
            steps(pool, step, before)

        @block.scalar
        def _(a):
            def exps(s, k):
                a.wait_ge(lo_done, s + 1)
                for j in range(3):
                    a.wait_ge(score_full, 3 * s + j + 1)
                    a.activation(p32[k][:KP, j * 448:(j + 1) * 448], score[j][:KP, 0:448], ACT.Exp, scale=HD ** -0.5).then_inc(exp_done, 1)

            def high(s, k):
                a.wait_ge(pv_done, s + 1)
                a.wait_ge(exp_done, 3 * s + 6)
                a.activation(p_hi[k][:KP, :], p32[k][:KP, :], ACT.Copy).then_inc(hi_done, 1)

            def side(piece, place):
                if piece[0] == "K":
                    c, half = piece[1], piece[3]
                    a.wait_ge(filled, place.at + 1)
                    a.activation(k_hi[c % 2][:, HALVES[half]], fill[place.bank][:, 0:width(half)], ACT.Copy, scale=some_now[:, 0:1]).then_inc(side_hi, 1)
                    if not (isinstance(place.k, int) and place.k < 2):
                        a.wait_ge(k_low, place.k - 1)
                    a.activation(k32[half][:, 0:width(half)], fill[place.bank][:, 0:width(half)], ACT.Copy, scale=some_now[:, 0:1]).then_inc(side_free, 1)
                if piece[0] == "V":
                    half, kc = piece[1], piece[3]
                    a.wait_ge(filled, place.at + 1)
                    a.activation(vals[:KP, kc, 8 * half:8 * half + 8, 0:32],
                                 fill[place.bank][:KP, 0:256].rearrange("p (h d) -> p h d", d=HD), ACT.Copy).then_inc(side_hi, 1)
                    if not (isinstance(place.v, int) and place.v < 2):
                        a.wait_ge(v_ready, place.v - 1)
                    a.activation(v_rest[kc % 2][:KP, :], fill[place.bank][:KP, 0:256], ACT.Copy).then_inc(side_free, 1)

            def free_before(piece, place, b):
                if piece[0] == "K" and piece[3] == 0:
                    c, ahead = piece[1], piece[2]
                    a.wait_ge(some_set, b + ahead + 1)
                    if c >= 2:
                        a.wait_ge(keys_in[c - 2], 208 * (b + ahead + 1))
                    elif not (isinstance(b, int) and b + ahead == 0):
                        a.wait_ge(keys_in[c + 2], 208 * (b + ahead))
                if piece[0] == "V" and b is not None:
                    half = piece[1]
                    if half == 0:
                        a.wait_ge(pv_done, 16 * b + 8 + 2)
                    elif not (isinstance(b, int) and b == 0):
                        a.wait_ge(pv_done, 16 * b + 2)

            def before(piece, place):
                if piece[0] == "K":
                    free_before(piece, place, 0)
                side(piece, place)

            def step(b, c, h, place, last):
                if not (last and (c, h) == (3, 3)):
                    exps(16 * b + 4 * c + h + 1, (h + 1) % 2)
                pieces = attention_fills(c, h, last)
                for i in range(len(pieces) + 1):
                    if i == min(3, len(pieces)) and not (last and (c, h) == (3, 3)):
                        high(16 * b + 4 * c + h + 1, (h + 1) % 2)
                    if i < len(pieces):
                        free_before(pieces[i], place, b)
                        side(pieces[i], place)
                        place.next(pieces[i])

            def begin():
                exps(0, 0)
                high(0, 0)
            a.sem_inc(exp_done, 3)
            steps(a, step, before, begin)

        @block.vector
        def _(v):
            v.sem_inc(lo_done, 2)
            v.sem_inc(o_ready, 2)
            v.wait_ge(prep_in, 48)
            v.tensor_scalar(mask_f[:], mask_u8[:], 1.0, -NEG, ALU.subtract, ALU.mult).then_inc(mask_ready, 1)
            v.tensor_reduce(some[:], mask_u8[:], AX.X, ALU.max).then_inc(mask_ready, 1)
            split_weights(v, w_raw[:], wk2[0][:], wk2[1][:], w_split, 0)
            for c in range(CH):
                v.memset(keys[c][96:128, :, :].bitcast(F32), 1.0).then_inc(ones_set, 1)
                v.memset(queries[c][96:128, :, :].bitcast(F32), 1.0).then_inc(ones_set, 1)
            v.wait_ge(wv_in, 16)
            split_weights(v, w_raw[:], wv2[0][:], wv2[1][:], w_split, 2)

            def take_some(b):
                v.tensor_copy(some_now[:], some_all[:, bass.ds(b, 1)]).then_inc(some_set, 1)

            v.wait_ge(some_in, 16)
            take_some(0)
            v.wait_ge(some_set, 1)

            def piece_of(piece, place):
                kind, bank = piece[0], fill[place.bank]
                if kind in "KV":
                    return
                v.wait_ge(filled, place.at + 1)
                if kind == "max":
                    c, h, qt, half = piece[1], *piece[3:]
                    v.tensor_reduce(mx[c % 2][:, 2 * h + qt, half:half + 1], bank[:112, 0:NH], AX.X, ALU.max).then_inc(fill_free, 1)
                else:
                    v.tensor_copy(m_rows[piece[1] % 2][:], bank[:8, 0:112]).then_inc(fill_free, 1)

            def close_max(piece, place):
                if piece[0] == "max" and piece[3:] == (3, 1, 1):
                    k = piece[1] % 2
                    v.wait_ge(fill_free, place.rest + 1)
                    v.tensor_reduce(neg_max[k][:], mx[k][:], AX.X, ALU.max, negate=True).then_inc(m_ready, 1)

            def low(s, k):
                v.wait_ge(hi_done, s + 1)
                v.wait_ge(pv_done, s + 1)
                v.tensor_tensor(p_lo[k][:KP, :], p32[k][:KP, :], p_hi[k][:KP, :], ALU.subtract).then_inc(lo_done, 1)

            def normalise(n, pair, c, b):
                v.wait_ge(o_ready, n + 2)
                v.wait_ge(pv_done, 2 * n + 4)
                bank = out[pair][:112, 0:4 * 97].rearrange("p (x w) -> p x w", w=97)
                v.tensor_reduce(o_sum[:], bank[:, :, 0:96].rearrange("p x (s d) -> p x d s", s=3), AX.X, ALU.add).then_inc(norm_step, 1)
                v.reciprocal(o_rec[:], bank[:, :, 96]).then_inc(norm_step, 1)
                if pair == 0:
                    v.wait_ge(o_stored[c % 2], 32 * b + 16 * (c // 2) + 16)
                v.wait_ge(norm_step, 2 * n + 2)
                v.tensor_tensor(o_out[c % 2][:, :, 64 * pair:64 * pair + 64].rearrange("p q (h d) -> p q h d", d=HD),
                                o_sum[:].rearrange("p (q h) d -> p q h d", q=2),
                                o_rec[:].rearrange("p (q h) -> p q h", q=2).unsqueeze(3).broadcast_to([112, 2, 2, HD]),
                                ALU.mult).then_inc(o_ready, 1)

            def before(piece, place):
                piece_of(piece, place)
                close_max(piece, place)

            def step(b, c, h, place, last):
                if h in (0, 2) and (c, h) != (0, 0):
                    pc, pair = (c - 1, 1) if h == 0 else (c, 0)
                    normalise(8 * b + 2 * pc + pair, pair, pc, b)
                if (c, h) == (1, 0) and not last:
                    v.wait_ge(side_free, place.side)
                    take_some(b + 1)
                for piece in attention_fills(c, h, last):
                    piece_of(piece, place)
                    close_max(piece, place)
                    place.next(piece)
                if not (last and (c, h) == (3, 3)):
                    low(16 * b + 4 * c + h + 1, (h + 1) % 2)
                if (c, h) == (3, 3):
                    normalise(8 * b + 7, 1, 3, b)

            steps(v, step, before, lambda: low(0, 0))

        @block.tensor
        def _(t):
            def product(piece, place, b):
                kind, bank = piece[0], fill[place.bank]
                c, ahead = piece[1], piece[2]
                place.wait_free(t)
                if kind == "K":
                    half = piece[3]
                    t.wait_ge(c_ready, b + ahead + 1)
                    for n, (pw, px) in enumerate(PASSES):
                        for d in range(CC):
                            mm = t.matmul(bank[:, 0:width(half)], wk2[pw][:, d, c * 128:(c + 1) * 128], c2[px][:, d, HALVES[half]],
                                          start=(n == 0 and d == 0), stop=(n == 2 and d == CC - 1))
                elif kind == "V":
                    half, kc = piece[1], piece[3]
                    t.wait_ge(c_ready, b + ahead + 1)
                    for n, (pw, px) in enumerate(PASSES):
                        for d in range(CC):
                            mm = t.matmul(bank[:KP, 0:256], c2[pw][:, d, kc * KP:(kc + 1) * KP], wv2[px][:, d, 256 * half:256 * half + 256],
                                          start=(n == 0 and d == 0), stop=(n == 2 and d == CC - 1))
                elif kind == "max":
                    h, qt, half = piece[3:]
                    if (h, qt, half) == (0, 0, 0):
                        t.wait_ge(keys_in[c], 208 * (b + ahead + 1))
                        t.wait_ge(q_in[c], 48 * (b + ahead + 1))
                    mm = t.matmul(bank[:112, 0:NH], queries[c][0:97, h, qt * 112:(qt + 1) * 112], keys[c][0:97, h, COVER[half]],
                                  start=True, stop=True)
                else:
                    t.wait_ge(m_ready, 4 * (b + ahead) + c + 1)
                    mm = t.transpose(bank[:8, 0:112], neg_max[c % 2][:], ident[:112, :112])
                mm.then_inc(filled, 1)

            def scores(s, b, c, h, banks=(0, 1, 2)):
                if h == 0 and 0 in banks:
                    t.wait_ge(m_in[c], 16 * (b + 1))
                for j in banks:
                    t.wait_ge(exp_done, 3 * s + j + 1)
                    for i in range(2):
                        kc = 2 * j + i
                        mm = t.matmul(score[j][:KP, i * S:(i + 1) * S], keys[c][0:98, h, kc * KP:(kc + 1) * KP], queries[c][0:98, h, :],
                                      start=True, stop=True)
                    mm.then_inc(score_full, 1)

            def weigh(s, b, c, h, qt):
                if qt == 0:
                    t.wait_ge(lo_done, s + 3)
                if h % 2 == 0 and qt == 0:
                    t.wait_ge(o_ready, 8 * b + 2 * c + h // 2 + 1)
                if h == 0 and c in (0, 2) and qt == 0:
                    t.wait_ge(v_ready, V0 + VB * b + (0 if c == 0 else KC))
                off = (2 * qt + h % 2) * 97
                for kc in range(KC):
                    for n, part in enumerate((p_hi, p_lo)):
                        mm = t.matmul(out[h // 2][:112, off:off + 97], part[h % 2][:KP, kc * S + qt * 112:kc * S + qt * 112 + 112],
                                      vals[:KP, kc, 4 * c + h, 0:97], start=(kc == 0 and n == 0), stop=(kc == KC - 1 and n == 1))
                if qt == 1:
                    mm.then_inc(pv_done, 1)

            def step(b, c, h, place, last):
                s = 16 * b + 4 * c + h
                nc_, nh, ahead = heads_after(c, h)
                pieces = attention_fills(c, h, last)

                def some_pieces(n):
                    for piece in pieces[:n]:
                        product(piece, place, b)
                        place.next(piece)
                    del pieces[:n]
                if not (last and ahead):
                    scores(s + 1, b + ahead, nc_, nh)
                some_pieces(3)
                weigh(s, b, c, h, 0)
                some_pieces(3)
                weigh(s, b, c, h, 1)
                some_pieces(len(pieces))

            t.sem_inc(pv_done, 2)
            t.wait_ge(prep_in, 48)
            t.wait_ge(w_split, 2)

            def before(piece, place):
                if piece[0] == "V":
                    t.wait_ge(w_split, 4)
                if piece[0] == "max":
                    t.wait_ge(ones_set, 9)
                product(piece, place, 0)
            steps(t, step, before, lambda: scores(0, 0, 0, 0))


def load_weight(sp, raw, w, sem):
    sp.dma_start(raw[:], w.rearrange("(c p) n -> p c n", p=128)).then_inc(sem, 16)


def is_first(g):
    return isinstance(g, int) and g == 0


def gates(nc, sems, g_xattn, g_ffn, glob):
    with Stage(nc, sems, "g") as st:
        raw = st.sb("raw", [128, 4])
        g_in, g_done, const_set = st.sem("in"), st.sem("done"), st.sem("const_set")
        block = st.stack.enter_context(nc.Block())

        @block.vector
        def _(v):
            v.memset(glob[:, ONE:ONE + 1], 1.0).then_inc(const_set, 1)
            v.memset(glob[:, RND:RND + 1], ROUND).then_inc(const_set, 1)
            v.memset(glob[:, NRND:NRND + 1], -ROUND).then_inc(const_set, 1)
            v.wait_ge(const_set, 3)

        @block.sync
        def _(sp):
            sp.dma_start(raw[:, 0:2], g_xattn.partition_broadcast(128)).then_inc(g_in, 16)
            sp.dma_start(raw[:, 2:4], g_ffn.partition_broadcast(128)).then_inc(g_in, 16)

        @block.scalar
        def _(a):
            a.wait_ge(g_in, 32)
            a.activation(glob[:, 0:4], raw[:], ACT.Tanh).then_inc(g_done, 1)
            a.wait_ge(g_done, 1)


def project_out(nc, sems, src, w_d, ident_d, glob, x, x_out, xn_out):
    with Stage(nc, sems, "o0") as st:
        ident = st.sb("ident", [128, 128])
        w_raw = st.sb("w_raw", [128, DC, D])
        w = [st.sb("w_hi", [128, DC, D], F32R), st.sb("w_lo", [128, DC, D], F32R)]
        at = [st.sb(f"a{k}", [128, 4, D]) for k in range(2)]
        xt = [st.sb(f"x{k}", [128, 4, D]) for k in range(2)]
        xo = [st.sb(f"xo{k}", [128, 4, D]) for k in range(2)]
        xn = [st.sb(f"xn{k}", [128, 4, D]) for k in range(2)]
        peak = st.sb("peak", [128, 1 + G5 * 4])
        out = st.ps("out", (128, 4, 512))
        a_in = [st.sem(f"a_in{k}") for k in range(2)]
        x_in = [st.sem(f"x_in{k}") for k in range(2)]
        stored = [st.sem(f"stored{k}") for k in range(2)]
        ident_in, w_in, w_split, mm_done = st.sem("ident_in"), st.sem("w_in"), st.sem("w_split"), st.sem("mm_done")
        a_ready, xo_ready, xn_ready, peaks, top = st.sem("a_ready"), st.sem("xo_ready"), st.sem("xn_ready"), st.sem("peaks"), st.sem("top")
        norm, turn = Norm(st, 128), Turn(st, 128, DC, None)
        TURNS = ((), (), (0, 1, 2, 3), ())
        block = st.stack.enter_context(nc.Block())

        def tiles(t, g):
            return t[bass.ds(g * 512, 512), :].rearrange("(j p) c -> p j c", p=128)

        @block.sync
        def _(sp):
            def load(g, k, u):
                if not (isinstance(g, int) and g < 2):
                    sp.wait_ge(turn.turned, 4 * g - 4)
                sp.dma_start(at[k][:], tiles(src, g)).then_inc(a_in[k], 16)
                if not (isinstance(g, int) and g < 2):
                    sp.wait_ge(xo_ready, 4 * g - 4)
                sp.dma_start(xt[k][:], tiles(x, g)).then_inc(x_in[k], 16)

            def store(g, k, u):
                sp.wait_ge(xo_ready, 4 * g + 4)
                sp.dma_start(tiles(x_out, g), xo[k][:]).then_inc(stored[k], 16)
                sp.wait_ge(xn_ready, 4 * g + 4)
                sp.dma_start(tiles(xn_out, g), xn[k][:]).then_inc(stored[k], 16)

            def step(g, k, u):
                store(g, k, u)
                load(g + 2, k, u + 1)
            load(0, 0, 0)
            sp.dma_start(ident[:], ident_d).then_inc(ident_in, 16)
            load_weight(sp, w_raw, w_d, w_in)
            load(1, 1, 0)
            sp.sem_inc(stored[0], 32)
            sp.sem_inc(stored[1], 32)
            pairs(sp, 0, G5 - 2, step)
            store(G5 - 2, 1, 2)
            store(G5 - 1, 0, 3)
            sp.wait_ge(stored[0], 32 + 32 * 4)
            sp.wait_ge(stored[1], 32 + 32 * 3)

        @block.scalar
        def _(a):
            def step(g, k, u, more=True):
                if more:
                    turn.scalar(a, g + 1, 1 - k, None if is_first(g) else (mm_done, 4 * g))
                norm.scalar(a, g)
            turn.scalar(a, 0, 0)
            step(0, 0, 0)
            pairs(a, 1, G5 - 1, step)
            step(G5 - 1, 0, 3, False)

        @block.vector
        def _(v):
            def step(g, k, u, more=True):
                v.wait_ge(x_in[k], 16 * u + 16)
                v.wait_ge(stored[k], 32 * u + 32)
                for j in range(4):
                    if more:
                        turn.vector(v, g + 1, 1 - k, TURNS[j])
                    v.wait_ge(mm_done, 4 * g + j + 1)
                    v.scalar_tensor_tensor(xo[k][:, j, :], out[:, j, :], glob[:, 0:1], xt[k][:, j, :], ALU.mult, ALU.add).then_inc(xo_ready, 1)
                v.wait_ge(xo_ready, 4 * g + 4)
                norm.vector(v, g, xo[k], xn[k], xn_ready)
                v.wait_ge(xn_ready, 4 * g + 4)
                v.tensor_reduce(peak[:, bass.ds(g, 1)], xn[k][:], AX.XY, ALU.max, apply_absolute_value=True).then_inc(peaks, 1)
            turn.vector(v, 0, 0)
            v.wait_ge(w_in, 16)
            split_weights(v, w_raw[:], w[0][:], w[1][:], w_split, 0)
            step(0, 0, 0)
            pairs(v, 1, G5 - 1, step)
            step(G5 - 1, 0, 3, False)
            v.wait_ge(peaks, G5)
            v.tensor_reduce(glob[:, 4:5], peak[:, 0:G5], AX.X, ALU.max).then_inc(top, 1)
            v.wait_ge(top, 1)

        @block.tensor
        def _(t):
            def step(g, k, u, more=True):
                x2 = (turn.hi[k], turn.lo[k])
                for j in range(4):
                    if j == 0:
                        t.wait_ge(turn.lo_ready, 4 * g + 4)
                    if not is_first(g):
                        t.wait_ge(xo_ready, 4 * g - 3 + j)
                    for n, (px, pw) in enumerate(PASSES):
                        for d in range(DC):
                            mm = t.matmul(out[:, j, :], x2[px][:, d, j * 128:(j + 1) * 128], w[pw][:, d, :],
                                          start=(n == 0 and d == 0), stop=(n == 2 and d == DC - 1))
                    mm.then_inc(mm_done, 1)
                    if TURNS[j] and more:
                        if 0 in TURNS[j]:
                            t.wait_ge(a_in[1 - k], 16 * (u + k) + 16)
                        turn.tensor(t, g + 1, at[1 - k], ident, TURNS[j])
            t.wait_ge(ident_in, 16)
            t.wait_ge(a_in[0], 16)
            turn.tensor(t, 0, at[0], ident)
            t.wait_ge(w_split, 2)
            step(0, 0, 0)
            pairs(t, 1, G5 - 1, step)
            step(G5 - 1, 0, 3, False)



(GX0, GX1, GF0, GF1, PEAK_X, SX, FX, PEAK_G, PEAK_U, SG, FG, SU, FU, PEAK_T, S2, F2, PEAK_V, SO, FO, GSO, ONE, RND, NRND) = range(23)
NGLOB = 24
WBLK = 32
QUADS = I0 // 512
UNITS = G5 * QUADS
UW, HUNITS = 1024, 2 * UNITS


def scales(nc, sems, glob, name, jobs):
    with Stage(nc, sems, name) as st:
        top = st.sb("top", [128, len(jobs)])
        unit, raw, rec = (st.sb(n, [128, len(jobs)]) for n in ("unit", "raw", "rec"))
        reduced, step = st.sem("reduced"), st.sem("step")
        block = st.stack.enter_context(nc.Block())

        @block.gpsimd
        def _(pool):
            for i, job in enumerate(jobs):
                pool.partition_all_reduce(top[:, i:i + 1], glob[:, job[0]:job[0] + 1], 128, bass.bass_isa.ReduceOp.max).then_inc(reduced, 1)

        @block.vector
        def _(v):
            n = 0
            for i, (_, a, b, const, s, f) in enumerate(jobs):
                def col(c):
                    return glob[:, c:c + 1]
                v.tensor_scalar(unit[:, i:i + 1], col(a), col(b), const, ALU.mult, ALU.mult).then_inc(step, 1)
                v.wait_ge(step, n + 1)
                v.wait_ge(reduced, i + 1)
                v.tensor_scalar(raw[:, i:i + 1], top[:, i:i + 1], unit[:, i:i + 1], 1.0 / QMAX, ALU.mult, ALU.mult).then_inc(step, 1)
                v.wait_ge(step, n + 2)
                v.tensor_scalar(col(s), raw[:, i:i + 1], 1e-12, None, ALU.max).then_inc(step, 1)
                v.wait_ge(step, n + 3)
                v.reciprocal(rec[:, i:i + 1], col(s)).then_inc(step, 1)
                v.wait_ge(step, n + 4)
                v.tensor_tensor(col(f), rec[:, i:i + 1], unit[:, i:i + 1], ALU.mult).then_inc(step, 1)
                v.wait_ge(step, n + 5)
                n += 5


def quantise_weights(nc, sems, glob, tiles, ident_d, w_parts):
    G, NB = len(tiles), 4 * 512 // WBLK
    with Stage(nc, sems, "qw") as st:
        ident = st.sb("ident", [128, 128])
        wt = [st.sb(f"w{k}", [128, 4, 512]) for k in range(4)]
        top, rec = st.sb("top", [128, NB]), st.sb("rec", [128, NB])
        s = [st.sb(f"s{k}", [128, NB]) for k in range(4)]
        ident_in, chain, divided, up, rounded, deq = (st.sem(n) for n in ("ident_in", "chain", "divided", "up", "rounded", "deq"))
        w_in = [st.sem(f"w_in{k}") for k in range(4)]
        w_out = [st.sem(f"w_out{k}") for k in range(2)]
        turn = Turn(st, 128, 4, deq, 1)
        block = st.stack.enter_context(nc.Block())

        def blocks(g):
            return wt[g % 4][:].rearrange("p j (n e) -> p (j n) e", e=WBLK)

        def spread(x):
            return x[:].unsqueeze(2).broadcast_to([128, NB, WBLK])

        @block.sync
        def _(sp):
            def load(g):
                if g >= 4:
                    sp.wait_ge(turn.turned, 4 * (g - 3))
                sp.dma_start(wt[g % 4][:], tiles[g]).then_inc(w_in[g % 4], 16)
            load(0)
            sp.dma_start(ident[:], ident_d).then_inc(ident_in, 16)
            load(1)
            load(2)
            load(3)
            for g in range(G):
                sp.wait_ge(turn.hi_ready, 4 * g + 4)
                sp.dma_start(w_parts[0][g], turn.hi[g % 2][:].bitcast(F32)).then_inc(w_out[g % 2], 16)
                sp.wait_ge(turn.lo_ready, 4 * g + 4)
                sp.dma_start(w_parts[1][g], turn.lo[g % 2][:].bitcast(F32)).then_inc(w_out[g % 2], 16)
                if g + 4 < G:
                    load(g + 4)
            sp.wait_ge(w_out[0], 32 * ((G + 1) // 2))
            sp.wait_ge(w_out[1], 32 * (G // 2))

        @block.vector
        def _(v):
            def divide(g):
                v.wait_ge(w_in[g % 4], 16 * (g // 4) + 16)
                v.tensor_reduce(top[:], blocks(g), AX.X, ALU.max, apply_absolute_value=True).then_inc(chain, 1)
                if g >= 4:
                    v.wait_ge(deq, g - 3)
                v.wait_ge(chain, 3 * g + 1)
                v.tensor_scalar(s[g % 4][:], top[:], 1.0 / 7.0, 1e-12, ALU.mult, ALU.max).then_inc(chain, 1)
                v.wait_ge(chain, 3 * g + 2)
                v.reciprocal(rec[:], s[g % 4][:]).then_inc(chain, 1)
                v.wait_ge(chain, 3 * g + 3)
                v.tensor_tensor(blocks(g), blocks(g), spread(rec), ALU.mult).then_inc(divided, 1)
            divide(0)
            v.wait_ge(divided, 1)
            divide(1)
            for g in range(G):
                if g + 2 < G:
                    v.wait_ge(divided, g + 2)
                    divide(g + 2)
                turn.vector(v, g, g % 2)

        @block.scalar
        def _(a):
            def to_integers(g):
                a.wait_ge(divided, g + 1)
                a.activation(wt[g % 4][:], wt[g % 4][:], ACT.Identity, bias=glob[:, RND:RND + 1]).then_inc(up, 1)
                a.wait_ge(up, g + 1)
                a.activation(wt[g % 4][:], wt[g % 4][:], ACT.Identity, bias=glob[:, NRND:NRND + 1]).then_inc(rounded, 1)
            to_integers(0)
            to_integers(1)
            for g in range(G):
                turn.scalar(a, g, g % 2, (w_out[g % 2], 32 * (g // 2)) if g >= 2 else None)
                if g + 2 < G:
                    to_integers(g + 2)

        @block.gpsimd
        def _(pool):
            for g in range(G):
                pool.wait_ge(rounded, g + 1)
                pool.tensor_tensor(blocks(g), blocks(g), spread(s[g % 4]), ALU.mult).then_inc(deq, 1)

        @block.tensor
        def _(t):
            t.wait_ge(ident_in, 16)
            for g in range(G):
                turn.tensor(t, g, wt[g % 4], ident)


def up_gate(nc, sems, xn, gate_w, up_w, ident_d, glob, gate_d, up_d):
    with Stage(nc, sems, "ug") as st:
        ident = st.sb("ident", [128, 128])
        w = [[st.sb(f"w{s}{p}", [128, DC, I0], F32R) for p in range(2)] for s in range(2)]
        xt = [st.sb(f"x{k}", [128, 4, D]) for k in range(2)]
        h = [st.sb(f"h{k}", [128, 4, 512]) for k in range(2)]
        now, best = st.sb("now", [128, 2 * QUADS]), st.sb("best", [128, 2 * QUADS])
        out = st.ps("out", (128, 4, 512))
        x_in = [st.sem(f"x_in{k}") for k in range(2)]
        stored = [st.sem(f"stored{k}") for k in range(2)]
        ident_in, r_ready, xq_ready = st.sem("ident_in"), st.sem("r_ready"), st.sem("xq_ready")
        w_in = [st.sem(f"w_in{i}") for i in range(4)]
        mm_done, copied, peaked, topped = st.sem("mm_done"), st.sem("copied"), st.sem("peaked"), st.sem("topped")
        turn = Turn(st, 128, DC, xq_ready, 1)
        CHUNKS, Q2 = 8 * QUADS, 2 * QUADS
        TURN_AT = (8, 10, 12, 14)
        block = st.stack.enter_context(nc.Block())

        @block.sync
        def _(sp):
            def load(g, k, u):
                if not (isinstance(g, int) and g < 2):
                    sp.wait_ge(turn.turned, 4 * g - 4)
                sp.dma_start(xt[k][:], xn[bass.ds(g * 512, 512), :].rearrange("(j p) c -> p j c", p=128)).then_inc(x_in[k], 16)

            def store(g, k, u):
                for q in range(Q2):
                    dst = (gate_d, up_d)[q // QUADS]
                    sp.wait_ge(copied, CHUNKS * g + 4 * q + 4)
                    sp.dma_start(unit_view(dst, QUADS * g + q % QUADS), h[q % 2][:].rearrange("p (a j) n -> p a (j n)", a=2)).then_inc(stored[q % 2], 16)

            def step(g, k, u):
                load(g + 2, k, u + 1)
                store(g, k, u)
            load(0, 0, 0)
            sp.dma_start(ident[:], ident_d).then_inc(ident_in, 16)
            for s, parts in enumerate((gate_w, up_w)):
                for half in range(2):
                    cols = slice(half * I0 // 2, (half + 1) * I0 // 2)
                    for p in range(2):
                        sp.dma_start(w[s][p][:, :, cols].bitcast(F32), parts[p][:, cols].rearrange("(c p) n -> p c n", p=128)).then_inc(w_in[2 * s + half], 16)
                if s == 0:
                    load(1, 1, 0)
            sp.sem_inc(stored[0], 16)
            sp.sem_inc(stored[1], 16)
            pairs(sp, 0, G5 - 2, step)
            store(G5 - 2, 1, 2)
            store(G5 - 1, 0, 3)
            for k in range(2):
                sp.wait_ge(stored[k], 16 + 16 * QUADS * G5)

        @block.scalar
        def _(a):
            def step(g, k, u, more=True):
                for c in range(CHUNKS):
                    if c in TURN_AT and more:
                        turn.scalar(a, g + 1, 1 - k, None if is_first(g) else (mm_done, CHUNKS * g), (TURN_AT.index(c),))
                    if c % 4 == 0:
                        q = c // 4
                        a.wait_ge(stored[q % 2], 16 * QUADS * g + 16 * (q // 2) + 16)
                        a.wait_ge(peaked, Q2 * g + q + 1)
                    a.wait_ge(mm_done, CHUNKS * g + c + 1)
                    a.activation(h[(c // 4) % 2][:, c % 4, :], out[:, c % 4, :], ACT.Copy).then_inc(copied, 1)
            turn.scalar(a, 0, 0)
            step(0, 0, 0)
            pairs(a, 1, G5 - 1, step)
            step(G5 - 1, 0, 3, False)

        @block.vector
        def _(v):
            def front(g, k, u):
                v.wait_ge(x_in[k], 16 * u + 16)
                v.tensor_scalar(xt[k][:], xt[k][:], glob[:, FX:FX + 1], ROUND, ALU.mult, ALU.add).then_inc(r_ready, 1)
                v.wait_ge(r_ready, g + 1)
                v.tensor_scalar(xt[k][:], xt[k][:], ROUND, None, ALU.subtract).then_inc(xq_ready, 1)

            def step(g, k, u, more=True):
                if more:
                    front(g + 1, 1 - k, u + k)
                v.wait_ge(topped, g + 1)
                for q in range(Q2):
                    if more:
                        turn.vector(v, g + 1, 1 - k, [d for d in range(DC) if TURN_AT[d] // 4 == q])
                    v.wait_ge(copied, CHUNKS * g + 4 * q + 4)
                    v.tensor_reduce(now[:, q:q + 1], h[q % 2][:], AX.XY, ALU.max, apply_absolute_value=True).then_inc(peaked, 1)
                v.wait_ge(peaked, Q2 * (g + 1) + 2)
                v.tensor_tensor(best[:], best[:], now[:], ALU.max).then_inc(topped, 1)
            v.memset(best[:], 0.0).then_inc(topped, 1)
            v.sem_inc(peaked, 2)
            front(0, 0, 0)
            turn.vector(v, 0, 0)
            step(0, 0, 0)
            pairs(v, 1, G5 - 1, step)
            step(G5 - 1, 0, 3, False)
            v.wait_ge(topped, G5 + 1)
            for s, c in enumerate((PEAK_G, PEAK_U)):
                v.tensor_reduce(glob[:, c:c + 1], best[:, s * QUADS:(s + 1) * QUADS], AX.X, ALU.max).then_inc(topped, 1)
            v.wait_ge(topped, G5 + 3)

        @block.tensor
        def _(t):
            def step(g, k, u, more=True):
                x2 = (turn.hi[k], turn.lo[k])
                for c in range(CHUNKS):
                    if c in TURN_AT and more:
                        turn.tensor(t, g + 1, xt[1 - k], ident, (TURN_AT.index(c),))
                    if c == 0:
                        t.wait_ge(turn.lo_ready, 4 * g + 4)
                    if not (is_first(g) and c < 4):
                        t.wait_ge(copied, CHUNKS * g + c - 3)
                    if is_first(g) and c % 6 == 0:
                        t.wait_ge(w_in[c // 6], 32)
                    s, f = divmod(c, 4 * QUADS)
                    for n, (pw, px) in enumerate(PASSES):
                        for d in range(DC):
                            mm = t.matmul(out[:, c % 4, :], w[s][pw][:, d, f * 128:(f + 1) * 128], x2[px][:, d, :],
                                          start=(n == 0 and d == 0), stop=(n == 2 and d == DC - 1))
                    mm.then_inc(mm_done, 1)
            t.wait_ge(ident_in, 16)
            turn.tensor(t, 0, xt[0], ident)
            step(0, 0, 0)
            pairs(t, 1, G5 - 1, step)
            step(G5 - 1, 0, 3, False)


def unit_view(t, n):
    return t[bass.ds(2 * n, 2), :, :].rearrange("a p n -> p a n")


def half_view(t, n):
    return t[bass.ds(n, 1), :, :].rearrange("a p n -> (a p) n")


def gate_sigmoid(nc, sems, gate_d, gated, glob):
    N = UW
    with Stage(nc, sems, "gs") as st:
        gt = [st.sb(f"g{k}", [128, N]) for k in range(6)]
        sg = [st.sb(f"s{k}", [128, N]) for k in range(3)]
        now, best = st.sb("now", [128, 1]), st.sb("best", [128, 1])
        g_in = [st.sem(f"g_in{k}") for k in range(6)]
        r_ready, gq_ready, sig_ready, sr_ready, sq_ready = (st.sem(n) for n in ("r_ready", "gq_ready", "sig_ready", "sr_ready", "sq_ready"))
        t_ready, peaked, topped = st.sem("t_ready"), st.sem("peaked"), st.sem("topped")
        block = st.stack.enter_context(nc.Block())

        @block.sync
        def _(sp):
            def load(n, k, u):
                if not (isinstance(n, int) and n < 6):
                    sp.wait_ge(t_ready, n - 5)
                sp.dma_start(gt[k][:], half_view(gate_d, n)).then_inc(g_in[k], 16)
            for n in range(6):
                load(n, n, 0)
            sixes(sp, 6, HUNITS, load)

        @block.scalar
        def _(a):
            def first(n, k, u):
                a.wait_ge(g_in[k], 16 * u + 16)
                a.activation(gt[k][:], gt[k][:], ACT.Identity, bias=glob[:, RND:RND + 1], scale=glob[:, FG:FG + 1]).then_inc(r_ready, 1)

            def step(n, k, u, more=True):
                a.wait_ge(gq_ready, n + 1)
                if not (isinstance(n, int) and n < 3):
                    a.wait_ge(t_ready, n - 2)
                a.activation(sg[k % 3][:], gt[k][:], ACT.Sigmoid, scale=glob[:, SG:SG + 1]).then_inc(sig_ready, 1)
                if more:
                    first(n + 2, (k + 2) % 6, u + (k + 2) // 6)
                a.wait_ge(sig_ready, n + 1)
                a.activation(sg[k % 3][:], sg[k % 3][:], ACT.Identity, bias=glob[:, RND:RND + 1], scale=65536.0).then_inc(sr_ready, 1)
            first(0, 0, 0)
            first(1, 1, 0)
            for n in range(6):
                step(n, n, 0)
            sixes(a, 6, HUNITS - 2, step)
            for n in (HUNITS - 2, HUNITS - 1):
                step(n, n % 6, 0, False)

        @block.gpsimd
        def _(pool):
            def step(n, k, u):
                pool.wait_ge(r_ready, n + 1)
                pool.tensor_tensor(gt[k][:], gt[k][:], glob[:, NRND:NRND + 1].broadcast_to([128, N]), ALU.add).then_inc(gq_ready, 1)
            sixes(pool, 0, HUNITS, step)

        @block.vector
        def _(v):
            def peak(n):
                v.tensor_reduce(now[:], unit(n), AX.X, ALU.max, apply_absolute_value=True).then_inc(peaked, 1)

            def unit(n):
                return gated[:, bass.ds(n, 1), :].rearrange("p a n -> p (a n)")

            def step(n, k, u):
                v.wait_ge(sr_ready, n + 1)
                if not is_first(n):
                    v.wait_ge(t_ready, n)
                    v.wait_ge(topped, n)
                v.tensor_scalar(sg[k % 3][:], sg[k % 3][:], ROUND, 65535.0, ALU.subtract, ALU.min).then_inc(sq_ready, 1)
                if not is_first(n):
                    peak(n - 1)
                v.wait_ge(sq_ready, n + 1)
                v.tensor_tensor(unit(n), gt[k][:], sg[k % 3][:], ALU.mult).then_inc(t_ready, 1)
                if not is_first(n):
                    v.wait_ge(peaked, n)
                    v.tensor_tensor(best[:], best[:], now[:], ALU.max).then_inc(topped, 1)
            v.memset(best[:], 0.0).then_inc(topped, 1)
            step(0, 0, 0)
            sixes(v, 1, HUNITS, step)
            v.wait_ge(t_ready, HUNITS)
            v.wait_ge(topped, HUNITS)
            peak(HUNITS - 1)
            v.wait_ge(peaked, HUNITS)
            v.tensor_tensor(glob[:, PEAK_T:PEAK_T + 1], best[:], now[:], ALU.max).then_inc(topped, 1)
            v.wait_ge(topped, HUNITS + 1)


def gate_times_up(nc, sems, gated, up_d, v_d, glob):
    N = UW
    with Stage(nc, sems, "gu") as st:
        ut = [st.sb(f"u{k}", [128, N]) for k in range(6)]
        vt = [st.sb(f"v{k}", [128, N]) for k in range(3)]
        now, best = st.sb("now", [128, 1]), st.sb("best", [128, 1])
        u_in = [st.sem(f"u_in{k}") for k in range(6)]
        stored = [st.sem(f"stored{k}") for k in range(3)]
        r_ready, t_ready, uq_ready, v_ready, peaked, topped = (st.sem(n) for n in ("r_ready", "t_ready", "uq_ready", "v_ready", "peaked", "topped"))
        block = st.stack.enter_context(nc.Block())

        @block.sync
        def _(sp):
            def load(n, k, u):
                if not (isinstance(n, int) and n < 6):
                    sp.wait_ge(v_ready, n - 5)
                sp.dma_start(ut[k][:], half_view(up_d, n)).then_inc(u_in[k], 16)

            def store(n, k, u):
                sp.wait_ge(v_ready, n + 1)
                sp.dma_start(half_view(v_d, n), vt[k % 3][:]).then_inc(stored[k % 3], 16)

            def step(n, k, u):
                store(n, k, u)
                load(n + 6, k, u + 1)
            for k in range(3):
                sp.sem_inc(stored[k], 16)
            for k in range(6):
                load(k, k, 0)
            sixes(sp, 0, HUNITS - 6, step)
            for n in range(HUNITS - 6, HUNITS):
                store(n, n % 6, 0)
            for k in range(3):
                sp.wait_ge(stored[k], 16 + 16 * HUNITS // 3)

        @block.scalar
        def _(a):
            def step(n, k, u):
                a.wait_ge(u_in[k], 16 * u + 16)
                a.wait_ge(stored[k % 3], 32 * u + 16 * (k // 3) + 16)
                a.wait_ge(peaked, n + 1)
                a.activation(ut[k][:], ut[k][:], ACT.Identity, bias=glob[:, RND:RND + 1], scale=glob[:, FU:FU + 1]).then_inc(r_ready, 1)
                a.activation(vt[k % 3][:], gated[:, bass.ds(n, 1), :].rearrange("p a n -> p (a n)"), ACT.Identity,
                             bias=glob[:, RND:RND + 1], scale=glob[:, F2:F2 + 1]).then_inc(t_ready, 1)
            sixes(a, 0, HUNITS, step)

        @block.gpsimd
        def _(pool):
            def step(n, k, u):
                pool.wait_ge(r_ready, n + 1)
                pool.tensor_tensor(ut[k][:], ut[k][:], glob[:, NRND:NRND + 1].broadcast_to([128, N]), ALU.add).then_inc(uq_ready, 1)
            sixes(pool, 0, HUNITS, step)

        @block.vector
        def _(v):
            def step(n, k, u):
                v.wait_ge(t_ready, n + 1)
                v.wait_ge(uq_ready, n + 1)
                v.scalar_tensor_tensor(vt[k % 3][:], vt[k % 3][:], -ROUND, ut[k][:], ALU.add, ALU.mult).then_inc(v_ready, 1)
                v.wait_ge(v_ready, n + 1)
                v.wait_ge(topped, n + 1)
                v.tensor_reduce(now[:], vt[k % 3][:], AX.X, ALU.max, apply_absolute_value=True).then_inc(peaked, 1)
                v.wait_ge(peaked, n + 4)
                v.tensor_tensor(best[:], best[:], now[:], ALU.max).then_inc(topped, 1)
            v.sem_inc(peaked, 3)
            v.memset(best[:], 0.0).then_inc(topped, 1)
            sixes(v, 0, HUNITS, step)
            v.wait_ge(topped, HUNITS + 1)
            v.tensor_copy(glob[:, PEAK_V:PEAK_V + 1], best[:]).then_inc(peaked, 1)
            v.wait_ge(peaked, HUNITS + 4)


def down(nc, sems, v_d, w_parts, glob, x, x_out, xn_out):
    N = 2048
    with Stage(nc, sems, "dn") as st:
        w = [st.sb(f"w{p}", [128, 4 * QUADS, D], F32R) for p in range(2)]
        vt = [st.sb(f"v{k}", [128, N]) for k in range(2)]
        hi = [st.sb(f"hi{k}", [128, N], F32R) for k in range(2)]
        lo = [st.sb(f"lo{k}", [128, N], F32R) for k in range(2)]
        xt = [st.sb(f"x{k}", [128, 4, D]) for k in range(2)]
        xo = [st.sb(f"xo{k}", [128, 4, D]) for k in range(2)]
        xn = [st.sb(f"xn{k}", [128, 4, D]) for k in range(2)]
        out = [st.ps(f"out{k}", (128, 4, 512)) for k in range(2)]
        v_in = [st.sem(f"v_in{k}") for k in range(2)]
        x_in = [st.sem(f"x_in{k}") for k in range(2)]
        stored = [st.sem(f"stored{k}") for k in range(2)]
        w_in = [st.sem(f"w_in{q}") for q in range(QUADS)]
        r_ready, hi_ready, lo_ready, mm_done = (st.sem(n) for n in ("r_ready", "hi_ready", "lo_ready", "mm_done"))
        xo_ready, xn_ready, scale_set = st.sem("xo_ready"), st.sem("xn_ready"), st.sem("scale_set")
        norm = Norm(st, 128)
        block = st.stack.enter_context(nc.Block())

        def tiles(t, g):
            return t[bass.ds(g * 512, 512), :].rearrange("(j p) c -> p j c", p=128)

        def units(g, k, u, body):
            for q in range(QUADS):
                body(QUADS * g + q, (k + q) % 2, QUADS * u + (QUADS * k + q) // 2)

        @block.sync
        def _(sp):
            def load_unit(n, k, weights=False):
                if weights:
                    for p in range(2):
                        sp.dma_start(w[p][:, 4 * n:4 * n + 4, :].bitcast(F32),
                                     w_parts[p][512 * n:512 * (n + 1), :].rearrange("(c p) n -> p c n", p=128)).then_inc(w_in[n], 16)
                if not (isinstance(n, int) and n < 2):
                    sp.wait_ge(lo_ready, n - 1)
                sp.dma_start(vt[k][:].rearrange("p (a n) -> p a n", a=2), unit_view(v_d, n)).then_inc(v_in[k], 16)

            def load_x(g, k):
                if not (isinstance(g, int) and g < 2):
                    sp.wait_ge(xo_ready, 4 * g - 4)
                sp.dma_start(xt[k][:], tiles(x, g)).then_inc(x_in[k], 16)

            def store(g, k, u):
                sp.wait_ge(xo_ready, 4 * g + 4)
                sp.dma_start(tiles(x_out, g), xo[k][:]).then_inc(stored[k], 16)
                sp.wait_ge(xn_ready, 4 * g + 4)
                sp.dma_start(tiles(xn_out, g), xn[k][:]).then_inc(stored[k], 16)

            def step(g, k, u, units=3):
                for q in range(units):
                    load_unit(QUADS * g + 5 + q, (k + 1 + q) % 2)
                load_x(g + 1, 1 - k)
                store(g, k, u)
            assert QUADS == 3
            for n in range(5):
                load_unit(n, n % 2, n < QUADS)
                if n == 1:
                    load_x(0, 0)
            sp.sem_inc(stored[0], 32)
            sp.sem_inc(stored[1], 32)
            step(0, 0, 0)
            pairs(sp, 1, G5 - 2, step)
            step(G5 - 2, 1, 2, 1)
            store(G5 - 1, 0, 3)
            sp.wait_ge(stored[0], 32 + 32 * 4)
            sp.wait_ge(stored[1], 32 + 32 * 3)

        @block.scalar
        def _(a):
            def one(n, s, used):
                a.wait_ge(v_in[s], 16 * used + 16)
                a.activation(vt[s][:], vt[s][:], ACT.Identity, bias=glob[:, RND:RND + 1], scale=glob[:, FO:FO + 1]).then_inc(r_ready, 1)

            def step(g, k, u, more=True):
                if more:
                    units(g + 1, 1 - k, u + k, one)
                norm.scalar(a, g)
            units(0, 0, 0, one)
            step(0, 0, 0)
            pairs(a, 1, G5 - 1, step)
            step(G5 - 1, 0, 3, False)

        @block.vector
        def _(v):
            def one(n, s, used):
                v.wait_ge(r_ready, n + 1)
                v.wait_ge(mm_done, n + 1)
                v.tensor_scalar(hi[s][:], vt[s][:], ROUND, None, ALU.subtract).then_inc(hi_ready, 1)
                v.wait_ge(hi_ready, n + 1)
                v.scalar_tensor_tensor(lo[s][:], vt[s][:], -ROUND, hi[s][:].bitcast(F32), ALU.add, ALU.subtract).then_inc(lo_ready, 1)

            def step(g, k, u, more=True):
                if more:
                    units(g + 1, 1 - k, u + k, one)
                v.wait_ge(mm_done, QUADS * (g + 1) + 2)
                v.wait_ge(x_in[k], 16 * u + 16)
                v.wait_ge(stored[k], 32 * u + 32)
                for j in range(4):
                    v.scalar_tensor_tensor(xo[k][:, j, :], out[k][:, j, :], glob[:, GSO:GSO + 1], xt[k][:, j, :], ALU.mult, ALU.add).then_inc(xo_ready, 1)
                v.wait_ge(xo_ready, 4 * g + 4)
                norm.vector(v, g, xo[k], xn[k], xn_ready)
            v.sem_inc(mm_done, 2)
            v.tensor_tensor(glob[:, GSO:GSO + 1], glob[:, GF0:GF0 + 1], glob[:, SO:SO + 1], ALU.mult).then_inc(scale_set, 1)
            v.wait_ge(scale_set, 1)
            units(0, 0, 0, one)
            step(0, 0, 0)
            pairs(v, 1, G5 - 1, step)
            step(G5 - 1, 0, 3, False)

        @block.tensor
        def _(t):
            def step(g, k, u):
                if not (isinstance(g, int) and g < 2):
                    t.wait_ge(xo_ready, 4 * g - 4)
                q = iter(range(QUADS))

                def one(n, s, used):
                    quad = next(q)
                    if is_first(g):
                        t.wait_ge(w_in[quad], 32)
                    t.wait_ge(lo_ready, n + 1)
                    for j in range(4):
                        for c in range(4):
                            for m, (px, pw) in enumerate(PASSES):
                                at = c * 512 + j * 128
                                mm = t.matmul(out[k][:, j, :], (hi, lo)[px][s][:, at:at + 128], w[pw][:, 4 * quad + c, :],
                                              start=(quad == 0 and m == 0 and c == 0), stop=(quad == QUADS - 1 and m == 2 and c == 3))
                    mm.then_inc(mm_done, 1)
                units(g, k, u, one)
            step(0, 0, 0)
            step(1, 1, 0)
            pairs(t, 2, G5, step)


def ffn0(nc, sems, xn, w_gate, w_up, w_down, w_parts, ident_d, glob, gate_d, up_d, v_d, x, x_out, xn_out):
    gate_t, up_t, down_t = w_parts
    def down_views(w):
        return [w[:, g * 512:(g + 1) * 512].rearrange("(j p) c -> p j c", p=128) for g in range(QUADS)]

    def up_views(w):
        return [w[g * 512:(g + 1) * 512, :].rearrange("(j p) c -> p j c", p=128) for g in range(QUADS)]
    quantise_weights(nc, sems, glob, up_views(w_gate) + up_views(w_up) + down_views(w_down), ident_d,
                     [down_views(gate_t[p]) + down_views(up_t[p]) + up_views(down_t[p]) for p in range(2)])
    scales(nc, sems, glob, "sc_x", [(PEAK_X, ONE, ONE, 1.0, SX, FX)])
    up_gate(nc, sems, xn, gate_t, up_t, ident_d, glob, gate_d, up_d)
    scales(nc, sems, glob, "sc_gu", [(PEAK_G, SX, ONE, 1.0, SG, FG), (PEAK_U, SX, ONE, 1.0, SU, FU)])
    with nc.sbuf_tensor("gated", [128, HUNITS, UW], F32) as gated:
        gate_sigmoid(nc, sems, gate_d, gated, glob)
        scales(nc, sems, glob, "sc_t", [(PEAK_T, SG, ONE, 1.0 / 65536.0, S2, F2)])
        gate_times_up(nc, sems, gated, up_d, v_d, glob)
    scales(nc, sems, glob, "sc_v", [(PEAK_V, S2, SU, 1.0, SO, FO)])
    down(nc, sems, v_d, down_t, glob, x, x_out, xn_out)



def after(eng, sem, value):
    if not (isinstance(value, int) and value <= 0):
        eng.wait_ge(sem, value)


def attend1(nc, sems, xn, ctx, ctx_t, wq, bq, wk, bk, wv_t, bv, ident_d, glob, x, x_out, xn_out):
    NG, W, Q = B // 2, 2 * S, S // 2
    with Stage(nc, sems, "a1") as st:
        ident = st.sb("ident", [128, 128])
        bq_sb, bk_sb = st.sb("bq", [128, DC]), st.sb("bk", [128, DC])
        wv_raw, gbv = st.sb("wv_raw", [128, CC, D]), st.sb("gbv", [Q, D])
        wv2 = [st.sb(f"wv{p}", [128, CC, D], F32R) for p in range(2)]
        a2 = [st.sb(f"a{p}", [128, DC, C], F32R) for p in range(2)]
        cb, wcq, bb = st.sb("cb", [128, CC]), st.sb("wcq", [128, DC], F32R), st.sb("bb", [1, 1])
        ones = st.sb("ones", [1, NH], F32R)
        ones_col, p_sum = st.sb("ones_col", [128, 1]), st.sb("p_sum", [KP, S])
        xt = st.sb("xt", [Q, 4, D])
        x2 = [st.sb(f"xT{p}", [128, DC, W], F32R) for p in range(2)]
        q2 = [st.sb(f"q{p}", [128, CC, W], F32R) for p in range(2)]
        cq = st.sb("cq", [1, W], F32R)
        ct_raw, cn_raw = st.sb("ct_raw", [128, CC, M]), st.sb("cn_raw", [128, KC, C])
        ct2 = [[st.sb(f"ct{k}{p}", [128, CC, M], F32R) for p in range(2)] for k in range(2)]
        cn2 = [[st.sb(f"cn{k}{p}", [KP, KC, C], F32R) for p in range(2)] for k in range(2)]
        wq_sb = ct_raw[:].rearrange("p c m -> p (c m)")[:, 0:DC * D].rearrange("p (c n) -> p c n", n=D)
        wk_sb = cn_raw[:].rearrange("p c m -> p (c m)")[:, 0:DC * C].rearrange("p (c n) -> p c n", n=C)
        neg_max, row = st.sb("neg_max", [Q, 2]), st.sb("row", [1, S], F32R)
        p32 = st.sb("p32", [KP, KC * S])
        p2 = [st.sb(f"p{p}", [KP, KC * S], F32R) for p in range(2)]
        pc2 = [st.sb(f"pc{p}", [128, CC, S], F32R) for p in range(2)]
        rec, rg = st.sb("rec", [Q, 2]), st.sb("rg", [Q, 2])
        xr = [st.sb(f"xr{k}", [Q, 2, D]) for k in range(2)]
        xo = [st.sb(f"xo{k}", [Q, 2, D]) for k in range(2)]
        xno = [st.sb(f"xno{k}", [Q, 2, D]) for k in range(2)]

        turn_bank = st.ps("turn")
        sc = st.ps("sc", (128, 3, 512))
        mx = st.ps("mx", (128, 2, 512))
        pc = st.ps("pc", (128, 2, 512))

        (w_in, bias_in, wv_in, ones_set, pre_mm, pre_hi, pre_done, gbv_set, wv_split) = (st.sem(n) for n in (
            "w_in", "bias_in", "wv_in", "ones_set", "pre_mm", "pre_hi", "pre_done", "gbv_set", "wv_split"))
        x_in, ct_in, cn_in = st.sem("x_in"), st.sem("ct_in"), st.sem("cn_in")
        xr_in = [st.sem(f"xr_in{k}") for k in range(2)]
        stored = [st.sem(f"stored{k}") for k in range(2)]
        turned, q_full, mx_full, row_full, st_full, pc_full, wv_full = (st.sem(n) for n in (
            "turned", "q_full", "mx_full", "row_full", "st_full", "pc_full", "wv_full"))
        x_hi, cq_done, q_hi, ct_hi, cn_hi, exp_done, p_hi, pc_hi = (st.sem(n) for n in (
            "x_hi", "cq_done", "q_hi", "ct_hi", "cn_hi", "exp_done", "p_hi", "pc_hi"))
        x_lo, q_lo, ct_lo, cn_lo, p_lo, pc_lo = (st.sem(n) for n in ("x_lo", "q_lo", "ct_lo", "cn_lo", "p_lo", "pc_lo"))
        mx_done, row_done, sum_step, xb_done, xo_ready, xn_ready = (st.sem(n) for n in (
            "mx_done", "row_done", "sum_step", "xb_done", "xo_ready", "xn_ready"))
        p_sums = st.sem("p_sums")
        norm = Norm(st, Q, 2)
        block = st.stack.enter_context(nc.Block())

        def batches(eng, step):
            step(0, 0, 0, True, True)
            step(1, 1, 0, True, True)
            with eng.Fori(0, NG - 3) as r:
                step(2 * r + 2, 0, r + 1, True, True)
                step(2 * r + 3, 1, r + 1, True, True)
            step(B - 4, 0, NG - 2, True, True)
            step(B - 3, 1, NG - 2, True, True)
            step(B - 2, 0, NG - 1, True, False)
            step(B - 1, 1, NG - 1, False, False)

        def rows(t, b):
            return t[bass.ds(b * S, S), :].rearrange("(q p) c -> p q c", p=Q)

        def pre_bank(i):
            return sc[:, i, :] if i < 3 else mx[:, 0, :]

        @block.sync
        def _(sp):
            def load_x(g):
                after(sp, turned, 5 * g - 1)
                sp.dma_start(xt[:], xn[bass.ds(g * W, W), :].rearrange("(j p) c -> p j c", p=Q)).then_inc(x_in, 16)

            def load_ct(b):
                after(sp, ct_lo, b)
                sp.dma_start(ct_raw[:], ctx_t[bass.ds(b, 1), :, :].rearrange("a (c p) m -> p (a c) m", p=128)).then_inc(ct_in, 16)

            def load_cn(b):
                after(sp, cn_lo, b)
                sp.dma_start(cn_raw[:KP], ctx[bass.ds(b, 1), :, :].rearrange("a (c p) m -> p (a c) m", p=KP)).then_inc(cn_in, 16)

            def load_xr(b, k):
                after(sp, xo_ready, 2 * b - 2)
                sp.dma_start(xr[k][:], rows(x, b)).then_inc(xr_in[k], 16)

            def step(b, e, g, more, turn):
                if e == 1 and turn and not (isinstance(g, int) and g + 2 >= NG):
                    load_x(g + 2)
                if turn:
                    load_ct(b + 2)
                    load_cn(b + 2)
                sp.wait_ge(xo_ready, 2 * b + 2)
                sp.dma_start(rows(x_out, b), xo[e][:]).then_inc(stored[e], 16)
                if turn:
                    load_xr(b + 2, e)
                sp.wait_ge(xn_ready, 2 * b + 2)
                sp.dma_start(rows(xn_out, b), xno[e][:]).then_inc(stored[e], 16)

            sp.dma_start(wq_sb, wq.rearrange("(c p) n -> p c n", p=128)).then_inc(w_in, 16)
            sp.dma_start(wk_sb, wk.rearrange("(c p) n -> p c n", p=128)).then_inc(w_in, 16)
            sp.dma_start(bq_sb[:], bq.rearrange("(c p) -> p c", p=128), allow_slow_non_contiguous=True).then_inc(bias_in, 16)
            sp.dma_start(bk_sb[:], bk.rearrange("(c p) -> p c", p=128), allow_slow_non_contiguous=True).then_inc(bias_in, 16)
            sp.dma_start(ident[:], ident_d).then_inc(bias_in, 16)
            sp.dma_start(xt[:], xn[0:W, :].rearrange("(j p) c -> p j c", p=Q)).then_inc(x_in, 16)
            sp.dma_start(wv_raw[:], wv_t.rearrange("(c p) n -> p c n", p=128)).then_inc(wv_in, 16)
            sp.dma_start(gbv[:], bv.partition_broadcast(Q)).then_inc(wv_in, 16)
            load_xr(0, 0)
            load_xr(1, 1)
            sp.wait_ge(pre_mm, DC + 1)
            load_ct(0)
            load_cn(0)
            load_ct(1)
            load_cn(1)
            load_x(1)
            sp.sem_inc(stored[0], 32)
            sp.sem_inc(stored[1], 32)
            batches(sp, step)
            for k in range(2):
                sp.wait_ge(stored[k], 32 + 16 * B)

        @block.gpsimd
        def _(pool):
            def split_ct(b, k):
                pool.wait_ge(ct_hi, b + 1)
                pool.tensor_tensor(ct2[k][1][:], ct_raw[:], ct2[k][0][:].bitcast(F32), ALU.subtract).then_inc(ct_lo, 1)

            def split_cn(b, k):
                pool.wait_ge(cn_hi, b + 1)
                pool.tensor_tensor(cn2[k][1][:], cn_raw[:KP], cn2[k][0][:].bitcast(F32), ALU.subtract).then_inc(cn_lo, 1)

            def add_bias(b, k, used):
                pool.wait_ge(xr_in[k], 16 * used + 16)
                pool.tensor_tensor(xr[k][:], xr[k][:], gbv[:].unsqueeze(1).broadcast_to([Q, 2, D]), ALU.add).then_inc(xb_done, 1)

            def step(b, e, g, more, turn):
                if more:
                    split_cn(b + 1, 1 - e)
                if turn:
                    split_ct(b + 2, e)
                    add_bias(b + 2, e, g + 1)

            split_ct(0, 0)
            split_cn(0, 0)
            split_ct(1, 1)
            pool.wait_ge(gbv_set, 1)
            add_bias(0, 0, 0)
            add_bias(1, 1, 0)
            batches(pool, step)

        @block.scalar
        def _(a):
            def split_ct(b, k):
                after(a, st_full, 3 * b - 3)
                a.wait_ge(ct_in, 16 * b + 16)
                a.activation(ct2[k][0][:], ct_raw[:], ACT.Copy).then_inc(ct_hi, 1)

            def split_cn(b, k):
                after(a, pc_full, 2 * b - 2)
                a.wait_ge(cn_in, 16 * b + 16)
                a.activation(cn2[k][0][:], cn_raw[:KP], ACT.Copy).then_inc(cn_hi, 1)

            def turn_hi(g, d):
                if d == 0:
                    after(a, q_full, 3 * g)
                a.wait_ge(turned, 5 * g + d + 1)
                a.activation(x2[0][:, d, :], turn_bank[:, 0:W], ACT.Copy).then_inc(x_hi, 1)

            def queries(g):
                after(a, st_full, 6 * g)
                for c in range(CC):
                    a.wait_ge(q_full, 3 * g + c + 1)
                    a.activation(q2[0][:, c, :], sc[:, c, 0:W], ACT.Identity, bias=cb[:, c:c + 1]).then_inc(q_hi, 1)
                after(a, row_done, 2 * g)
                a.wait_ge(turned, 5 * g + 5)
                a.activation(cq[:], turn_bank[0:1, 0:W], ACT.Identity, bias=bb[:, 0:1]).then_inc(cq_done, 1)

            def probs(b):
                after(a, p_sums, b)
                after(a, p_lo, b)
                for j in range(3):
                    a.wait_ge(st_full, 3 * b + j + 1)
                    a.activation(p32[:, j * 448:(j + 1) * 448], sc[:KP, j, 0:448], ACT.Exp, scale=D ** -0.5).then_inc(exp_done, 1)
                after(a, pc_full, 2 * b)
                a.wait_ge(exp_done, 3 * b + 3)
                a.activation(p2[0][:], p32[:], ACT.Copy).then_inc(p_hi, 1)

            def step(b, e, g, more, turn):
                if e == 1 and turn:
                    queries(g + 1)
                if e == 0 and turn:
                    turn_hi(g + 1, 0)
                if more:
                    split_cn(b + 1, 1 - e)
                after(a, wv_full, 2 * b)
                for i, (c0, c1) in enumerate(((0, 2), (2, 3))):
                    a.wait_ge(pc_full, 2 * b + i + 1)
                    a.activation(pc2[0][:, c0:c1, :], pc[:, i, 0:(c1 - c0) * S].rearrange("p (c q) -> p c q", q=S), ACT.Copy).then_inc(pc_hi, 1)
                if e == 0 and turn:
                    turn_hi(g + 1, 1)
                if more:
                    probs(b + 1)
                if e == 0 and turn:
                    turn_hi(g + 1, 2)
                    turn_hi(g + 1, 3)
                if turn:
                    split_ct(b + 2, e)
                norm.scalar(a, b)

            for d in range(DC):
                turn_hi(0, d)
            for i in range(DC):
                a.wait_ge(pre_mm, i + 1)
                a.activation(a2[0][:, i, :], pre_bank(i)[:, 0:C], ACT.Copy).then_inc(pre_hi, 1)
            a.wait_ge(pre_done, 6)
            split_ct(0, 0)
            split_cn(0, 0)
            a.wait_ge(ct_lo, 1)
            split_ct(1, 1)
            queries(0)
            probs(0)
            batches(a, step)

        @block.vector
        def _(v):
            def turn_lo(g, d):
                v.wait_ge(x_hi, 4 * g + d + 1)
                v.tensor_tensor(x2[1][:, d, :], turn_bank[:, 0:W], x2[0][:, d, :].bitcast(F32), ALU.subtract).then_inc(x_lo, 1)

            def queries(g):
                for c in range(CC):
                    v.wait_ge(q_hi, 3 * g + c + 1)
                    v.scalar_tensor_tensor(q2[1][:, c, :], sc[:, c, 0:W], cb[:, c:c + 1], q2[0][:, c, :].bitcast(F32), ALU.add, ALU.subtract).then_inc(q_lo, 1)

            def maxima(b):
                after(v, row_full, b)
                for qt in range(2):
                    v.wait_ge(mx_full, 2 * b + qt + 1)
                    v.tensor_reduce(neg_max[:, qt:qt + 1], (mx, sc)[qt][:Q, 0:2, 0:NH], AX.XY, ALU.max, negate=True).then_inc(mx_done, 1)

            def shift(b, e):
                v.wait_ge(row_full, b + 1)
                v.tensor_tensor(row[:].rearrange("p (q t) -> p q t", q=2), mx[0:1, :, 384:384 + Q],
                                cq[:, e * S:(e + 1) * S].bitcast(F32).rearrange("p (q t) -> p q t", q=2), ALU.add).then_inc(row_done, 1)

            def low(b):
                v.wait_ge(p_hi, b + 1)
                after(v, pc_full, 2 * b)
                v.tensor_reduce(p_sum[:], p32[:].rearrange("p (k q) -> p q k", q=S), AX.X, ALU.add).then_inc(p_sums, 1)
                v.tensor_tensor(p2[1][:], p32[:], p2[0][:].bitcast(F32), ALU.subtract).then_inc(p_lo, 1)

            def step(b, e, g, more, turn):
                if e == 1 and turn:
                    queries(g + 1)
                if more:
                    maxima(b + 1)
                if e == 0 and turn:
                    turn_lo(g + 1, 0)
                if more:
                    v.wait_ge(cq_done, g + 1 + e)
                    shift(b + 1, 1 - e)
                for i, (c0, c1) in enumerate(((0, 2), (2, 3))):
                    v.wait_ge(pc_hi, 2 * b + i + 1)
                    v.tensor_tensor(pc2[1][:, c0:c1, :], pc[:, i, 0:(c1 - c0) * S].rearrange("p (c q) -> p c q", q=S),
                                    pc2[0][:, c0:c1, :].bitcast(F32), ALU.subtract).then_inc(pc_lo, 1)
                v.reciprocal(rec[:], pc[:Q, 1, 256:258]).then_inc(sum_step, 1)
                v.wait_ge(sum_step, 2 * b + 1)
                v.tensor_scalar(rg[:], rec[:], glob[:Q, GX1:GX1 + 1], None, ALU.mult).then_inc(sum_step, 1)
                if e == 0 and turn:
                    turn_lo(g + 1, 1)
                if more:
                    low(b + 1)
                if e == 0 and turn:
                    turn_lo(g + 1, 2)
                v.wait_ge(stored[e], 32 * g + 32)
                v.wait_ge(xb_done, b + 1)
                v.wait_ge(sum_step, 2 * b + 2)
                for qt in range(2):
                    v.wait_ge(wv_full, 2 * b + qt + 1)
                    v.scalar_tensor_tensor(xo[e][:, qt, :], mx[:Q, qt, :], rg[:, qt:qt + 1], xr[e][:, qt, :], ALU.mult, ALU.add).then_inc(xo_ready, 1)
                if e == 0 and turn:
                    turn_lo(g + 1, 3)
                v.wait_ge(xo_ready, 2 * b + 2)
                norm.vector(v, b, xo[e], xno[e], xn_ready)

            v.memset(ones[:].bitcast(F32), 1.0).then_inc(ones_set, 1)
            v.memset(ones_col[:], 1.0).then_inc(ones_set, 1)
            for d in range(DC):
                turn_lo(0, d)
            v.wait_ge(pre_mm, DC + 1)
            v.tensor_copy(cb[:], pc[:, 0, 0:CC]).then_inc(pre_done, 1)
            v.tensor_copy(wcq[:], pc[:, 0, CC:CC + DC]).then_inc(pre_done, 1)
            v.tensor_copy(bb[:], pc[0:1, 0, 8:9]).then_inc(pre_done, 1)
            for i in range(DC):
                v.wait_ge(pre_hi, i + 1)
                v.tensor_tensor(a2[1][:, i, :], pre_bank(i)[:, 0:C], a2[0][:, i, :].bitcast(F32), ALU.subtract).then_inc(pre_done, 1)
            v.wait_ge(wv_in, 32)
            v.tensor_scalar(gbv[:], gbv[:], glob[:Q, GX1:GX1 + 1], None, ALU.mult).then_inc(gbv_set, 1)
            split_weights(v, wv_raw[:], wv2[0][:], wv2[1][:], wv_split, 0)
            queries(0)
            maxima(0)
            v.wait_ge(cq_done, 1)
            shift(0, 0)
            low(0)
            batches(v, step)

        @block.tensor
        def _(t):
            def turn_tile(g, d):
                if d == 0:
                    t.wait_ge(x_in, 16 * g + 16)
                    after(t, cq_done, g)
                else:
                    t.wait_ge(x_lo, 4 * g + d)
                for j in range(4):
                    mm = t.transpose(turn_bank[:, j * Q:(j + 1) * Q], xt[:, j, d * 128:(d + 1) * 128], ident[:Q, :Q])
                mm.then_inc(turned, 1)

            def queries(g):
                t.wait_ge(x_lo, 4 * g + 4)
                after(t, exp_done, 6 * g)
                for c in range(CC):
                    for n, (pw, px) in enumerate(PASSES):
                        for d in range(DC):
                            mm = t.matmul(sc[:, c, 0:W], a2[pw][:, d, c * 128:(c + 1) * 128], x2[px][:, d, :],
                                          start=(n == 0 and d == 0), stop=(n == 2 and d == DC - 1))
                    mm.then_inc(q_full, 1)
                for d in range(DC):
                    mm = t.matmul(turn_bank[0:1, 0:W], wcq[:, d:d + 1], x2[0][:, d, :], start=(d == 0), stop=(d == DC - 1))
                mm.then_inc(turned, 1)

            def maxima(b, e, g, k):
                t.wait_ge(ct_hi, b + 1)
                t.wait_ge(q_hi, 3 * g + 3)
                t.wait_ge(cq_done, g + 1)
                after(t, xo_ready, 2 * b - 2)
                for qt in range(2):
                    if qt == 1:
                        after(t, exp_done, 3 * b)
                        t.wait_ge(q_lo, 3 * g + 3)
                    off = e * S + qt * Q
                    for half in range(2):
                        bank = (mx, sc)[qt][:Q, half, 0:NH]
                        for c in range(CC):
                            t.matmul(bank, q2[0][:, c, off:off + Q], ct2[k][0][:, c, COVER[half]], start=(c == 0), stop=False)
                        mm = t.matmul(bank, cq[:, off:off + Q], ones[:, 0:NH], start=False, stop=True)
                    mm.then_inc(mx_full, 1)

            def turn_maxima(b):
                t.wait_ge(mx_done, 2 * b + 2)
                for qt in range(2):
                    mm = t.transpose(mx[0:1, qt, 384:384 + Q], neg_max[:, qt:qt + 1], ident[:Q, :Q])
                mm.then_inc(row_full, 1)

            def scores(b, e, k):
                t.wait_ge(row_done, b + 1)
                t.wait_ge(ct_lo, b + 1)
                for j in range(3):
                    for i in range(2):
                        kc = 2 * j + i
                        bank = sc[:KP, j, i * S:(i + 1) * S]
                        for n, (pc_, pq) in enumerate(PASSES):
                            for c in range(CC):
                                t.matmul(bank, ct2[k][pc_][:, c, kc * KP:(kc + 1) * KP], q2[pq][:, c, e * S:(e + 1) * S],
                                         start=(n == 0 and c == 0), stop=False)
                        mm = t.matmul(bank, ones[:, 0:KP], row[:], start=False, stop=True)
                    mm.then_inc(st_full, 1)

            def weigh(b, k):
                t.wait_ge(p_sums, b + 1)
                t.wait_ge(p_lo, b + 1)
                t.wait_ge(cn_lo, b + 1)
                after(t, pc_lo, 2 * b)
                after(t, sum_step, 2 * b)
                for c in range(CC):
                    bank = pc[:, c // 2, (c % 2) * S:(c % 2 + 1) * S]
                    for n, (pw, pp) in enumerate(PASSES):
                        for kc in range(KC):
                            mm = t.matmul(bank, cn2[k][pw][:, kc, c * 128:(c + 1) * 128], p2[pp][:, kc * S:(kc + 1) * S],
                                          start=(n == 0 and kc == 0), stop=(n == 2 and kc == KC - 1))
                    if c == 1:
                        mm.then_inc(pc_full, 1)
                for qt in range(2):
                    mm = t.matmul(pc[:Q, 1, 256 + qt:257 + qt], p_sum[:, qt * Q:(qt + 1) * Q], ones_col[:KP, :], start=True, stop=True)
                mm.then_inc(pc_full, 1)

            def values(b):
                t.wait_ge(pc_lo, 2 * b + 2)
                for qt in range(2):
                    for n, (pp, pw) in enumerate(PASSES):
                        for c in range(CC):
                            mm = t.matmul(mx[:Q, qt, :], pc2[pp][:, c, qt * Q:(qt + 1) * Q], wv2[pw][:, c, :],
                                          start=(n == 0 and c == 0), stop=(n == 2 and c == CC - 1))
                    mm.then_inc(wv_full, 1)

            def step(b, e, g, more, turn):
                if e == 1 and turn:
                    queries(g + 1)
                if more:
                    maxima(b + 1, 1 - e, g + e, 1 - e)
                if e == 0 and turn:
                    turn_tile(g + 1, 0)
                weigh(b, e)
                if e == 0 and turn:
                    turn_tile(g + 1, 1)
                if more:
                    turn_maxima(b + 1)
                    scores(b + 1, 1 - e, 1 - e)
                if e == 0 and turn:
                    turn_tile(g + 1, 2)
                values(b)
                if e == 0 and turn:
                    turn_tile(g + 1, 3)

            t.wait_ge(bias_in, 48)
            for d in range(DC):
                turn_tile(0, d)
            t.wait_ge(w_in, 32)
            for i in range(DC):
                for o in range(DC):
                    mm = t.matmul(pre_bank(i)[:, 0:C], wq_sb[:, o, i * 128:(i + 1) * 128], wk_sb[:, o, :], start=(o == 0), stop=(o == DC - 1))
                mm.then_inc(pre_mm, 1)
            for c in range(CC):
                for o in range(DC):
                    t.matmul(pc[:, 0, c:c + 1], wk_sb[:, o, c * 128:(c + 1) * 128], bq_sb[:, o:o + 1], start=(o == 0), stop=(o == DC - 1))
            for c in range(DC):
                for o in range(DC):
                    t.matmul(pc[:, 0, CC + c:CC + c + 1], wq_sb[:, o, c * 128:(c + 1) * 128], bk_sb[:, o:o + 1], start=(o == 0), stop=(o == DC - 1))
            for o in range(DC):
                mm = t.matmul(pc[0:1, 0, 8:9], bq_sb[:, o:o + 1], bk_sb[:, o:o + 1], start=(o == 0), stop=(o == DC - 1))
            mm.then_inc(pre_mm, 1)
            t.wait_ge(pre_done, 7)
            t.wait_ge(ones_set, 2)
            queries(0)
            maxima(0, 0, 0, 0)
            turn_maxima(0)
            scores(0, 0, 0)
            t.wait_ge(wv_split, 2)
            batches(t, step)



NTOP = NBLK // 4
OFF = -1e30
TINY = -87.3365
TAKEN, SPARE = -3e38, -2e38


def load_ffn1(nc, sems, router_t, w1_t, w2_t, rw, w1, w2):
    with Stage(nc, sems, "fw") as st:
        raw = [st.sb(f"raw{k}", [128, I1]) for k in range(4)]
        w_in = [st.sem(f"w_in{k}") for k in range(4)]
        hi_done, lo_done = st.sem("hi_done"), st.sem("lo_done")
        block = st.stack.enter_context(nc.Block())

        def flat(t):
            return t.rearrange("p c n -> p (c n)")
        pieces = [(router_t.rearrange("(c p) n -> p c n", p=128), [flat(r[:]) for r in rw], DC)]
        pieces += [(w1_t[c * 128:(c + 1) * 128, :].unsqueeze(1), [w[:, c, :] for w in w1], 1) for c in range(DC)]
        pieces += [(w2_t[c * 512:(c + 1) * 512, :].rearrange("(c p) n -> p c n", p=128),
                    [flat(w[:, 4 * c:4 * c + 4, :]) for w in w2], 4) for c in range(NBLK // 4)]

        def columns(i):
            return DC * NBLK if i == 0 else I1

        @block.sync
        def _(sp):
            for i, (src, _, rows) in enumerate(pieces):
                if i >= 4:
                    sp.wait_ge(lo_done, i - 3)
                sp.dma_start(raw[i % 4][:, 0:columns(i)].rearrange("p (c n) -> p c n", c=rows), src).then_inc(w_in[i % 4], 16)

        @block.scalar
        def _(a):
            for i, (_, parts, _) in enumerate(pieces):
                a.wait_ge(w_in[i % 4], 16 * (i // 4) + 16)
                a.activation(parts[0], raw[i % 4][:, 0:columns(i)], ACT.Copy).then_inc(hi_done, 1)

        @block.vector
        def _(v):
            for i, (_, parts, _) in enumerate(pieces):
                v.wait_ge(hi_done, i + 1)
                v.tensor_tensor(parts[1], raw[i % 4][:, 0:columns(i)], parts[0].bitcast(F32), ALU.subtract).then_inc(lo_done, 1)
            v.wait_ge(lo_done, len(pieces))


def ffn1(nc, sems, xn, router_t, router_b, w1_t, b1, w2_t, b2, ident_d, glob, x, result):
    with Stage(nc, sems, "f1") as st:
        ident = st.sb("ident", [128, 128])
        w1 = [st.sb(f"w1{p}", [128, DC, I1], F32R) for p in range(2)]
        w2 = [st.sb(f"w2{p}", [128, NBLK, D], F32R) for p in range(2)]
        rw = [st.sb(f"rw{p}", [128, DC, NBLK], F32R) for p in range(2)]
        load_ffn1(nc, sems, router_t, w1_t, w2_t, rw, w1, w2)
        b1_sb, rb, gb2 = st.sb("b1", [128, NBLK]), st.sb("rb", [128, NBLK]), st.sb("gb2", [128, D])
        select = st.sb("select", [NBLK, NBLK, 128], BF16)
        xt, xr = st.sb("xt", [128, 4, D]), st.sb("xr", [128, 4, D])
        x2 = [[st.sb(f"xT{k}{p}", [128, DC, 512], F32R) for p in range(2)] for k in range(2)]
        r32 = [st.sb(f"r32_{k}", [128, 512]) for k in range(2)]
        h2 = [[st.sb(f"h{s}{p}", [128, 512], F32R) for p in range(2)] for s in range(4)]
        lg, z, unused = (st.sb(n, [128, 4, NBLK]) for n in ("lg", "z", "unused"))
        zc, left = (st.sb(n, [128, 4, NBLK + 8 - NTOP]) for n in ("zc", "left"))
        top1, top8, top4 = st.sb("top1", [128, 4]), st.sb("top8", [128, 4, 8]), st.sb("top4", [128, 4, 8])
        off = [st.sb(f"off{k}", [NBLK, 512], BF16) for k in range(2)]

        turn_bank, route_bank = st.ps("turn"), st.ps("route")
        hid = [st.ps(f"hid{k}") for k in range(2)]
        out = st.ps("out", (128, 4, 512))

        small_in, rb_in, x_in, xr_in, stored = (st.sem(n) for n in ("small_in", "rb_in", "x_in", "xr_in", "stored"))
        turned, lg_full, off_full, h_full, dn_done = (st.sem(n) for n in ("turned", "lg_full", "off_full", "h_full", "dn_done"))
        x_hi, relu_done, h_hi, x_lo, h_lo = (st.sem(n) for n in ("x_hi", "relu_done", "h_hi", "x_lo", "h_lo"))
        prep = st.sem("prep")
        route, xb_done, off_ready, xo_ready = st.sem("route"), st.sem("xb_done"), st.sem("off_ready"), st.sem("xo_ready")
        TURN_AT, ROUTE_AT, OFF_AT = (2, 4, 6, 8), 10, 13
        ROUTE_STEPS = 14
        block = st.stack.enter_context(nc.Block())

        def tiles(t, g):
            return t[bass.ds(g * 512, 512), :].rearrange("(j p) c -> p j c", p=128)

        @block.sync
        def _(sp):
            def load_x(g):
                after(sp, turned, 4 * g)
                sp.dma_start(xt[:], tiles(xn, g)).then_inc(x_in, 16)

            def load_xr(g):
                after(sp, stored, 16 * g)
                sp.dma_start(xr[:], tiles(x, g)).then_inc(xr_in, 16)

            def step(g, k, u, more=True):
                if more:
                    load_x(g + 1)
                sp.wait_ge(xo_ready, 4 * g + 4)
                sp.dma_start(tiles(result, g), xr[:]).then_inc(stored, 16)
                if more:
                    load_xr(g + 1)
            load_x(0)
            sp.dma_start(ident[:], ident_d).then_inc(small_in, 16)
            sp.dma_start(b1_sb[:], b1.rearrange("(c p) -> p c", p=128), allow_slow_non_contiguous=True).then_inc(small_in, 16)
            sp.dma_start(rb[:], router_b.partition_broadcast(128)).then_inc(rb_in, 16)
            sp.dma_start(gb2[:], b2.partition_broadcast(128)).then_inc(rb_in, 16)
            load_xr(0)
            step(0, 0, 0)
            pairs(sp, 1, G5 - 1, step)
            step(G5 - 1, 0, 3, False)
            sp.wait_ge(stored, 16 * G5)

        @block.gpsimd
        def _(pool):
            def step(g, k, u):
                pool.wait_ge(xr_in, 16 * g + 16)
                pool.tensor_tensor(xr[:], xr[:], gb2[:].unsqueeze(1).broadcast_to([128, 4, D]), ALU.add).then_inc(xb_done, 1)
            pool.wait_ge(prep, 3)
            pairs(pool, 0, G5, step)

        @block.scalar
        def _(a):
            def turn_hi(g, k, d):
                if d == 0:
                    after(a, h_full, 16 * g - 16)
                a.wait_ge(turned, 4 * g + d + 1)
                a.activation(x2[k][0][:, d, :], turn_bank[:], ACT.Copy).then_inc(x_hi, 1)

            def step(g, k, u, more=True):
                for i in range(NBLK):
                    if not (is_first(g) and i < 2):
                        a.wait_ge(h_lo, 16 * g + i - 1)
                    a.wait_ge(h_full, 16 * g + i + 1)
                    a.activation(r32[i % 2][:], hid[i % 2][:], ACT.Relu, bias=b1_sb[:, i:i + 1]).then_inc(relu_done, 1)
                    if not (is_first(g) and i < 4):
                        a.wait_ge(dn_done, 16 * g + i - 3)
                    a.wait_ge(relu_done, 16 * g + i + 1)
                    a.activation(h2[i % 4][0][:], r32[i % 2][:], ACT.Copy).then_inc(h_hi, 1)
                    if i in TURN_AT and more:
                        turn_hi(g + 1, 1 - k, TURN_AT.index(i))
            for d in range(DC):
                turn_hi(0, 0, d)
            step(0, 0, 0)
            pairs(a, 1, G5 - 1, step)
            step(G5 - 1, 0, 3, False)

        @block.vector
        def _(v):
            def turn_lo(g, k, d):
                v.wait_ge(x_hi, 4 * g + d + 1)
                v.tensor_tensor(x2[k][1][:, d, :], turn_bank[:], x2[k][0][:, d, :].bitcast(F32), ALU.subtract).then_inc(x_lo, 1)

            def choose(g):
                at = ROUTE_STEPS * g
                v.wait_ge(lg_full, g + 1)
                v.tensor_tensor(lg[:], route_bank[:, 0:4 * NBLK].rearrange("p (j n) -> p j n", n=NBLK),
                                rb[:].unsqueeze(1).broadcast_to([128, 4, NBLK]), ALU.add).then_inc(route, 1)
                v.wait_ge(route, at + 1)
                v.tensor_reduce(top1[:], lg[:], AX.X, ALU.max).then_inc(route, 1)
                v.wait_ge(route, at + 2)
                v.tensor_tensor(z[:], lg[:], top1[:].unsqueeze(2).broadcast_to([128, 4, NBLK]), ALU.subtract).then_inc(route, 1)
                v.wait_ge(route, at + 3)
                v.tensor_scalar(zc[:, :, 0:NBLK], z[:], TINY, None, ALU.max).then_inc(route, 1)
                v.wait_ge(route, at + 4)
                v.memset(top4[:, :, NTOP:8], SPARE).then_inc(route, 1)
                for j in range(4):
                    v.max(top8[:, j, :], zc[:, j, 0:NBLK]).then_inc(route, 1)
                v.wait_ge(route, at + 9)
                v.tensor_copy(top4[:, :, 0:NTOP], top8[:, :, 0:NTOP]).then_inc(route, 1)

            def take_out(g):
                at = ROUTE_STEPS * g
                for j in range(4):
                    v.match_replace(left[:, j, :], top4[:, j, :], zc[:, j, :], TAKEN).then_inc(route, 1)
                v.wait_ge(route, at + 14)
                v.tensor_scalar(unused[:], left[:, :, 0:NBLK], TAKEN, None, ALU.not_equal).then_inc(off_ready, 1)

            def take_off(g, k):
                v.wait_ge(off_full, g + 1)
                after(v, h_full, 16 * g - 16)
                v.tensor_copy(off[k][:], route_bank[:NBLK, :]).then_inc(off_ready, 1)

            def step(g, k, u, more=True):
                for i in range(NBLK):
                    if not (is_first(g) and i < 4):
                        v.wait_ge(dn_done, 16 * g + i - 3)
                    v.wait_ge(h_hi, 16 * g + i + 1)
                    if i == ROUTE_AT + 1 and more:
                        v.wait_ge(route, ROUTE_STEPS * (g + 1) + 10)
                    v.tensor_tensor(h2[i % 4][1][:], r32[i % 2][:], h2[i % 4][0][:].bitcast(F32), ALU.subtract).then_inc(h_lo, 1)
                    if i in TURN_AT and more:
                        turn_lo(g + 1, 1 - k, TURN_AT.index(i))
                    if i == ROUTE_AT and more:
                        choose(g + 1)
                    if i == ROUTE_AT + 1 and more:
                        take_out(g + 1)
                    if i == OFF_AT and more:
                        take_off(g + 1, 1 - k)
                v.wait_ge(dn_done, 16 * g + 16)
                v.wait_ge(xb_done, g + 1)
                for j in range(4):
                    v.scalar_tensor_tensor(xr[:, j, :], out[:, j, :], glob[:, GF1:GF1 + 1], xr[:, j, :], ALU.mult, ALU.add).then_inc(xo_ready, 1)
            v.memset(zc[:, :, NBLK:], SPARE).then_inc(prep, 1)
            v.wait_ge(small_in, 32)
            v.tensor_scalar(select[:], ident[:NBLK, 0:NBLK].unsqueeze(2).broadcast_to([NBLK, NBLK, 128]), OFF, None, ALU.mult).then_inc(prep, 1)
            v.wait_ge(rb_in, 32)
            v.tensor_scalar(gb2[:], gb2[:], glob[:, GF1:GF1 + 1], None, ALU.mult).then_inc(prep, 1)
            v.wait_ge(prep, 3)
            for d in range(DC):
                turn_lo(0, 0, d)
            choose(0)
            v.wait_ge(route, 10)
            take_out(0)
            take_off(0, 0)
            step(0, 0, 0)
            pairs(v, 1, G5 - 1, step)
            step(G5 - 1, 0, 3, False)

        @block.tensor
        def _(t):
            def turn_tile(g, d):
                if d == 0:
                    t.wait_ge(x_in, 16 * g + 16)
                after(t, x_lo, 4 * g + d)
                for j in range(4):
                    mm = t.transpose(turn_bank[:, j * 128:(j + 1) * 128], xt[:, j, d * 128:(d + 1) * 128], ident[:])
                mm.then_inc(turned, 1)

            def logits(g, k):
                t.wait_ge(x_lo, 4 * g + 4)
                after(t, off_ready, 2 * g)
                for j in range(4):
                    for n, (px, pw) in enumerate(PASSES):
                        for d in range(DC):
                            mm = t.matmul(route_bank[:, j * NBLK:(j + 1) * NBLK], x2[k][px][:, d, j * 128:(j + 1) * 128], rw[pw][:, d, :],
                                          start=(n == 0 and d == 0), stop=(n == 2 and d == DC - 1))
                mm.then_inc(lg_full, 1)

            def turn_off(g):
                t.wait_ge(off_ready, 2 * g + 1)
                for j in range(4):
                    mm = t.transpose(route_bank[:NBLK, j * 128:(j + 1) * 128], unused[:, j, :], ident[:])
                mm.then_inc(off_full, 1)

            def up(g, k, i):
                if i == 0:
                    t.wait_ge(off_ready, 2 * g + 2)
                if not (is_first(g) and i < 2):
                    t.wait_ge(relu_done, 16 * g + i - 1)
                for n, (pw, px) in enumerate(PASSES):
                    for d in range(DC):
                        t.matmul(hid[i % 2][:], w1[pw][:, d, i * 128:(i + 1) * 128], x2[k][px][:, d, :], start=(n == 0 and d == 0), stop=False)
                t.matmul(hid[i % 2][:], select[:, i, :], off[k][:], start=False, stop=True).then_inc(h_full, 1)

            def down_chunk(g, i):
                t.wait_ge(h_lo, 16 * g + i + 1)
                if i == 0:
                    after(t, xo_ready, 4 * g)
                for j in range(4):
                    for n, (ph, pw) in enumerate(PASSES):
                        mm = t.matmul(out[:, j, :], h2[i % 4][ph][:, j * 128:(j + 1) * 128], w2[pw][:, i, :],
                                      start=(i == 0 and n == 0), stop=(i == NBLK - 1 and n == 2))
                mm.then_inc(dn_done, 1)

            def step(g, k, u, more=True):
                for i in range(NBLK + 2):
                    if i < NBLK:
                        up(g, k, i)
                    if i >= 2:
                        down_chunk(g, i - 2)
                    if i in TURN_AT and more:
                        turn_tile(g + 1, TURN_AT.index(i))
                    if i == ROUTE_AT and more:
                        logits(g + 1, 1 - k)
                    if i == OFF_AT and more:
                        turn_off(g + 1)
            t.wait_ge(small_in, 32)
            for d in range(DC):
                turn_tile(0, d)
            t.wait_ge(prep, 2)
            logits(0, 0)
            turn_off(0)
            step(0, 0, 0)
            pairs(t, 1, G5 - 1, step)
            step(G5 - 1, 0, 3, False)


def gated_stack(nc, ins, result):
    def dram(name, *shape):
        return nc.dram_tensor(name, shape, F32).ap()
    q_parts = [dram(f"q_part{p}", D, TOK) for p in range(2)]
    mask_row, some_row, attn = dram("mask_row", B, M), dram("some_row", B), dram("attn", TOK, D)
    w_parts = [[dram(f"{n}{p}", *shape) for p in range(2)] for n, shape in (("gate_t", (D, I0)), ("up_t", (D, I0)), ("down_t", (I0, D)))]
    gate_d, up_d, v_d = (dram(n, HUNITS, 128, UW) for n in ("gate", "up", "hidden"))
    x1, x2, x3 = (dram(f"x{i}", TOK, D) for i in range(1, 4))
    xn1, xn2, xn3 = (dram(f"xn{i}", TOK, D) for i in range(1, 4))
    x, ident = ins["x"], ins["ident"]
    sems = []
    with nc.sbuf_tensor("glob", [128, NGLOB], F32) as glob:
        gates(nc, sems, ins["g_xattn"], ins["g_ffn"], glob)
        project_queries(nc, sems, x, ins["L0_xattn_Wq"], ident, q_parts)
        attend0(nc, sems, ins["ctx_t"], ins["mask"], ins["L0_xattn_Wk"], ins["L0_xattn_Wv"], q_parts, mask_row, some_row, ident, attn)
        project_out(nc, sems, attn, ins["L0_xattn_Wo"], ident, glob, x, x1, xn1)
        clear(nc, sems)
        ffn0(nc, sems, xn1, ins["L0_ffn_w_gate"], ins["L0_ffn_w_up"], ins["L0_ffn_w_down"], w_parts, ident, glob,
             gate_d, up_d, v_d, x1, x2, xn2)
        clear(nc, sems)
        attend1(nc, sems, xn2, ins["ctx"], ins["ctx_t"], ins["L1_xattn_Wq"], ins["L1_xattn_bq"], ins["L1_xattn_Wk"], ins["L1_xattn_bk"],
                ins["L1_wv_t"], ins["L1_xattn_bv"], ident, glob, x2, x3, xn3)
        ffn1(nc, sems, xn3, ins["L1_router_t"], ins["L1_ffn_router_b"], ins["L1_w1_t"], ins["L1_ffn_b1"], ins["L1_w2_t"], ins["L1_ffn_b2"],
             ident, glob, x3, result)


def kernel(**inputs):
    import numpy as np
    import concourse.bacc as bacc
    from concourse.bass_utils import run_bass_kernel_spmd

    given = {n: np.asarray(a) for n, a in inputs.items()}
    ins = {n: given[n] for n in ("g_xattn", "g_ffn", "L0_xattn_Wq", "L0_xattn_Wk", "L0_xattn_Wv", "L0_xattn_Wo",
                                 "L0_ffn_w_gate", "L0_ffn_w_up", "L0_ffn_w_down", "L1_xattn_Wq", "L1_xattn_bq", "L1_xattn_Wk",
                                 "L1_xattn_bk", "L1_xattn_bv", "L1_ffn_router_b", "L1_ffn_b1", "L1_ffn_b2")}
    ins["x"] = given["x"].reshape(TOK, D)
    ins["ctx"] = given["ctx_768"]
    ins["ctx_t"] = given["ctx_768"].transpose(0, 2, 1)
    ins["mask"] = np.ascontiguousarray(given["mask_BxS2_bf1"]).view(np.uint8)
    ins["L1_wv_t"] = given["L1_xattn_Wv"].T
    ins["L1_router_t"] = given["L1_ffn_router_w"].T
    ins["L1_w1_t"] = given["L1_ffn_w1"].T
    ins["L1_w2_t"] = given["L1_ffn_w2"].T
    ins["ident"] = np.eye(128, dtype=np.float32)

    nc = bacc.Bacc("TRN2", target_bir_lowering=False, num_devices=1)
    arrays, aps = {}, {}
    for name, a in ins.items():
        a = np.ascontiguousarray(a)
        arrays[f"in_{name}_dram"] = a
        aps[name] = nc.dram_tensor(f"in_{name}_dram", a.shape, mybir.dt.from_np(a.dtype), kind="ExternalInput").ap()
    out = nc.dram_tensor("out_0_dram", (TOK, D), F32, kind="ExternalOutput").ap()
    gated_stack(nc, aps, out)
    r = run_bass_kernel_spmd(nc, [arrays], core_ids=[0])
    return r.results[0]["out_0_dram"].reshape(B, S, D)
```
